# Optimizing a Trainium2 kernel written in Bass

```python
import numpy as np
import jax
import jax.numpy as jnp

def _softmax(x, axis=-1):
    return jax.nn.softmax(x, axis=axis)

def _gelu(x):
    return jax.nn.gelu(x, approximate=True)

def _silu(x):
    return jax.nn.silu(x)

def _sigmoid(x):
    return jax.nn.sigmoid(x)

def _layernorm(x, axis=-1, eps=1e-05):
    m = jnp.mean(x, axis=axis, keepdims=True)
    v = jnp.var(x, axis=axis, keepdims=True)
    return (x - m) / jnp.sqrt(v + eps)

def _scatter_add(tgt, idx, src, axis=0):
    return tgt.at[idx].add(src)

def _segment_sum(src, seg, n):
    return jax.ops.segment_sum(src, seg, n)
kernel_name = 'mk_decoder_postln_d2_seqx_r8_de455b'

def setup_inputs(seed: int=0):
    np.random.seed(seed)
    _w = jnp.asarray

    def _rec_inputs():
        import jax
        import jax.numpy as jnp
        _rk = jax.random.key(seed)
        x = -0.0002928 + 1 * jax.random.normal(jax.random.fold_in(_rk, 1), (4, 256, 128), jnp.float32)
        _lenS = 256 - jax.random.randint(jax.random.fold_in(_rk, 7), (4,), 0, max(1, 256 // 4) + 1, jnp.int32)
        _lenS2 = 1601 - jax.random.randint(jax.random.fold_in(_rk, 8), (4,), 0, max(1, 1601 // 4) + 1, jnp.int32)
        _ctx_512P = jax.random.normal(jax.random.fold_in(_rk, 11), (4, 16, 64), jnp.float32)
        _ctx_512c = jax.random.dirichlet(jax.random.fold_in(_rk, 511), 0.3 * jnp.ones((16,), jnp.float32), (4, 1601))
        _ctx_512t = jnp.einsum('bsk,bkd->bsd', _ctx_512c, _ctx_512P)
        _ctx_512t = _ctx_512t * jax.lax.rsqrt(jnp.mean(jnp.square(_ctx_512t)) + 1e-12) * 0.953939
        ctx_512 = 0.00222621 + 0.99962 * (_ctx_512t + 0.3 * jax.random.normal(jax.random.fold_in(_rk, 611), (4, 1601, 64), jnp.float32))
        return (x, ctx_512)
    x, ctx_512 = _rec_inputs()

    def _L0_attn_setup():
        import jax, jax.numpy as jnp
        import numpy as np
        NUM_HEADS = 16
        key = jax.random.key(seed)
        ks = jax.random.split(key, 5)
        B, N, C = (2, 256, 128)
        x = jax.random.normal(ks[0], (B, N, C), dtype=jnp.float32)
        s_in = 1.0 / np.sqrt(C)
        Wq = jax.random.normal(ks[1], (C, 2 * C), dtype=jnp.float32) * s_in
        Wk = jax.random.normal(ks[2], (C, 2 * C), dtype=jnp.float32) * s_in
        Wv = jax.random.normal(ks[3], (C, 2 * C), dtype=jnp.float32) * s_in
        Wo = jax.random.normal(ks[4], (2 * C, C), dtype=jnp.float32) * (1.0 / np.sqrt(2 * C))
        return {'x': x, 'Wq': Wq, 'Wk': Wk, 'Wv': Wv, 'Wo': Wo}
    _L0_attn_all = _L0_attn_setup()
    _L0_attn_in = {k: v for k, v in _L0_attn_all.items() if k in ('Wq', 'Wk', 'Wv', 'Wo')}
    del _L0_attn_all

    def _L0_xattn_setup():
        import jax, jax.numpy as jnp
        import numpy as np
        B, T, TC, C, CC, H = (2, 256, 64, 128, 64, 16)
        D = C // H

        def _heads(t):
            b, l, _ = t.shape
            return t.reshape(b, l, H, D).transpose(0, 2, 1, 3)
        key = jax.random.key(seed)
        ks = jax.random.split(key, 18)
        w = lambda k, i, o: jax.random.normal(k, (i, o), jnp.float32) / np.sqrt(i).astype(np.float32)
        return {'x': jax.random.normal(ks[0], (B, T, C), jnp.float32), 'cross_input': jax.random.normal(ks[1], (B, TC, CC), jnp.float32), 'Wk': w(ks[2], C, C), 'bk': jnp.zeros((C,), jnp.float32), 'Wq': w(ks[3], C, C), 'bq': jnp.zeros((C,), jnp.float32), 'Wv': w(ks[4], C, C), 'bv': jnp.zeros((C,), jnp.float32), 'Wck': w(ks[5], CC, C), 'bck': jnp.zeros((C,), jnp.float32), 'Wcq': w(ks[6], C, C), 'bcq': jnp.zeros((C,), jnp.float32), 'Wcv': w(ks[7], CC, C), 'bcv': jnp.zeros((C,), jnp.float32), 'Wp': w(ks[8], C, C), 'bp': jnp.zeros((C,), jnp.float32)}
    _L0_xattn_all = _L0_xattn_setup()
    _L0_xattn_in = {k: v for k, v in _L0_xattn_all.items() if k in ('Wk', 'bk', 'Wq', 'bq', 'Wv', 'bv', 'Wck', 'bck', 'Wcq', 'bcq', 'Wcv', 'bcv', 'Wp', 'bp')}
    del _L0_xattn_all

    def _L0_ffn_setup():
        import jax, jax.numpy as jnp
        import numpy as np
        EPS = 0.05
        N_ITERS = 20
        TOP_K = 2

        def _sinkhorn(cost, n_iters=N_ITERS, epsilon=EPS):
            la = cost / epsilon
            for _ in range(n_iters):
                la = la - jax.scipy.special.logsumexp(la, axis=-1, keepdims=True)
                la = la - jax.scipy.special.logsumexp(la, axis=-2, keepdims=True)
            return jnp.exp(la)
        key = jax.random.key(seed)
        k0, k1, k2, k3, k4 = jax.random.split(key, 5)
        B, T, D, F, E = (2, 256, 128, 512, 8)
        x = jax.random.normal(k0, (B, T, D), dtype=jnp.float32)
        gate_W = jax.random.normal(k1, (E, D), dtype=jnp.float32) * 0.02
        W_gate = jax.random.normal(k2, (E, F, D), dtype=jnp.float32) * 0.02
        W_up = jax.random.normal(k3, (E, F, D), dtype=jnp.float32) * 0.02
        W_down = jax.random.normal(k4, (E, D, F), dtype=jnp.float32) * 0.02
        return {'x': x, 'gate_W': gate_W, 'W_gate': W_gate, 'W_up': W_up, 'W_down': W_down}
    _L0_ffn_all = _L0_ffn_setup()
    _L0_ffn_in = {k: v for k, v in _L0_ffn_all.items() if k in ('gate_W', 'W_gate', 'W_up', 'W_down')}
    del _L0_ffn_all

    def _L1_attn_setup():
        import jax, jax.numpy as jnp
        import numpy as np
        DIM = 128
        HEADS = 16
        DIM_HEAD = 64
        NUM_FREQS = 16
        INNER = HEADS * DIM_HEAD

        def rotate_half(x):
            x1 = x[..., ::2]
            x2 = x[..., 1::2]
            return jnp.concatenate((-x2, x1), axis=-1)

        def rope_fourier_cache(seq_len, head_dim, num_freqs):
            freqs = 10000.0 ** (-jnp.arange(0, head_dim, 2, dtype=jnp.float32) / head_dim)
            pos = jnp.arange(seq_len, dtype=jnp.float32)[:, None]
            angles = pos * freqs
            sin = jnp.sin(angles)
            cos = jnp.cos(angles)
            sin = jnp.stack([sin, sin], axis=-1).reshape(seq_len, head_dim)
            cos = jnp.stack([cos, cos], axis=-1).reshape(seq_len, head_dim)
            ffreqs = jnp.arange(1, num_freqs + 1, dtype=jnp.float32)
            p = jnp.arange(seq_len, dtype=jnp.float32)[:, None]
            fourier = jnp.concatenate([jnp.sin(p * ffreqs), jnp.cos(p * ffreqs)], axis=-1)
            return (sin, cos, fourier)
        key = jax.random.key(seed)
        ks = jax.random.split(key, 6)
        b, n = (4, 256)
        x = jax.random.normal(ks[0], (b, n, DIM), dtype=jnp.float32)
        w_qkv = jax.random.normal(ks[1], (3 * INNER, DIM), dtype=jnp.float32) * DIM ** (-0.5)
        w_fproj = jax.random.normal(ks[2], (DIM_HEAD, 2 * NUM_FREQS), dtype=jnp.float32) * (2 * NUM_FREQS) ** (-0.5)
        b_fproj = jax.random.normal(ks[3], (DIM_HEAD,), dtype=jnp.float32) * 0.02
        w_out = jax.random.normal(ks[4], (DIM, INNER), dtype=jnp.float32) * INNER ** (-0.5)
        b_out = jax.random.normal(ks[5], (DIM,), dtype=jnp.float32) * 0.02
        return {'x': x, 'w_qkv': w_qkv, 'w_fproj': w_fproj, 'b_fproj': b_fproj, 'w_out': w_out, 'b_out': b_out}
    _L1_attn_all = _L1_attn_setup()
    _L1_attn_in = {k: v for k, v in _L1_attn_all.items() if k in ('w_qkv', 'w_fproj', 'b_fproj', 'w_out', 'b_out')}
    del _L1_attn_all

    def _L1_xattn_setup():
        import jax, jax.numpy as jnp
        import numpy as np
        H, D, C1, C2, S, M, B, W = (16, 32, 128, 64, 256, 64, 2, 4)

        def _ln(x, g, b):
            m = jnp.mean(x, -1, keepdims=True)
            v = jnp.var(x, -1, keepdims=True)
            return (x - m) * jax.lax.rsqrt(v + 1e-05) * g + b

        def _mha(x, y, wq, wk, wv, li1_w, li1_b, lnx_g, lnx_b, lny_g, lny_b, ln3_g, ln3_b, li2_w, li2_b, li3_w, li3_b, causal):
            xn = _ln(x, lnx_g, lnx_b)
            yn = _ln(y, lny_g, lny_b)
            q = jnp.einsum('bsc,hcd->bhsd', xn, wq)
            k = jnp.einsum('btc,hcd->bhtd', yn, wk)
            v = jnp.einsum('btc,hcd->bhtd', yn, wv)
            a = jax.nn.softmax(jnp.einsum('bhsd,bhtd->bhst', q, k) * D ** (-0.5), axis=-1)
            if causal:
                s, t = (a.shape[-2], a.shape[-1])
                mask = (jnp.arange(t)[None, :] > jnp.arange(s)[:, None]).astype(a.dtype)
                a = a * mask
            o = jnp.einsum('bhst,bhtd->bhsd', a, v)
            o = o.transpose(0, 2, 1, 3).reshape(x.shape[0], x.shape[1], H * D)
            x_out = x + o @ li1_w + li1_b
            h = jax.nn.gelu(_ln(x_out, ln3_g, ln3_b) @ li2_w + li2_b, approximate=False)
            return x_out + h @ li3_w + li3_b
        key = jax.random.key(seed)
        ks = iter(jax.random.split(key, 64))

        def w(shape, scale=0.02):
            return jax.random.normal(next(ks), shape, jnp.float32) * scale
        inp = {'xx': jax.random.normal(next(ks), (B, S, C1), jnp.float32), 'ee': jax.random.normal(next(ks), (B, M, C2), jnp.float32), 'ln1_g': jnp.ones(C1, jnp.float32), 'ln1_b': jnp.zeros(C1, jnp.float32), 'ln2_g': jnp.ones(C1, jnp.float32), 'ln2_b': jnp.zeros(C1, jnp.float32)}
        for pfx, cy in (('a1', C1), ('a2', C2)):
            inp[pfx + '_wq'] = w((H, C1, D))
            inp[pfx + '_wk'] = w((H, cy, D))
            inp[pfx + '_wv'] = w((H, cy, D))
            inp[pfx + '_li1_w'] = w((H * D, C1))
            inp[pfx + '_li1_b'] = jnp.zeros(C1, jnp.float32)
            inp[pfx + '_lnx_g'] = jnp.ones(C1, jnp.float32)
            inp[pfx + '_lnx_b'] = jnp.zeros(C1, jnp.float32)
            inp[pfx + '_lny_g'] = jnp.ones(cy, jnp.float32)
            inp[pfx + '_lny_b'] = jnp.zeros(cy, jnp.float32)
            inp[pfx + '_ln3_g'] = jnp.ones(C1, jnp.float32)
            inp[pfx + '_ln3_b'] = jnp.zeros(C1, jnp.float32)
            inp[pfx + '_li2_w'] = w((C1, C1 * W))
            inp[pfx + '_li2_b'] = jnp.zeros(C1 * W, jnp.float32)
            inp[pfx + '_li3_w'] = w((C1 * W, C1))
            inp[pfx + '_li3_b'] = jnp.zeros(C1, jnp.float32)
        inp['training'] = 0
        return inp
    _L1_xattn_all = _L1_xattn_setup()
    _L1_xattn_in = {k: v for k, v in _L1_xattn_all.items() if k in ('ln1_g', 'ln1_b', 'ln2_g', 'ln2_b', 'a1_wq', 'a1_wk', 'a1_wv', 'a1_li1_w', 'a1_li1_b', 'a1_lnx_g', 'a1_lnx_b', 'a1_lny_g', 'a1_lny_b', 'a1_ln3_g', 'a1_ln3_b', 'a1_li2_w', 'a1_li2_b', 'a1_li3_w', 'a1_li3_b', 'a2_wq', 'a2_wk', 'a2_wv', 'a2_li1_w', 'a2_li1_b', 'a2_lnx_g', 'a2_lnx_b', 'a2_lny_g', 'a2_lny_b', 'a2_ln3_g', 'a2_ln3_b', 'a2_li2_w', 'a2_li2_b', 'a2_li3_w', 'a2_li3_b')}
    del _L1_xattn_all

    def _L1_ffn_setup():
        import jax, jax.numpy as jnp
        import numpy as np
        E, D, F = (8, 128, 512)
        B, S = (4, 256)

        def _layernorm(x, g, b, eps=1e-05):
            mu = jnp.mean(x, axis=-1, keepdims=True)
            var = jnp.var(x, axis=-1, keepdims=True)
            return (x - mu) * jax.lax.rsqrt(var + eps) * g + b
        key = jax.random.key(seed)
        ks = jax.random.split(key, 5)
        return {'input_features': jax.random.normal(ks[0], (B, S, D), jnp.float32), 'centroids': jax.random.normal(ks[1], (E, D), jnp.float32) * 0.1, 'ln_g': jnp.ones((E, D), jnp.float32), 'ln_b': jnp.zeros((E, D), jnp.float32), 'w1': jax.random.normal(ks[2], (E, F, D), jnp.float32) * (1.0 / np.sqrt(D).astype(np.float32)), 'b1': jnp.zeros((E, F), jnp.float32), 'w2': jax.random.normal(ks[3], (E, D, F), jnp.float32) * (1.0 / np.sqrt(F).astype(np.float32)), 'b2': jnp.zeros((E, D), jnp.float32)}
    _L1_ffn_all = _L1_ffn_setup()
    _L1_ffn_in = {k: v for k, v in _L1_ffn_all.items() if k in ('centroids', 'ln_g', 'ln_b', 'w1', 'b1', 'w2', 'b2')}
    del _L1_ffn_all
    return {'x': x, 'ctx_512': ctx_512, 'L0_attn_Wq': _L0_attn_in['Wq'], 'L0_attn_Wk': _L0_attn_in['Wk'], 'L0_attn_Wv': _L0_attn_in['Wv'], 'L0_attn_Wo': _L0_attn_in['Wo'], 'L0_xattn_Wk': _L0_xattn_in['Wk'], 'L0_xattn_bk': _L0_xattn_in['bk'], 'L0_xattn_Wq': _L0_xattn_in['Wq'], 'L0_xattn_bq': _L0_xattn_in['bq'], 'L0_xattn_Wv': _L0_xattn_in['Wv'], 'L0_xattn_bv': _L0_xattn_in['bv'], 'L0_xattn_Wck': _L0_xattn_in['Wck'], 'L0_xattn_bck': _L0_xattn_in['bck'], 'L0_xattn_Wcq': _L0_xattn_in['Wcq'], 'L0_xattn_bcq': _L0_xattn_in['bcq'], 'L0_xattn_Wcv': _L0_xattn_in['Wcv'], 'L0_xattn_bcv': _L0_xattn_in['bcv'], 'L0_xattn_Wp': _L0_xattn_in['Wp'], 'L0_xattn_bp': _L0_xattn_in['bp'], 'L0_ffn_gate_W': _L0_ffn_in['gate_W'], 'L0_ffn_W_gate': _L0_ffn_in['W_gate'], 'L0_ffn_W_up': _L0_ffn_in['W_up'], 'L0_ffn_W_down': _L0_ffn_in['W_down'], 'L1_attn_w_qkv': _L1_attn_in['w_qkv'], 'L1_attn_w_fproj': _L1_attn_in['w_fproj'], 'L1_attn_b_fproj': _L1_attn_in['b_fproj'], 'L1_attn_w_out': _L1_attn_in['w_out'], 'L1_attn_b_out': _L1_attn_in['b_out'], 'L1_xattn_ln1_g': _L1_xattn_in['ln1_g'], 'L1_xattn_ln1_b': _L1_xattn_in['ln1_b'], 'L1_xattn_ln2_g': _L1_xattn_in['ln2_g'], 'L1_xattn_ln2_b': _L1_xattn_in['ln2_b'], 'L1_xattn_a1_wq': _L1_xattn_in['a1_wq'], 'L1_xattn_a1_wk': _L1_xattn_in['a1_wk'], 'L1_xattn_a1_wv': _L1_xattn_in['a1_wv'], 'L1_xattn_a1_li1_w': _L1_xattn_in['a1_li1_w'], 'L1_xattn_a1_li1_b': _L1_xattn_in['a1_li1_b'], 'L1_xattn_a1_lnx_g': _L1_xattn_in['a1_lnx_g'], 'L1_xattn_a1_lnx_b': _L1_xattn_in['a1_lnx_b'], 'L1_xattn_a1_lny_g': _L1_xattn_in['a1_lny_g'], 'L1_xattn_a1_lny_b': _L1_xattn_in['a1_lny_b'], 'L1_xattn_a1_ln3_g': _L1_xattn_in['a1_ln3_g'], 'L1_xattn_a1_ln3_b': _L1_xattn_in['a1_ln3_b'], 'L1_xattn_a1_li2_w': _L1_xattn_in['a1_li2_w'], 'L1_xattn_a1_li2_b': _L1_xattn_in['a1_li2_b'], 'L1_xattn_a1_li3_w': _L1_xattn_in['a1_li3_w'], 'L1_xattn_a1_li3_b': _L1_xattn_in['a1_li3_b'], 'L1_xattn_a2_wq': _L1_xattn_in['a2_wq'], 'L1_xattn_a2_wk': _L1_xattn_in['a2_wk'], 'L1_xattn_a2_wv': _L1_xattn_in['a2_wv'], 'L1_xattn_a2_li1_w': _L1_xattn_in['a2_li1_w'], 'L1_xattn_a2_li1_b': _L1_xattn_in['a2_li1_b'], 'L1_xattn_a2_lnx_g': _L1_xattn_in['a2_lnx_g'], 'L1_xattn_a2_lnx_b': _L1_xattn_in['a2_lnx_b'], 'L1_xattn_a2_lny_g': _L1_xattn_in['a2_lny_g'], 'L1_xattn_a2_lny_b': _L1_xattn_in['a2_lny_b'], 'L1_xattn_a2_ln3_g': _L1_xattn_in['a2_ln3_g'], 'L1_xattn_a2_ln3_b': _L1_xattn_in['a2_ln3_b'], 'L1_xattn_a2_li2_w': _L1_xattn_in['a2_li2_w'], 'L1_xattn_a2_li2_b': _L1_xattn_in['a2_li2_b'], 'L1_xattn_a2_li3_w': _L1_xattn_in['a2_li3_w'], 'L1_xattn_a2_li3_b': _L1_xattn_in['a2_li3_b'], 'L1_ffn_centroids': _L1_ffn_in['centroids'], 'L1_ffn_ln_g': _L1_ffn_in['ln_g'], 'L1_ffn_ln_b': _L1_ffn_in['ln_b'], 'L1_ffn_w1': _L1_ffn_in['w1'], 'L1_ffn_b1': _L1_ffn_in['b1'], 'L1_ffn_w2': _L1_ffn_in['w2'], 'L1_ffn_b2': _L1_ffn_in['b2']}

def reference(x, ctx_512, L0_attn_Wq, L0_attn_Wk, L0_attn_Wv, L0_attn_Wo, L0_xattn_Wk, L0_xattn_bk, L0_xattn_Wq, L0_xattn_bq, L0_xattn_Wv, L0_xattn_bv, L0_xattn_Wck, L0_xattn_bck, L0_xattn_Wcq, L0_xattn_bcq, L0_xattn_Wcv, L0_xattn_bcv, L0_xattn_Wp, L0_xattn_bp, L0_ffn_gate_W, L0_ffn_W_gate, L0_ffn_W_up, L0_ffn_W_down, L1_attn_w_qkv, L1_attn_w_fproj, L1_attn_b_fproj, L1_attn_w_out, L1_attn_b_out, L1_xattn_ln1_g, L1_xattn_ln1_b, L1_xattn_ln2_g, L1_xattn_ln2_b, L1_xattn_a1_wq, L1_xattn_a1_wk, L1_xattn_a1_wv, L1_xattn_a1_li1_w, L1_xattn_a1_li1_b, L1_xattn_a1_lnx_g, L1_xattn_a1_lnx_b, L1_xattn_a1_lny_g, L1_xattn_a1_lny_b, L1_xattn_a1_ln3_g, L1_xattn_a1_ln3_b, L1_xattn_a1_li2_w, L1_xattn_a1_li2_b, L1_xattn_a1_li3_w, L1_xattn_a1_li3_b, L1_xattn_a2_wq, L1_xattn_a2_wk, L1_xattn_a2_wv, L1_xattn_a2_li1_w, L1_xattn_a2_li1_b, L1_xattn_a2_lnx_g, L1_xattn_a2_lnx_b, L1_xattn_a2_lny_g, L1_xattn_a2_lny_b, L1_xattn_a2_ln3_g, L1_xattn_a2_ln3_b, L1_xattn_a2_li2_w, L1_xattn_a2_li2_b, L1_xattn_a2_li3_w, L1_xattn_a2_li3_b, L1_ffn_centroids, L1_ffn_ln_g, L1_ffn_ln_b, L1_ffn_w1, L1_ffn_b1, L1_ffn_w2, L1_ffn_b2):
    import jax
    import jax.numpy as jnp

    def _L0_attn_ref(x, Wq, Wk, Wv, Wo):
        import jax, jax.numpy as jnp
        import numpy as np
        NUM_HEADS = 16
        B, N, C = x.shape
        H = NUM_HEADS
        hd = C // H

        def proj(W):
            return (x @ W).reshape(B, N, H, 2 * hd).transpose(0, 2, 1, 3)
        q = proj(Wq)
        k = proj(Wk)
        v = proj(Wv)
        q_r, q_i = (q[..., :hd], q[..., hd:])
        k_r, k_i = (k[..., :hd], k[..., hd:])
        v_r, v_i = (v[..., :hd], v[..., hd:])
        scores = (jnp.einsum('bhnd,bhmd->bhnm', q_r, k_r) + jnp.einsum('bhnd,bhmd->bhnm', q_i, k_i)) / jnp.sqrt(jnp.float32(hd))
        causal = jnp.tril(jnp.ones((N, N), dtype=bool))
        scores = jnp.where(causal[None, None], scores, -jnp.inf)
        probs = jax.nn.softmax(scores, axis=-1)
        out_r = jnp.einsum('bhnm,bhmd->bhnd', probs, v_r)
        out_i = jnp.einsum('bhnm,bhmd->bhnd', probs, v_i)
        out = jnp.concatenate([out_r, out_i], axis=-1)
        out = out.transpose(0, 2, 1, 3).reshape(B, N, 2 * C)
        return out @ Wo

    def _L0_xattn_ref(x, cross_input, Wk, bk, Wq, bq, Wv, bv, Wck, bck, Wcq, bcq, Wcv, bcv, Wp, bp):
        import jax, jax.numpy as jnp
        import numpy as np
        B, T, TC, C, CC, H = (2, 256, 64, 128, 64, 16)
        D = C // H

        def _heads(t):
            b, l, _ = t.shape
            return t.reshape(b, l, H, D).transpose(0, 2, 1, 3)
        scale = np.float32(1.0 / np.sqrt(D))
        q = _heads(x @ Wq + bq)
        k = _heads(x @ Wk + bk)
        v = _heads(x @ Wv + bv)
        att = jnp.einsum('bhqd,bhkd->bhqk', q, k) * scale
        causal = jnp.tril(jnp.ones((T, T), bool))
        att = jnp.where(causal[None, None], att, -jnp.inf)
        y = jnp.einsum('bhqk,bhkd->bhqd', jax.nn.softmax(att, axis=-1), v)
        qc = _heads(x @ Wcq + bcq)
        kc = _heads(cross_input @ Wck + bck)
        vc = _heads(cross_input @ Wcv + bcv)
        attc = jnp.einsum('bhqd,bhkd->bhqk', qc, kc) * scale
        y = y + jnp.einsum('bhqk,bhkd->bhqd', jax.nn.softmax(attc, axis=-1), vc)
        y = y.transpose(0, 2, 1, 3).reshape(x.shape[0], T, C)
        return y @ Wp + bp

    def _L0_ffn_ref(x, gate_W, W_gate, W_up, W_down):
        import jax, jax.numpy as jnp
        import numpy as np
        EPS = 0.05
        N_ITERS = 20
        TOP_K = 2

        def _sinkhorn(cost, n_iters=N_ITERS, epsilon=EPS):
            la = cost / epsilon
            for _ in range(n_iters):
                la = la - jax.scipy.special.logsumexp(la, axis=-1, keepdims=True)
                la = la - jax.scipy.special.logsumexp(la, axis=-2, keepdims=True)
            return jnp.exp(la)
        B, T, D = x.shape
        xf = x.reshape(B * T, D)
        logits = xf @ gate_W.T
        pi = _sinkhorn(-logits)
        _, top_idx = jax.lax.top_k(pi, TOP_K)
        g = jnp.einsum('nd,efd->enf', xf, W_gate)
        u = jnp.einsum('nd,efd->enf', xf, W_up)
        y = jnp.einsum('enf,edf->end', jax.nn.silu(g) * u, W_down)
        n_ar = jnp.arange(xf.shape[0])
        out = jnp.zeros_like(xf)
        for k in range(TOP_K):
            out = out + y[top_idx[:, k], n_ar] * pi[:, k:k + 1]
        return out.reshape(B, T, D)

    def _L1_attn_ref(x, w_qkv, w_fproj, b_fproj, w_out, b_out):
        import jax, jax.numpy as jnp
        import numpy as np
        DIM = 128
        HEADS = 16
        DIM_HEAD = 64
        NUM_FREQS = 16
        INNER = HEADS * DIM_HEAD

        def rotate_half(x):
            x1 = x[..., ::2]
            x2 = x[..., 1::2]
            return jnp.concatenate((-x2, x1), axis=-1)

        def rope_fourier_cache(seq_len, head_dim, num_freqs):
            freqs = 10000.0 ** (-jnp.arange(0, head_dim, 2, dtype=jnp.float32) / head_dim)
            pos = jnp.arange(seq_len, dtype=jnp.float32)[:, None]
            angles = pos * freqs
            sin = jnp.sin(angles)
            cos = jnp.cos(angles)
            sin = jnp.stack([sin, sin], axis=-1).reshape(seq_len, head_dim)
            cos = jnp.stack([cos, cos], axis=-1).reshape(seq_len, head_dim)
            ffreqs = jnp.arange(1, num_freqs + 1, dtype=jnp.float32)
            p = jnp.arange(seq_len, dtype=jnp.float32)[:, None]
            fourier = jnp.concatenate([jnp.sin(p * ffreqs), jnp.cos(p * ffreqs)], axis=-1)
            return (sin, cos, fourier)
        b, n, _ = x.shape
        scale = DIM_HEAD ** (-0.5)
        qkv = x @ w_qkv.T
        q, k, v = jnp.split(qkv, 3, axis=-1)

        def to_heads(t):
            return t.reshape(b, n, HEADS, DIM_HEAD).transpose(0, 2, 1, 3)
        q, k, v = (to_heads(q), to_heads(k), to_heads(v))
        sin, cos, fourier = rope_fourier_cache(n, DIM_HEAD, NUM_FREQS)
        fenc = fourier @ w_fproj.T + b_fproj
        fenc = fenc[None, None]
        q = q * cos + rotate_half(q) * sin + fenc
        k = k * cos + rotate_half(k) * sin + fenc
        dots = jnp.einsum('bhid,bhjd->bhij', q, k) * scale
        attn = jax.nn.softmax(dots, axis=-1)
        out = jnp.einsum('bhij,bhjd->bhid', attn, v)
        out = out.transpose(0, 2, 1, 3).reshape(b, n, INNER)
        return out @ w_out.T + b_out

    def _L1_xattn_ref(xx, ee, ln1_g, ln1_b, ln2_g, ln2_b, a1_wq, a1_wk, a1_wv, a1_li1_w, a1_li1_b, a1_lnx_g, a1_lnx_b, a1_lny_g, a1_lny_b, a1_ln3_g, a1_ln3_b, a1_li2_w, a1_li2_b, a1_li3_w, a1_li3_b, a2_wq, a2_wk, a2_wv, a2_li1_w, a2_li1_b, a2_lnx_g, a2_lnx_b, a2_lny_g, a2_lny_b, a2_ln3_g, a2_ln3_b, a2_li2_w, a2_li2_b, a2_li3_w, a2_li3_b, training):
        import jax, jax.numpy as jnp
        import numpy as np
        H, D, C1, C2, S, M, B, W = (16, 32, 128, 64, 256, 64, 2, 4)

        def _ln(x, g, b):
            m = jnp.mean(x, -1, keepdims=True)
            v = jnp.var(x, -1, keepdims=True)
            return (x - m) * jax.lax.rsqrt(v + 1e-05) * g + b

        def _mha(x, y, wq, wk, wv, li1_w, li1_b, lnx_g, lnx_b, lny_g, lny_b, ln3_g, ln3_b, li2_w, li2_b, li3_w, li3_b, causal):
            xn = _ln(x, lnx_g, lnx_b)
            yn = _ln(y, lny_g, lny_b)
            q = jnp.einsum('bsc,hcd->bhsd', xn, wq)
            k = jnp.einsum('btc,hcd->bhtd', yn, wk)
            v = jnp.einsum('btc,hcd->bhtd', yn, wv)
            a = jax.nn.softmax(jnp.einsum('bhsd,bhtd->bhst', q, k) * D ** (-0.5), axis=-1)
            if causal:
                s, t = (a.shape[-2], a.shape[-1])
                mask = (jnp.arange(t)[None, :] > jnp.arange(s)[:, None]).astype(a.dtype)
                a = a * mask
            o = jnp.einsum('bhst,bhtd->bhsd', a, v)
            o = o.transpose(0, 2, 1, 3).reshape(x.shape[0], x.shape[1], H * D)
            x_out = x + o @ li1_w + li1_b
            h = jax.nn.gelu(_ln(x_out, ln3_g, ln3_b) @ li2_w + li2_b, approximate=False)
            return x_out + h @ li3_w + li3_b
        x = _ln(xx, ln1_g, ln1_b)
        x = x + _mha(x, x, a1_wq, a1_wk, a1_wv, a1_li1_w, a1_li1_b, a1_lnx_g, a1_lnx_b, a1_lny_g, a1_lny_b, a1_ln3_g, a1_ln3_b, a1_li2_w, a1_li2_b, a1_li3_w, a1_li3_b, causal=True)
        x = _ln(x, ln2_g, ln2_b)
        return x + _mha(x, ee, a2_wq, a2_wk, a2_wv, a2_li1_w, a2_li1_b, a2_lnx_g, a2_lnx_b, a2_lny_g, a2_lny_b, a2_ln3_g, a2_ln3_b, a2_li2_w, a2_li2_b, a2_li3_w, a2_li3_b, causal=False)

    def _L1_ffn_ref(input_features, centroids, ln_g, ln_b, w1, b1, w2, b2):
        import jax, jax.numpy as jnp
        import numpy as np
        E, D, F = (8, 128, 512)
        B, S = (4, 256)

        def _layernorm(x, g, b, eps=1e-05):
            mu = jnp.mean(x, axis=-1, keepdims=True)
            var = jnp.var(x, axis=-1, keepdims=True)
            return (x - mu) * jax.lax.rsqrt(var + eps) * g + b
        Bf, Sf, Df = input_features.shape
        x = input_features.reshape(-1, Df)
        aff = x @ centroids.T
        assign = jnp.argmax(aff, axis=1)
        order = jnp.argsort(assign)
        xs = x[order]
        es = assign[order]
        alpha = jax.nn.sigmoid(jnp.take_along_axis(aff[order], es[:, None], axis=1))
        nE = centroids.shape[0]
        y = jnp.zeros_like(xs)
        for e in range(nE):
            h = _layernorm(xs, ln_g[e], ln_b[e])
            h = jax.nn.relu(h @ w1[e].T + b1[e])
            ye = xs + h @ w2[e].T + b2[e]
            y = y + jnp.where((es == e)[:, None], ye, 0.0)
        out_sorted = alpha * y + (1.0 - alpha) * xs
        inv = jnp.argsort(order)
        return out_sorted[inv].reshape(Bf, Sf, Df)
    x = _layernorm(x + _L0_attn_ref(x, L0_attn_Wq, L0_attn_Wk, L0_attn_Wv, L0_attn_Wo), axis=-1)
    x = _layernorm(x + _L0_xattn_ref(x, ctx_512, L0_xattn_Wk, L0_xattn_bk, L0_xattn_Wq, L0_xattn_bq, L0_xattn_Wv, L0_xattn_bv, L0_xattn_Wck, L0_xattn_bck, L0_xattn_Wcq, L0_xattn_bcq, L0_xattn_Wcv, L0_xattn_bcv, L0_xattn_Wp, L0_xattn_bp), axis=-1)
    x = _layernorm(x + _L0_ffn_ref(x, L0_ffn_gate_W, L0_ffn_W_gate, L0_ffn_W_up, L0_ffn_W_down), axis=-1)
    x = _layernorm(x + _L1_attn_ref(x, L1_attn_w_qkv, L1_attn_w_fproj, L1_attn_b_fproj, L1_attn_w_out, L1_attn_b_out), axis=-1)
    x = _layernorm(x + _L1_xattn_ref(x, ctx_512, L1_xattn_ln1_g, L1_xattn_ln1_b, L1_xattn_ln2_g, L1_xattn_ln2_b, L1_xattn_a1_wq, L1_xattn_a1_wk, L1_xattn_a1_wv, L1_xattn_a1_li1_w, L1_xattn_a1_li1_b, L1_xattn_a1_lnx_g, L1_xattn_a1_lnx_b, L1_xattn_a1_lny_g, L1_xattn_a1_lny_b, L1_xattn_a1_ln3_g, L1_xattn_a1_ln3_b, L1_xattn_a1_li2_w, L1_xattn_a1_li2_b, L1_xattn_a1_li3_w, L1_xattn_a1_li3_b, L1_xattn_a2_wq, L1_xattn_a2_wk, L1_xattn_a2_wv, L1_xattn_a2_li1_w, L1_xattn_a2_li1_b, L1_xattn_a2_lnx_g, L1_xattn_a2_lnx_b, L1_xattn_a2_lny_g, L1_xattn_a2_lny_b, L1_xattn_a2_ln3_g, L1_xattn_a2_ln3_b, L1_xattn_a2_li2_w, L1_xattn_a2_li2_b, L1_xattn_a2_li3_w, L1_xattn_a2_li3_b, 0), axis=-1)
    x = _layernorm(x + _L1_ffn_ref(x, L1_ffn_centroids, L1_ffn_ln_g, L1_ffn_ln_b, L1_ffn_w1, L1_ffn_b1, L1_ffn_w2, L1_ffn_b2), axis=-1)
    return x

_drawn_inputs = setup_inputs


def setup_inputs(seed=0):
    import zlib

    import numpy as np

    out = dict(_drawn_inputs(seed))
    spreads = {'L0_xattn_bk': (0.0, 0.8),
     'L0_xattn_bq': (0.0, 0.1),
     'L0_xattn_bv': (0.0, 0.1),
     'L0_xattn_bck': (0.0, 0.8),
     'L0_xattn_bcq': (0.0, 0.1),
     'L0_xattn_bcv': (0.0, 0.1),
     'L0_xattn_bp': (0.0, 0.1),
     'L1_xattn_ln1_g': (1.0, 0.2),
     'L1_xattn_ln1_b': (0.0, 0.1),
     'L1_xattn_ln2_g': (1.0, 0.2),
     'L1_xattn_ln2_b': (0.0, 0.1),
     'L1_xattn_a1_li1_b': (0.0, 0.1),
     'L1_xattn_a1_lnx_g': (1.0, 0.6),
     'L1_xattn_a1_lnx_b': (0.0, 0.8),
     'L1_xattn_a1_lny_g': (1.0, 0.6),
     'L1_xattn_a1_lny_b': (0.0, 0.436),
     'L1_xattn_a1_ln3_g': (1.0, 0.6),
     'L1_xattn_a1_ln3_b': (0.0, 0.651),
     'L1_xattn_a1_li2_b': (0.0, 0.292),
     'L1_xattn_a1_li3_b': (0.0, 0.1),
     'L1_xattn_a2_li1_b': (0.0, 0.1),
     'L1_xattn_a2_lnx_g': (1.0, 0.6),
     'L1_xattn_a2_lnx_b': (0.0, 0.8),
     'L1_xattn_a2_lny_g': (1.0, 0.6),
     'L1_xattn_a2_lny_b': (0.0, 0.8),
     'L1_xattn_a2_ln3_g': (1.0, 0.6),
     'L1_xattn_a2_ln3_b': (0.0, 0.328),
     'L1_xattn_a2_li2_b': (0.0, 0.437),
     'L1_xattn_a2_li3_b': (0.0, 0.1),
     'L1_ffn_ln_g': (1.0, 0.2),
     'L1_ffn_ln_b': (0.0, 0.273),
     'L1_ffn_b1': (0.0, 0.269),
     'L1_ffn_b2': (0.0, 0.1)}
    factors = {'L0_ffn_gate_W': 8.0,
     'L0_ffn_W_gate': 8.0,
     'L0_ffn_W_up': 8.0,
     'L0_ffn_W_down': 8.0,
     'L1_xattn_a1_wq': 8.0,
     'L1_xattn_a1_wk': 8.0,
     'L1_xattn_a2_wq': 8.0,
     'L1_xattn_a2_wk': 8.0}
    for name, (base, spread) in spreads.items():
        noise = np.random.default_rng([zlib.crc32(name.encode()), seed]).standard_normal(out[name].shape)
        drawn = base * np.exp(spread * noise) if base else spread * noise
        out[name] = jnp.asarray(drawn.astype(out[name].dtype))
    for name, factor in factors.items():
        out[name] = (out[name] * factor).astype(out[name].dtype)
    return out
```

```python
from contextlib import ExitStack

import numpy as np

import concourse.bass as bass
from concourse import mybir

F32 = mybir.dt.float32
BF16 = mybir.dt.bfloat16
ALU = mybir.AluOpType
ACT = mybir.ActivationFunctionType
AX = mybir.AxisListType

P = 128
B = 4
N = 256
C = 128
CC = 64
T_CTX = 1601
KT_CTX = -(-T_CTX // P)
TAIL = T_CTX - (KT_CTX - 1) * P
NT = B * N // P
H = 16
BH = B * H
E = 8
F = 512
FB = F // P
EPS = 1e-5
CREDIT = 16
NEG = -1e30
SINK_ITERS = 20
SINK_EPS = 0.05

Q_PART = {1: (0, 0, 0, 1, 1, 2), 2: (0, 0, 1, 1, 0, 2)}
K_PART = {1: (0, 1, 2, 0, 1, 0), 2: (0, 1, 0, 1, 2, 0)}


class Sem:

    def __init__(self, ctx, nc, name):
        self.s = ctx.enter_context(nc.semaphore(name))
        self.base = CREDIT

    def at(self, n):
        return n + self.base

    def passed(self, n):
        self.base += n


class K:

    def __init__(self):
        self.sems = {}


def columns(widths):
    at, n = {}, 0
    for name, w in widths:
        at[name] = (n, w)
        n += w
    return at, n


W0, W0_N = columns([("wq", 256), ("wk", 256), ("wv", 256), ("wo", 4 * C), ("xk", 128), ("xq", 128),
                    ("xv", 128), ("xcq", 128), ("xp", 4 * C), ("gate", E)])
WC0, WC0_N = columns([("ck", 128), ("cv", 128)])
W1, W1_N = columns([("q", 1024), ("qr", 1024), ("k", 1024), ("kr", 1024), ("v", 1024), ("o", 1024),
                    ("cos", N), ("sin", N)])
WF, WF_N = columns([("fp", 128), ("fourier", N)])
WX, WX_N = columns([(n, 512) for n in ("q", "k", "v", "li1", "li2", "li3")])
WC1, WC1_N = columns([("k", 512), ("v", 512)])
COL, COL_N = columns([("xk", 1), ("xq", 1), ("xcq", 1), ("xck", 1), ("fp", 1)]
                     + [(a + n, w) for a in ("a1", "a2") for n, w in
                        (("lnx_g", 1), ("lnx_b", 1), ("lny_g", 1), ("lny_b", 1), ("ln3_g", 1), ("ln3_b", 1),
                         ("li2_b", FB))]
                     + [("ln_g", E), ("ln_b", E), ("b1", E * FB)])
ROW, ROW_N = columns([("xv", 128), ("xcv", 128), ("xp", 128), ("out", 128), ("a1li1", 128), ("a1li3", 128),
                      ("a2li1", 128), ("a2li3", 128), ("ln1_g", 128), ("ln1_b", 128), ("ln2_g", 128),
                      ("ln2_b", 128), ("iota", E)])


def sub(tensor, table, name, rows=P):
    a, w = table[name]
    return tensor[0:rows, a:a + w]


def rounds(eng, end, n, body):
    assert end % n == 0 and end > n
    with eng.Fori(0, end // n) as i:
        for r in range(n):
            body(i * n + r, r)


def stage_setup(nc, k, ctx, d):
    def sb(name, shape, dt=F32):
        return ctx.enter_context(nc.sbuf_tensor(name, shape, dt))

    k.ps = ctx.enter_context(nc.psum_tensor("ps", [P, 8, 512], F32))
    k.x = sb("x", [P, NT, C])
    k.xT = sb("xT", [P, NT * P])
    k.ident = sb("ident", [P, P])
    k.identb = sb("identb", [P, P], BF16)
    k.mask_qk = sb("mask_qk", [P, P], BF16)
    k.mask_kq = sb("mask_kq", [P, P], BF16)
    k.keep_kq = sb("keep_kq", [P, P])
    k.ones = sb("ones", [P, P])
    k.col = sb("col", [P, COL_N])
    k.row = sb("row", [P, ROW_N])
    k.eps = sb("eps", [P, 1])
    k.ln_st = sb("ln_st", [P, NT, 6])
    k.ln_mv = sb("ln_mv", [P, NT, 2])
    k.ln_lg = sb("ln_lg", [P, NT])
    k.ln_rs = sb("ln_rs", [P, NT])
    for name in ("loaded", "filled", "mm", "read", "read2", "mm2", "st1", "st2", "act", "act2", "pool", "vec",
                 "scores", "scores_read", "negmax", "shift_t", "shift_in", "st_ready", "exp_done",
                 "probs_used", "out_read", "masked", "ops0", "ops1", "ops2", "ops3", "weights0", "weights1",
                 "wrote0", "wrote1", "wrote2", "wrote3", "vwrote0", "vwrote1", "vwrote2", "vwrote3", "out"):
        k.sems[name] = Sem(ctx, nc, name)
    sems = k.sems
    with nc.Block() as block:
        @block.sync
        def _(sp):
            for s in sems.values():
                sp.sem_inc(s.s, CREDIT)
            sp.dma_start(k.col[:, :], d["col"]).then_inc(sems["loaded"].s, 16)
            sp.dma_start(k.row[:, :], d["row"].broadcast_to([P, ROW_N])).then_inc(sems["loaded"].s, 16)
            sp.dma_start(k.x[:, :, :], d["x"].rearrange("(t p) c -> p t c", p=P)).then_inc(sems["loaded"].s, 16)
    with nc.Block() as block:
        @block.sync
        def _(sp):
            sp.wait_ge(sems["loaded"].s, sems["loaded"].at(48))

        @block.gpsimd
        def _(g):
            f = sems["filled"]
            g.memset(k.ident[:, :], 0.0).then_inc(f.s, 1)
            g.memset(k.mask_qk[:, :], 0.0).then_inc(f.s, 1)
            g.memset(k.mask_kq[:, :], 0.0).then_inc(f.s, 1)
            g.memset(k.keep_kq[:, :], 0.0).then_inc(f.s, 1)
            g.memset(k.ones[:, :], 1.0).then_inc(f.s, 1)
            g.memset(k.eps[:, :], EPS).then_inc(f.s, 1)
            g.wait_ge(f.s, f.at(6))
            g.affine_select(out=k.ident[:, :], in_=k.ident[:, :], compare_op=ALU.not_equal, fill=1.0,
                            base=0, pattern=[[-1, P]], channel_multiplier=1).then_inc(f.s, 1)
            g.affine_select(out=k.mask_qk[:, :], in_=k.mask_qk[:, :], compare_op=ALU.is_ge, fill=NEG,
                            base=0, pattern=[[-1, P]], channel_multiplier=1).then_inc(f.s, 1)
            g.affine_select(out=k.mask_kq[:, :], in_=k.mask_kq[:, :], compare_op=ALU.is_ge, fill=NEG,
                            base=0, pattern=[[1, P]], channel_multiplier=-1).then_inc(f.s, 1)
            g.affine_select(out=k.keep_kq[:, :], in_=k.keep_kq[:, :], compare_op=ALU.is_ge, fill=1.0,
                            base=0, pattern=[[1, P]], channel_multiplier=-1).then_inc(f.s, 1)
            g.wait_ge(f.s, f.at(10))
            g.tensor_copy(k.identb[:, :], k.ident[:, :]).then_inc(f.s, 1)
            g.wait_ge(f.s, f.at(11))
    sems["loaded"].passed(48)
    sems["filled"].passed(11)


def stage_norm(nc, k, src, dst, gain=None, shift=None):
    vec, act = k.sems["vec"], k.sems["act"]
    nv = [0]
    with nc.Block() as block:
        @block.vector
        def _(v):
            for t in range(NT):
                ins = v.bn_stats(k.ln_st[:, t, :], src[:, t, :])
            ins.then_inc(vec.s, 1)
            v.wait_ge(vec.s, vec.at(1))
            for t in range(NT):
                ins = v.bn_aggr(k.ln_mv[:, t, :], k.ln_st[:, t, :])
            ins.then_inc(vec.s, 1)
            v.wait_ge(act.s, act.at(2))
            for t in range(NT):
                ins = v.tensor_scalar(dst[:, t, :], src[:, t, :], k.ln_mv[:, t, 0:1], k.ln_rs[:, t:t + 1],
                                      ALU.subtract, ALU.mult)
            ins.then_inc(vec.s, 1)
            nv[0] = 3
            if gain is not None:
                g3 = gain.unsqueeze(1).broadcast_to([P, NT, C])
                b3 = shift.unsqueeze(1).broadcast_to([P, NT, C])
                v.wait_ge(vec.s, vec.at(3))
                v.tensor_tensor(dst[:, :, :], dst[:, :, :], g3, ALU.mult).then_inc(vec.s, 1)
                v.wait_ge(vec.s, vec.at(4))
                v.tensor_tensor(dst[:, :, :], dst[:, :, :], b3, ALU.add).then_inc(vec.s, 1)
                nv[0] = 5

        @block.scalar
        def _(a):
            a.wait_ge(vec.s, vec.at(2))
            a.activation(k.ln_lg[:, :], k.ln_mv[:, :, 1], ACT.Ln, bias=k.eps[:, 0:1]).then_inc(act.s, 1)
            a.wait_ge(act.s, act.at(1))
            a.activation(k.ln_rs[:, :], k.ln_lg[:, :], ACT.Exp, scale=-0.5).then_inc(act.s, 1)
    vec.passed(nv[0])
    act.passed(2)


def stage_transpose(nc, k, src, outs):
    mm, read = k.sems["mm"], k.sems["read"]
    with nc.Block() as block:
        @block.tensor
        def _(pe):
            for t in range(NT):
                ins = pe.transpose(k.ps[:, t // 4, (t % 4) * P:(t % 4 + 1) * P], src[:, t, :], k.ident[:, :])
                if t % 4 == 3:
                    ins.then_inc(mm.s, 1)

        @block.vector
        def _(v):
            for half in range(2):
                v.wait_ge(mm.s, mm.at(half + 1))
                for dst, gain, shift in outs:
                    o = dst[:, half * 512:(half + 1) * 512]
                    if gain is None:
                        v.tensor_copy(o, k.ps[:, half, :]).then_inc(read.s, 1)
                    else:
                        v.tensor_scalar(o, k.ps[:, half, :], gain, shift, ALU.mult, ALU.add).then_inc(read.s, 1)
    mm.passed(2)
    read.passed(2 * len(outs))


def stage_load(nc, k, moves):
    loaded = k.sems["loaded"]
    with nc.Block() as block:
        @block.sync
        def _(sp):
            for dst, src in moves:
                sp.dma_start(dst, src).then_inc(loaded.s, 16)
            sp.wait_ge(loaded.s, loaded.at(16 * len(moves)))
    loaded.passed(16 * len(moves))


class Scratch:

    def __init__(self, nc, name, D, T, which, exact=False):
        self.D, self.T = D, T
        self.exact = exact
        self.passes = 1 if exact or 6 * D <= P else 2
        self.spp = 1 if exact else 6 // self.passes
        self.R = D * self.spp
        self.ap = nc.dram_tensor(name, (self.passes, BH * D, self.spp, T), F32 if exact else BF16,
                                 kind="Internal").ap()
        part = (Q_PART if which == "q" else K_PART)[self.passes]
        self.moves = []
        for n, p in enumerate(part):
            ps, sl = divmod(n, self.spp) if not exact else (0, 0)
            if self.moves and self.moves[-1][0] == ps:
                mp, ms, mn, m0, rep = self.moves[-1]
                if p == m0 and (mn == 1 or rep):
                    self.moves[-1] = (mp, ms, mn + 1, m0, True)
                    continue
                if p == m0 + mn and not rep:
                    self.moves[-1] = (mp, ms, mn + 1, m0, False)
                    continue
            self.moves.append((ps, sl, 1, p, False))

    def store(self, sp, sem, row0, tile, col0, width):
        for ps, slot, n, part, rep in self.moves:
            i = tile[:, part:part + 1, :].broadcast_to([P, n, width]) if rep else tile[:, part:part + n, :]
            sp.dma_start(self.ap[ps, bass.ds(row0, P), slot:slot + n, col0:col0 + width], i).then_inc(sem.s, 16)


class Values:

    def __init__(self, nc, name, D, T):
        self.D, self.T = D, T
        self.DP = max(D, 32)
        self.G = P // self.DP
        self.NB = H // self.G
        self.ap = nc.dram_tensor(name, (B * self.NB, T, P), F32, kind="Internal").ap()

    def store(self, sp, sem, b, t0, n, tile):
        sp.dma_start(self.ap[bass.ds(b * self.NB, self.NB), t0:t0 + n, :].rearrange("k t c -> t k c"),
                     tile[0:n, :].rearrange("p (k c) -> p k c", c=P)).then_inc(sem.s, 16)


RING = 4
LAG = 2


def stage_project(nc, k, name, heads, values):
    mm, read, act, vec, pool = (k.sems[n] for n in ("mm", "read", "act", "vec", "pool"))
    wrote = [k.sems["wrote%d" % n] for n in range(RING)]
    vwrote = [k.sems["vwrote%d" % n] for n in range(RING)]
    units = [(item, c) for item in heads for c in range(2)]
    U = len(units)
    NV = NT if values else 0
    stored = [0] * RING
    before = []
    for u, (item, c) in enumerate(units):
        before.append(stored[u % RING])
        stored[u % RING] += 16 * 2 * len(item[3].moves)
    if values:
        vsrc, vw, vbias, vals = values
        D, DP = vals.D, vals.DP
    with ExitStack() as ctx:
        full = ctx.enter_context(nc.sbuf_tensor(name + "_full", [P, RING, 512], F32))
        rest = ctx.enter_context(nc.sbuf_tensor(name + "_rest", [P, RING, 512], F32))
        part = ctx.enter_context(nc.sbuf_tensor(name + "_part", [P, RING, 3, 512], BF16))
        if values:
            vt = ctx.enter_context(nc.sbuf_tensor(name + "_vt", [P, RING, H * DP], F32))
            if DP > D:
                with nc.Block() as block:
                    @block.vector
                    def _(v):
                        v.memset(vt[:, :, :], 0.0)
        with nc.Block() as block:
            @block.tensor
            def _(pe):
                for u, ((srcT, w, bias, scr, row0), c) in enumerate(units):
                    pe.wait_ge(vec.s, vec.at(halves(u - 4)))
                    pe.matmul(k.ps[:, u % 4, :], w, srcT[:, c * 512:(c + 1) * 512],
                              start=True, stop=True).then_inc(mm.s, 1)
                for t in range(NV):
                    pe.wait_ge(read.s, read.at(t - 3))
                    pe.matmul(k.ps[:, 4 + t % 4, 0:H * D], vsrc[:, t * P:(t + 1) * P], vw,
                              start=True, stop=True).then_inc(mm.s, 1)

            @block.scalar
            def _(a):
                for u in range(U + LAG):
                    if u < U:
                        bias = units[u][0][2]
                        a.wait_ge(mm.s, mm.at(u + 1))
                        a.wait_ge(vec.s, vec.at(halves(u - RING)))
                        if bias is None:
                            ins = a.activation(full[:, u % RING, :], k.ps[:, u % 4, :], ACT.Copy)
                        else:
                            ins = a.activation(full[:, u % RING, :], k.ps[:, u % 4, :], ACT.Identity, bias=bias)
                        ins.then_inc(act.s, 1)
                    if u >= LAG:
                        w_ = u - LAG
                        a.wait_ge(pool.s, pool.at(w_ + 1))
                        a.activation(part[:, w_ % RING, 1, :], rest[:, w_ % RING, :], ACT.Copy).then_inc(act.s, 1)

            @block.vector
            def _(v):
                for u in range(U + LAG):
                    if u < U:
                        v.wait_ge(act.s, act.at(firsts(u)))
                        v.wait_ge(wrote[u % RING].s, wrote[u % RING].at(before[u]))
                        v.tensor_copy(part[:, u % RING, 0, :], full[:, u % RING, :]).then_inc(vec.s, 1)
                    if u >= LAG:
                        w_ = u - LAG
                        v.wait_ge(act.s, act.at(seconds(w_, U)))
                        v.tensor_tensor(part[:, w_ % RING, 2, :], rest[:, w_ % RING, :], part[:, w_ % RING, 1, :],
                                        ALU.subtract).then_inc(vec.s, 1)
                for t in range(NV):
                    v.wait_ge(mm.s, mm.at(U + t + 1))
                    v.wait_ge(vwrote[t % RING].s, vwrote[t % RING].at(16 * (t // RING)))
                    o = vt[:, t % RING, :].rearrange("p (h d) -> p h d", d=DP)[:, :, 0:D]
                    i = k.ps[:, 4 + t % 4, 0:H * D].rearrange("p (h d) -> p h d", d=D)
                    if vbias is None:
                        v.tensor_copy(o, i).then_inc(read.s, 1)
                    else:
                        v.tensor_tensor(o, i, vbias.rearrange("p (h d) -> p h d", d=D), ALU.add).then_inc(read.s, 1)

            @block.gpsimd
            def _(g):
                for u in range(U):
                    g.wait_ge(vec.s, vec.at(firsts(u)))
                    g.tensor_tensor(rest[:, u % RING, :], full[:, u % RING, :], part[:, u % RING, 0, :],
                                    ALU.subtract).then_inc(pool.s, 1)

            @block.sync
            def _(sp):
                for u, ((srcT, w, bias, scr, row0), c) in enumerate(units):
                    sp.wait_ge(vec.s, vec.at(seconds(u, U)))
                    for bb in range(2):
                        scr.store(sp, wrote[u % RING], (2 * c + bb) * H * scr.D + row0,
                                  part[:, u % RING, :, bb * N:(bb + 1) * N], 0, N)
                for t in range(NV):
                    sp.wait_ge(read.s, read.at(t + 1))
                    vals.store(sp, vwrote[t % RING], t // 2, (t % 2) * P, P, vt[:, t % RING, :])
                for n in range(RING):
                    sp.wait_ge(wrote[n].s, wrote[n].at(stored[n]))
                    sp.wait_ge(vwrote[n].s, vwrote[n].at(16 * NV // RING))
    mm.passed(U + NV)
    act.passed(2 * U)
    vec.passed(2 * U)
    pool.passed(U)
    read.passed(NV)
    for n in range(RING):
        wrote[n].passed(stored[n])
        vwrote[n].passed(16 * NV // RING)


def firsts(u):
    return u + 1 + max(0, u - LAG)


def seconds(u, total):
    return min(u + LAG + 1, total) + u + 1


def halves(u):
    return 0 if u < 0 else u + LAG + 1 + u + 1


def stage_attention(nc, k, name, T, scale, mask, qs, ks, vals, out):
    cross = T == T_CTX
    fp32 = qs.exact
    dt = F32 if fp32 else BF16
    passes, R, G, DP = qs.passes, qs.R, vals.G, vals.DP
    SR = 64 if fp32 else 96
    NSH = 1 if fp32 else 2
    RS = R if fp32 else SR
    ident = k.ident if fp32 else k.identb
    NS = BH // G
    KT = KT_CTX if cross else 2
    NBUF = 2 if cross else 4
    CW = 401
    if cross:
        slots = [(qt, g, 1, c) for g in range(G) for qt in range(2) for c in range(4)]
    elif mask == "causal":
        slots = [(0, 0, G, 0), (1, 0, 2, 0), (1, 2, 2, 0)]
    else:
        slots = [(qt, g, 2, 0) for qt in range(2) for g in range(0, G, 2)]
    groups = [[kt] for kt in range(KT)] if G == 4 else [[0, 1]]
    NSL, NG = len(slots), len(groups)
    (scores, scores_read, negmax, shift_t, shift_in, st_ready, exp_done, probs_used, out_read,
     masked, vec, filled) = (k.sems[n] for n in (
         "scores", "scores_read", "negmax", "shift_t", "shift_in", "st_ready", "exp_done", "probs_used",
         "out_read", "masked", "vec", "filled"))
    ops = [k.sems["ops%d" % n] for n in range(NBUF)]
    NDMA = 2 * passes + (2 if cross else 1)
    VI = cross + (not fp32)
    NF = 5 if RS > R else 1
    assert probs_used.base > (NBUF - 1) * NG

    with ExitStack() as ctx:
        def sb(n, shape, dtype=F32):
            return ctx.enter_context(nc.sbuf_tensor(name + "_" + n, shape, dtype))

        qb = sb("qb", [SR + NSH, NBUF, passes, G, N], dt)
        kb = sb("kb", [SR + NSH, NBUF, passes, G, T], dt)
        vs = sb("vs", [P, NBUF, KT, P])
        prob = sb("prob", [P, 2, 1024])
        pm = sb("pm", [P, 2, 2, G, P]) if mask == "after" else None
        mxp = sb("mxp", [P, 2 * G, 4]) if cross else None
        mx = sb("mx", [P, 2 * G])
        negm = sb("negm", [P, 2 * G, NSH], dt)
        rden = sb("rden", [P, N])

        def rows_of(p, shifted):
            return SR + NSH if shifted and p == 0 else (RS if p == 0 else R)

        def st_columns(g, kt):
            if G < 4:
                return (kt * G + g) * N, 0
            if mask == "causal" and kt == 1:
                return g * P, P
            return g * N, 0

        def tile_rows(kt):
            return TAIL if cross and kt == KT - 1 else P

        with nc.Block() as block:
            @block.sync
            def _(sp):
                def load(s, buf):
                    sp.wait_ge(probs_used.s, s * NG + (probs_used.base - (NBUF - 1) * NG))
                    for p in range(passes):
                        for dst, scr in ((qb, qs), (kb, ks)):
                            v = scr.ap[p].rearrange("r s t -> (r s) t")[bass.ds(s * (G * R), G * R), :]
                            sp.dma_start(dst[0:R, buf, p, :, :],
                                         v.rearrange("(g r) t -> r g t", g=G)).then_inc(ops[buf].s, 16)
                    v = vals.ap[bass.ds(s, 1), :, :].rearrange("s t c -> (s t) c")
                    if cross:
                        n = T_CTX - TAIL
                        sp.dma_start(vs[:, buf, 0:KT - 1, :], v[0:n, :].rearrange("(k p) c -> p k c", p=P)).then_inc(
                            ops[buf].s, 16)
                        sp.dma_start(vs[0:TAIL, buf, KT - 1, :], v[n:T_CTX, :]).then_inc(ops[buf].s, 16)
                    else:
                        sp.dma_start(vs[:, buf, :, :], v.rearrange("(k p) c -> p k c", p=P)).then_inc(ops[buf].s, 16)

                sp.wait_ge(filled.s, filled.at(NF))
                rounds(sp, NS, NBUF, load)

            @block.tensor
            def _(pe):
                def score_slot(s, buf, j):
                    qt, g0, ng, c = slots[j]
                    if j == 0:
                        pe.wait_ge(ops[buf].s, (s - buf) * (16 * NDMA // NBUF) + (16 * NDMA + ops[buf].base))
                    pe.wait_ge(scores_read.s, (s * NSL + (j - 1)) + scores_read.base)
                    bank = k.ps[:, (buf * NSL + j) % 2, :]
                    n = CW if cross else (P if mask == "causal" and qt == 0 else N)
                    k0 = c * (CW - 1)
                    for g in range(g0, g0 + ng):
                        o = bank[:, (g - g0) * n:(g - g0 + 1) * n]
                        r = rows_of(0, False)
                        ins = pe.matmul(o, qb[0:r, buf, 0, g, qt * P:(qt + 1) * P], kb[0:r, buf, 0, g, k0:k0 + n],
                                        start=True, stop=True)
                        if mask == "causal":
                            ins = pe.matmul(o[:, n - P:n], k.identb[:, :], k.mask_qk[:, :],
                                            start=False, stop=True, skip_group_check=True)
                    ins.then_inc(scores.s, 1)

                def shift_rows(s):
                    pe.wait_ge(negmax.s, (s + 1) + negmax.base)
                    for g in range(G):
                        for qt in range(2):
                            r0 = 32 * (g // 2)
                            c0 = (g % 2) * N + qt * P
                            ins = pe.matmul(k.ps[r0:r0 + NSH, 7, c0:c0 + P], negm[:, qt * G + g, :], ident[:, :],
                                            start=True, stop=True)
                    ins.then_inc(shift_t.s, 1)

                def transposed_scores(s, buf, grp):
                    ring = (buf * NG + grp) % 2
                    if grp == 0:
                        pe.wait_ge(shift_in.s, (s + 1) + shift_in.base)
                    pe.wait_ge(exp_done.s, (s * NG + (grp - 1)) + exp_done.base)
                    banks = k.ps[:, 2 + 2 * ring:4 + 2 * ring, :].rearrange("p a b -> p (a b)")
                    for kt in groups[grp]:
                        rows = tile_rows(kt)
                        for g in range(G):
                            c, q0 = st_columns(g, kt)
                            o = banks[0:rows, c:c + N - q0]
                            for p in range(passes):
                                r = rows_of(p, True)
                                ins = pe.matmul(o, kb[0:r, buf, p, g, kt * P:kt * P + rows],
                                                qb[0:r, buf, p, g, q0:N], start=(p == 0), stop=(p == passes - 1))
                            if mask == "causal":
                                ins = pe.matmul(o[:, 0:P], k.identb[:, :], k.mask_kq[:, :],
                                                start=False, stop=True, skip_group_check=True)
                    ins.then_inc(st_ready.s, 1)

                def weigh(s, buf, grp):
                    ring = (buf * NG + grp) % 2
                    pe.wait_ge(exp_done.s, (s * NG + (grp + 1)) + exp_done.base)
                    if grp == 0:
                        pe.wait_ge(out_read.s, s + out_read.base)
                    if mask == "after":
                        pe.wait_ge(masked.s, (s * NG + (grp + 1)) + masked.base)
                    for kt in groups[grp]:
                        rows = tile_rows(kt)
                        last = kt == KT - 1
                        for ones in (False, True):
                            for g in range(G):
                                c, q0 = st_columns(g, kt)
                                w = k.ones[0:rows, 0:DP] if ones else vs[0:rows, buf, kt, g * DP:(g + 1) * DP]
                                o = k.ps[g * DP:(g + 1) * DP, 6, (N if ones else 0):(2 * N if ones else N)]
                                pr = prob[0:rows, ring, c:c + N - q0]
                                if ones or mask != "after":
                                    ins = pe.matmul(o[:, q0:N], w, pr, start=(kt == 0 and not ones), stop=last,
                                                    skip_group_check=True)
                                    continue
                                ins = pe.matmul(o[:, kt * P:(kt + 1) * P], w, pm[:, ring, kt, g, :], start=(kt == 0),
                                                stop=last, skip_group_check=True)
                                if kt == 1:
                                    ins = pe.matmul(o[:, 0:P], w, pr[:, 0:P], start=False, stop=last,
                                                    skip_group_check=True)
                    ins.then_inc(probs_used.s, 1)

                def step(s, buf, more=True):
                    for grp in range(NG):
                        transposed_scores(s, buf, grp)
                        if more:
                            for j in range(grp * NSL // NG, (grp + 1) * NSL // NG):
                                score_slot(s + 1, (buf + 1) % NBUF, j)
                        if grp:
                            weigh(s, buf, grp - 1)
                    if more:
                        shift_rows(s + 1)
                    weigh(s, buf, NG - 1)

                pe.wait_ge(filled.s, filled.at(NF))
                for j in range(NSL):
                    score_slot(0, 0, j)
                shift_rows(0)
                rounds(pe, NS - NBUF, NBUF, step)
                for r in range(NBUF):
                    step(NS - NBUF + r, r, more=(r < NBUF - 1))

            @block.vector
            def _(v):
                def maxima(s, buf, before):
                    for j, (qt, g0, ng, c) in enumerate(slots):
                        v.wait_ge(scores.s, (s * NSL + (j + 1)) + scores.base)
                        bank = k.ps[:, (buf * NSL + j) % 2, :]
                        if cross:
                            i, o = bank[:, 0:CW], mxp[:, qt * G + g0, c:c + 1]
                        else:
                            n = P if mask == "causal" and qt == 0 else N
                            i = bank[:, 0:ng * n].rearrange("p (g n) -> p g n", g=ng)
                            o = mx[:, qt * G + g0:qt * G + g0 + ng]
                        v.tensor_reduce(o, i, AX.X, ALU.max).then_inc(scores_read.s, 1)
                    v.wait_ge(scores_read.s, (s + 1) * NSL + scores_read.base)
                    done = before
                    if cross:
                        v.tensor_reduce(mx[:, :], mxp[:, :, :], AX.X, ALU.max).then_inc(vec.s, 1)
                        done = done + 1
                        v.wait_ge(vec.s, done)
                    if fp32:
                        v.tensor_scalar(negm[:, :, 0], mx[:, :], -1.0, None, ALU.mult).then_inc(negmax.s, 1)
                    else:
                        v.tensor_scalar(negm[:, :, 0], mx[:, :], -1.0, None, ALU.mult).then_inc(vec.s, 1)
                        v.wait_ge(vec.s, done + 1)
                        v.scalar_tensor_tensor(out=negm[:, :, 1], in0=mx[:, :], scalar=-1.0, in1=negm[:, :, 0],
                                               op0=ALU.mult, op1=ALU.subtract).then_inc(negmax.s, 1)

                def outputs(s, before):
                    v.wait_ge(probs_used.s, (s + 1) * NG + probs_used.base)
                    v.reciprocal(rden[:, :], k.ps[:, 6, N:2 * N]).then_inc(vec.s, 1)
                    v.wait_ge(vec.s, before + 1)
                    v.tensor_tensor(out[:, bass.ds(s * N, N)], k.ps[:, 6, 0:N], rden[:, :],
                                    ALU.mult).then_inc(out_read.s, 1)

                maxima(0, 0, vec.base)

                def both(s, buf):
                    maxima(s + 1, (buf + 1) % NBUF, s * (VI + 1) + (VI + vec.base))
                    outputs(s, s * (VI + 1) + (2 * VI + vec.base))

                rounds(v, NS - NBUF, NBUF, both)
                for r in range(NBUF - 1):
                    both(NS - NBUF + r, r)
                outputs(NS - 1, NS * (VI + 1) - 1 + vec.base)

            @block.scalar
            def _(a):
                def shift(s, buf):
                    a.wait_ge(shift_t.s, (s + 1) + shift_t.base)
                    for g in range(0, G, 2):
                        ins = a.activation(qb[SR:SR + NSH, buf, 0, g:g + 2, :].rearrange("p g n -> p (g n)"),
                                           k.ps[16 * g:16 * g + NSH, 7, 0:2 * N], ACT.Copy)
                    ins.then_inc(shift_in.s, 1)

                def exps(s, buf):
                    for grp in range(NG):
                        ring = (buf * NG + grp) % 2
                        rows = tile_rows(groups[grp][-1])
                        n = G * P if mask == "causal" and grp == 1 else len(groups[grp]) * G * N
                        a.wait_ge(st_ready.s, (s * NG + (grp + 1)) + st_ready.base)
                        a.wait_ge(probs_used.s, (s * NG + (grp - 1)) + probs_used.base)
                        banks = k.ps[:, 2 + 2 * ring:4 + 2 * ring, :].rearrange("p a b -> p (a b)")
                        a.activation(prob[0:rows, ring, 0:n], banks[0:rows, 0:n], ACT.Exp,
                                     scale=scale).then_inc(exp_done.s, 1)

                def both(s, buf):
                    exps(s, buf)
                    shift(s + 1, (buf + 1) % NBUF)

                shift(0, 0)
                rounds(a, NS - NBUF, NBUF, both)
                for r in range(NBUF - 1):
                    both(NS - NBUF + r, r)
                exps(NS - 1, NBUF - 1)

            @block.gpsimd
            def _(g_):
                if RS > R:
                    for buf in (kb, qb):
                        for r in (32, 64):
                            g_.memset(buf[r:r + 32, :, :, :, :], 0.0).then_inc(filled.s, 1)
                g_.memset(kb[SR:SR + NSH, :, 0, :, :], 1.0).then_inc(filled.s, 1)
                g_.wait_ge(filled.s, filled.at(NF))

                def masks(s, buf):
                    keep = k.keep_kq[:, :].unsqueeze(1).broadcast_to([P, G, P])
                    for kt in range(2):
                        ring = (buf * NG + kt) % 2
                        g_.wait_ge(exp_done.s, (s * NG + (kt + 1)) + exp_done.base)
                        g_.wait_ge(probs_used.s, (s * NG + (kt - 1)) + probs_used.base)
                        i = prob[:, ring, :].rearrange("p (g n) -> p g n", g=G)
                        g_.tensor_tensor(pm[:, ring, kt, :, :], i[:, :, kt * P:(kt + 1) * P], keep,
                                         ALU.mult).then_inc(masked.s, 1)

                if mask == "after":
                    rounds(g_, NS, NBUF, masks)

    for s_, n_ in [(scores, NS * NSL), (scores_read, NS * NSL), (negmax, NS), (shift_t, NS), (shift_in, NS),
                   (st_ready, NS * NG), (exp_done, NS * NG), (probs_used, NS * NG), (out_read, NS),
                   (masked, NS * NG if mask == "after" else 0), (vec, (VI + 1) * NS), (filled, NF)] \
            + [(o, NS // NBUF * 16 * NDMA) for o in ops]:
        s_.passed(n_)


def stage_output(nc, k, terms, w, bias):
    mm2, vec = k.sems["mm2"], k.sems["vec"]
    nb = w.shape[1] // C
    with nc.Block() as block:
        @block.gpsimd
        def _(g):
            if bias is not None:
                g.tensor_tensor(k.x[:, :, :], k.x[:, :, :], bias.unsqueeze(1).broadcast_to([P, NT, C]),
                                ALU.add).then_inc(k.sems["pool"].s, 1)

        @block.tensor
        def _(pe):
            for t in range(NT):
                todo = [(o, j) for o in terms for j in range(nb)]
                for n, (o, j) in enumerate(todo):
                    c0 = ((t // 2) * nb + j) * N + (t % 2) * P
                    ins = pe.matmul(k.ps[:, t // 4, (t % 4) * P:(t % 4 + 1) * P], o[:, c0:c0 + P],
                                    w[:, j * C:(j + 1) * C], start=(n == 0), stop=(n == len(todo) - 1))
                if t % 4 == 3:
                    ins.then_inc(mm2.s, 1)

        @block.vector
        def _(v):
            if bias is not None:
                v.wait_ge(k.sems["pool"].s, k.sems["pool"].at(1))
            for half in range(2):
                v.wait_ge(mm2.s, mm2.at(half + 1))
                xs = k.x[:, half * 4:half * 4 + 4, :].rearrange("p t c -> p (t c)")
                v.tensor_tensor(xs, k.ps[:, half, :], xs, ALU.add).then_inc(vec.s, 1)
    mm2.passed(2)
    vec.passed(2)
    if bias is not None:
        k.sems["pool"].passed(1)


def stage_project_rotary(nc, k, w1, wf, qs, ks, values):
    mm, read, vec, pool, act = (k.sems[n] for n in ("mm", "read", "vec", "pool", "act"))
    wrote = (k.sems["wrote0"], k.sems["wrote1"])
    D = 64
    units = [(which, j, c) for which in "qk" for j in range(8) for c in range(2)]
    vunits = [(t, half) for t in range(NT) for half in range(2)]
    vwrote = [k.sems["vwrote%d" % n] for n in range(RING)]
    with ExitStack() as ctx:
        vt = ctx.enter_context(nc.sbuf_tensor("rot_vt", [P, RING, H * D], F32))
        fenc = ctx.enter_context(nc.sbuf_tensor("fenc", [P, N], F32))
        turned = ctx.enter_context(nc.sbuf_tensor("turned", [P, 2, 2, 512], F32))
        full = ctx.enter_context(nc.sbuf_tensor("rot_full", [P, 2, 512], F32))
        with nc.Block() as block:
            @block.tensor
            def _(pe):
                pe.matmul(k.ps[:, 7, 0:N], sub(wf, WF, "fp", 32), sub(wf, WF, "fourier", 32),
                          start=True, stop=True).then_inc(mm.s, 1)

            @block.scalar
            def _(a):
                a.wait_ge(mm.s, mm.at(1))
                a.activation(fenc[:, :], k.ps[:, 7, 0:N], ACT.Identity,
                             bias=sub(k.col, COL, "fp")).then_inc(act.s, 1)
        mm.passed(1)
        act.passed(1)
        with nc.Block() as block:
            @block.tensor
            def _(pe):
                for u, (which, j, c) in enumerate(units):
                    pe.wait_ge(vec.s, vec.at(2 * (u - 1)))
                    for r, suffix in enumerate(("", "r")):
                        a0 = W1[which + suffix][0] + j * P
                        ins = pe.matmul(k.ps[:, (u % 2) * 2 + r, :], w1[:, a0:a0 + P],
                                        k.xT[:, c * 512:(c + 1) * 512], start=True, stop=True)
                    ins.then_inc(mm.s, 1)
                for u, (t, half) in enumerate(vunits):
                    pe.wait_ge(act.s, act.at(u - 3))
                    a0 = W1["v"][0] + half * 512
                    pe.matmul(k.ps[:, 4 + u % 4, :], k.xT[:, t * P:(t + 1) * P], w1[:, a0:a0 + 512],
                              start=True, stop=True).then_inc(mm.s, 1)

            @block.vector
            def _(v):
                for u, (which, j, c) in enumerate(units):
                    v.wait_ge(mm.s, mm.at(u + 1))
                    v.wait_ge(pool.s, pool.at(2 * (u - 1)))
                    for r, table in enumerate(("cos", "sin")):
                        v.tensor_tensor(turned[:, u % 2, r, :].rearrange("p (b n) -> p b n", b=2),
                                        k.ps[:, (u % 2) * 2 + r, :].rearrange("p (b n) -> p b n", b=2),
                                        sub(w1, W1, table).unsqueeze(1).broadcast_to([P, 2, N]),
                                        ALU.mult).then_inc(vec.s, 1)

            @block.gpsimd
            def _(g):
                for u, (which, j, c) in enumerate(units):
                    g.wait_ge(vec.s, vec.at(2 * u + 2))
                    g.wait_ge(wrote[u % 2].s, wrote[u % 2].at(16 * (u // 2)))
                    g.tensor_tensor(full[:, u % 2, :], turned[:, u % 2, 0, :], turned[:, u % 2, 1, :],
                                    ALU.add).then_inc(pool.s, 1)
                    g.wait_ge(pool.s, pool.at(2 * u + 1))
                    f3 = full[:, u % 2, :].rearrange("p (b n) -> p b n", b=2)
                    g.tensor_tensor(f3, f3, fenc[:, :].unsqueeze(1).broadcast_to([P, 2, N]),
                                    ALU.add).then_inc(pool.s, 1)

            @block.scalar
            def _(a):
                for u, (t, half) in enumerate(vunits):
                    a.wait_ge(mm.s, mm.at(len(units) + u + 1))
                    a.wait_ge(vwrote[t % RING].s, vwrote[t % RING].at(16 * (t // RING)))
                    a.activation(vt[:, t % RING, half * 512:(half + 1) * 512], k.ps[:, 4 + u % 4, :],
                                 ACT.Copy).then_inc(act.s, 1)

            @block.sync
            def _(sp):
                for u, (which, j, c) in enumerate(units):
                    sp.wait_ge(pool.s, pool.at(2 * u + 2))
                    dst = (qs if which == "q" else ks).ap[0].rearrange("(b r) s t -> r b (s t)", b=B)
                    sp.dma_start(dst[j * P:(j + 1) * P, 2 * c:2 * c + 2, :],
                                 full[:, u % 2, :].rearrange("p (b n) -> p b n", b=2)).then_inc(wrote[u % 2].s, 16)
                for t in range(NT):
                    sp.wait_ge(act.s, act.at(2 * t + 2))
                    values.store(sp, vwrote[t % RING], t // 2, (t % 2) * P, P, vt[:, t % RING, :])
                for n in range(2):
                    sp.wait_ge(wrote[n].s, wrote[n].at(16 * len(units) // 2))
                for n in range(RING):
                    sp.wait_ge(vwrote[n].s, vwrote[n].at(16 * NT // RING))
    mm.passed(len(units) + len(vunits))
    vec.passed(2 * len(units))
    pool.passed(2 * len(units))
    act.passed(len(vunits))
    for w_ in vwrote:
        w_.passed(16 * NT // RING)
    for n in range(2):
        wrote[n].passed(16 * len(units) // 2)


def stage_context(nc, k, name, wk, wv, kbias, vbias, scratch, vals, ctxT=None, ctx_rows=None,
                  gain=None, shift=None):
    norm = ctx_rows is not None
    D, DP = vals.D, vals.DP
    HD = H * D
    widths = [401, 400, 400, 400]
    starts = [0, 401, 801, 1201]
    units = [(j, c) for j in range(HD // P) for c in range(4)]
    U = len(units)
    NTR = 4 if norm else 0
    RD = NTR + KT_CTX
    MM = NTR + U + KT_CTX
    ND = 16 * len(scratch.moves)
    NV = 2 * U + (3 if norm else 0)
    NA = 2 * U + (2 if norm else 0)
    NLOAD = 32 if norm else 16
    VN = [len(range(r, KT_CTX, RING)) * 16 for r in range(RING)]
    mm, read, act, vec, pool, loaded = (k.sems[n] for n in ("mm", "read", "act", "vec", "pool", "loaded"))
    wrote = [k.sems["wrote%d" % n] for n in range(RING)]
    vwrote = [k.sems["vwrote%d" % n] for n in range(RING)]
    va, vv = act.base + NA - 2 * U, vec.base + NV - 2 * U
    with ExitStack() as ctx:
        def sb(n, shape, dtype=F32):
            return ctx.enter_context(nc.sbuf_tensor(name + "_" + n, shape, dtype))

        cT = sb("cT", [CC, KT_CTX * P if norm else T_CTX])
        full = sb("full", [P, RING, 401])
        rest = sb("rest", [P, RING, 401])
        part = sb("part", [P, RING, 3, 401], BF16)
        vt = sb("vt", [P, RING, H * DP])
        if norm:
            rows = sb("rows", [P, KT_CTX, CC])
            st = sb("st", [P, KT_CTX, 6])
            mv = sb("mv", [P, KT_CTX, 2])
            lg = sb("lg", [P, KT_CTX])
            rs = sb("rs", [P, KT_CTX])
        with nc.Block() as block:
            @block.gpsimd
            def _(g):
                if norm:
                    g.memset(rows[:, KT_CTX - 1, :], 0.0)

            @block.vector
            def _(v):
                if DP > D:
                    v.memset(vt[:, :, :], 0.0)
        with nc.Block() as block:
            @block.sync
            def _(sp):
                with sp.Fori(0, B) as b:
                    sp.wait_ge(mm.s, b * MM + mm.base)
                    if norm:
                        src = ctx_rows[bass.ds(b * T_CTX, T_CTX), :]
                        sp.dma_start(rows[:, 0:KT_CTX - 1, :], src[0:T_CTX - TAIL, :].rearrange(
                            "(t p) c -> p t c", p=P)).then_inc(loaded.s, 16)
                        sp.dma_start(rows[0:TAIL, KT_CTX - 1, :], src[T_CTX - TAIL:T_CTX, :]).then_inc(loaded.s, 16)
                    else:
                        sp.dma_start(cT[:, :], ctxT[:, bass.ds(b * T_CTX, T_CTX)]).then_inc(loaded.s, 16)
                    for u, (j, c) in enumerate(units):
                        sp.wait_ge(vec.s, b * NV + (seconds(u, U) + vv))
                        scratch.store(sp, wrote[u % RING], b * HD + j * P, part[:, u % RING, :, 0:widths[c]],
                                      starts[c], widths[c])
                    for t in range(KT_CTX):
                        sp.wait_ge(read.s, b * RD + (NTR + t + 1 + read.base))
                        vals.store(sp, vwrote[t % RING], b, t * P, P if t < KT_CTX - 1 else TAIL,
                                   vt[:, t % RING, :])
                for n in range(RING):
                    sp.wait_ge(wrote[n].s, wrote[n].at(B * U // RING * ND))
                    sp.wait_ge(vwrote[n].s, vwrote[n].at(B * VN[n]))

            @block.tensor
            def _(pe):
                with pe.Fori(0, B) as b:
                    if norm:
                        pe.wait_ge(vec.s, b * NV + (3 + vec.base))
                        pe.wait_ge(read.s, b * RD + read.base)
                        pe.transpose(k.ps[:, 4, 0:P], k.x[:, 0, :], k.ident[:, :])
                        for t in range(KT_CTX):
                            ins = pe.transpose(k.ps[0:CC, 4 + t // 4, (t % 4) * P:(t % 4 + 1) * P],
                                               rows[:, t, :], k.ident[:, :])
                            if t % 4 == 3 or t == KT_CTX - 1:
                                ins.then_inc(mm.s, 1)
                        pe.wait_ge(read.s, b * RD + (NTR + read.base))
                    else:
                        pe.wait_ge(loaded.s, b * NLOAD + (NLOAD + loaded.base))
                    for u, (j, c) in enumerate(units):
                        done = halves(u - 4)
                        pe.wait_ge(vec.s, b * NV + ((min(done, 2 * U) if done else 0) + vv))
                        pe.matmul(k.ps[:, u % 4, 0:widths[c]], wk[:, j * P:(j + 1) * P],
                                  cT[:, starts[c]:starts[c] + widths[c]], start=True, stop=True).then_inc(mm.s, 1)
                    for t in range(KT_CTX):
                        n = P if t < KT_CTX - 1 else TAIL
                        pe.wait_ge(read.s, b * RD + ((NTR + t - 3 if t > 3 else NTR) + read.base))
                        pe.matmul(k.ps[0:n, 4 + t % 4, 0:HD], cT[:, t * P:t * P + n], wv,
                                  start=True, stop=True).then_inc(mm.s, 1)

            @block.scalar
            def _(a):
                with a.Fori(0, B) as b:
                    if norm:
                        a.wait_ge(vec.s, b * NV + (2 + vec.base))
                        a.activation(lg[:, :], mv[:, :, 1], ACT.Ln, bias=k.eps[:, 0:1]).then_inc(act.s, 1)
                        a.wait_ge(act.s, b * NA + (1 + act.base))
                        a.activation(rs[:, :], lg[:, :], ACT.Exp, scale=-0.5).then_inc(act.s, 1)
                    for u in range(U + LAG):
                        if u < U:
                            W = widths[units[u][1]]
                            i, o = k.ps[:, u % 4, 0:W], full[:, u % RING, 0:W]
                            a.wait_ge(mm.s, b * MM + (NTR + u + 1 + mm.base))
                            a.wait_ge(vec.s, b * NV + (halves(u - RING) + vv))
                            if kbias is None:
                                a.activation(o, i, ACT.Copy).then_inc(act.s, 1)
                            else:
                                a.activation(o, i, ACT.Identity, bias=kbias).then_inc(act.s, 1)
                        if u >= LAG:
                            w_, W = u - LAG, widths[units[u - LAG][1]]
                            a.wait_ge(pool.s, b * U + (w_ + 1 + pool.base))
                            a.activation(part[:, w_ % RING, 1, 0:W], rest[:, w_ % RING, 0:W],
                                         ACT.Copy).then_inc(act.s, 1)

            @block.vector
            def _(v):
                def value_tile(b, t):
                    n = P if t < KT_CTX - 1 else TAIL
                    v.wait_ge(mm.s, b * MM + (NTR + U + t + 1 + mm.base))
                    r = t % RING
                    v.wait_ge(vwrote[r].s, b * VN[r] + (16 * (t // RING) + vwrote[r].base))
                    o = vt[0:n, r, :].rearrange("p (h d) -> p h d", d=DP)[:, :, 0:D]
                    i = k.ps[0:n, 4 + t % 4, 0:HD].rearrange("p (h d) -> p h d", d=D)
                    if vbias is None:
                        v.tensor_copy(o, i).then_inc(read.s, 1)
                    else:
                        v.tensor_tensor(o, i, vbias[0:n, :].rearrange("p (h d) -> p h d", d=D),
                                        ALU.add).then_inc(read.s, 1)

                with v.Fori(0, B) as b:
                    if norm:
                        v.wait_ge(loaded.s, b * NLOAD + (NLOAD + loaded.base))
                        for t in range(KT_CTX):
                            ins = v.bn_stats(st[:, t, :], rows[:, t, :])
                        ins.then_inc(vec.s, 1)
                        v.wait_ge(vec.s, b * NV + (1 + vec.base))
                        v.memset(lg[:, :], 0.0)
                        for t in range(KT_CTX):
                            ins = v.bn_aggr(mv[:, t, :], st[:, t, :])
                        ins.then_inc(vec.s, 1)
                        v.wait_ge(act.s, b * NA + (2 + act.base))
                        for t in range(KT_CTX):
                            ins = v.tensor_scalar(rows[:, t, :], rows[:, t, :], mv[:, t, 0:1], rs[:, t:t + 1],
                                                  ALU.subtract, ALU.mult)
                        ins.then_inc(vec.s, 1)
                        for q in range(NTR):
                            n = 512 if q < 3 else P
                            v.wait_ge(mm.s, b * MM + (q + 1 + mm.base))
                            v.tensor_scalar(cT[:, q * 512:q * 512 + n], k.ps[0:CC, 4 + q, 0:n], gain, shift,
                                            ALU.mult, ALU.add).then_inc(read.s, 1)
                    for u in range(U + LAG):
                        if u < U:
                            W = widths[units[u][1]]
                            v.wait_ge(act.s, b * NA + (firsts(u) + va))
                            s_ = wrote[u % RING]
                            v.wait_ge(s_.s, b * (U // RING * ND) + (u // RING * ND + s_.base))
                            v.tensor_copy(part[:, u % RING, 0, 0:W], full[:, u % RING, 0:W]).then_inc(vec.s, 1)
                        if u >= LAG:
                            w_, W = u - LAG, widths[units[u - LAG][1]]
                            v.wait_ge(act.s, b * NA + (seconds(w_, U) + va))
                            v.tensor_tensor(part[:, w_ % RING, 2, 0:W], rest[:, w_ % RING, 0:W],
                                            part[:, w_ % RING, 1, 0:W], ALU.subtract).then_inc(vec.s, 1)
                    for t in range(KT_CTX):
                        value_tile(b, t)

            @block.gpsimd
            def _(g):
                with g.Fori(0, B) as b:
                    for u, (j, c) in enumerate(units):
                        W = widths[c]
                        g.wait_ge(vec.s, b * NV + (firsts(u) + vv))
                        g.tensor_tensor(rest[:, u % RING, 0:W], full[:, u % RING, 0:W], part[:, u % RING, 0, 0:W],
                                        ALU.subtract).then_inc(pool.s, 1)
    mm.passed(B * MM)
    read.passed(B * RD)
    act.passed(B * NA)
    vec.passed(B * NV)
    pool.passed(B * U)
    loaded.passed(B * NLOAD)
    for n in range(RING):
        wrote[n].passed(B * U // RING * ND)
        vwrote[n].passed(B * VN[n])


def stage_logits(nc, k, w, dst, scale):
    mm, vec = k.sems["mm"], k.sems["vec"]
    with nc.Block() as block:
        @block.tensor
        def _(pe):
            for t in range(NT):
                ins = pe.matmul(k.ps[:, 0, t * E:(t + 1) * E], k.xT[:, t * P:(t + 1) * P], w, start=True, stop=True)
            ins.then_inc(mm.s, 1)

        @block.vector
        def _(v):
            v.wait_ge(mm.s, mm.at(1))
            v.tensor_scalar(dst[:, :, :].rearrange("p t e -> p (t e)"), k.ps[:, 0, 0:NT * E], scale, None,
                            ALU.mult).then_inc(vec.s, 1)
    mm.passed(1)
    vec.passed(1)


def stage_sinkhorn(nc, k, la):
    mm, vec, act = k.sems["mm"], k.sems["vec"], k.sems["act"]
    with ExitStack() as ctx:
        def sb(n, shape):
            return ctx.enter_context(nc.sbuf_tensor("sink_" + n, shape, F32))

        mr, sm, lg = sb("mr", [P, NT]), sb("sm", [P, NT]), sb("lg", [P, NT])
        ex = sb("ex", [P, NT, E])
        mc, sc, lc = sb("mc", [P, E]), sb("sc", [P, E]), sb("lc", [P, E])
        m8, dg = sb("m8", [E, 1]), sb("dg", [E, E])
        la_et = la[:, :, :].rearrange("p t e -> p e t")

        def over_experts(a):
            return a.unsqueeze(2).broadcast_to([P, NT, E])

        def over_tiles(a):
            return a.unsqueeze(1).broadcast_to([P, NT, E])

        with nc.Block() as block:
            @block.vector
            def _(v):
                with v.Fori(0, SINK_ITERS) as i:
                    v.tensor_reduce(mr[:, :], la[:, :, :], AX.X, ALU.max).then_inc(vec.s, 1)
                    v.wait_ge(vec.s, i * 10 + (1 + vec.base))
                    v.tensor_tensor(la[:, :, :], la[:, :, :], over_experts(mr[:, :]), ALU.subtract).then_inc(vec.s, 1)
                    v.wait_ge(act.s, i * 4 + (1 + act.base))
                    v.tensor_reduce(sm[:, :], ex[:, :, :], AX.X, ALU.add).then_inc(vec.s, 1)
                    v.wait_ge(act.s, i * 4 + (2 + act.base))
                    v.tensor_tensor(la[:, :, :], la[:, :, :], over_experts(lg[:, :]), ALU.subtract).then_inc(vec.s, 1)
                    v.wait_ge(vec.s, i * 10 + (4 + vec.base))
                    v.tensor_reduce(mc[:, :], la_et, AX.X, ALU.max).then_inc(vec.s, 1)
                    v.wait_ge(mm.s, i * 3 + (1 + mm.base))
                    v.tensor_reduce(m8[:, :], k.ps[0:E, 0, 0:P], AX.X, ALU.max).then_inc(vec.s, 1)
                    v.wait_ge(vec.s, i * 10 + (6 + vec.base))
                    v.tensor_scalar(dg[:, :], k.ident[0:E, 0:E], m8[:, 0:1], None, ALU.mult).then_inc(vec.s, 1)
                    v.wait_ge(mm.s, i * 3 + (2 + mm.base))
                    v.tensor_tensor(la[:, :, :], la[:, :, :], over_tiles(k.ps[:, 1, 0:E]), ALU.subtract).then_inc(vec.s, 1)
                    v.wait_ge(mm.s, i * 3 + (3 + mm.base))
                    v.tensor_reduce(sc[:, :], k.ps[:, 2, 0:NT * E].rearrange("p (t e) -> p e t", e=E),
                                    AX.X, ALU.add).then_inc(vec.s, 1)
                    v.wait_ge(act.s, i * 4 + (4 + act.base))
                    v.tensor_tensor(la[:, :, :], la[:, :, :], over_tiles(lc[:, :]), ALU.subtract).then_inc(vec.s, 1)
                    v.wait_ge(vec.s, i * 10 + (10 + vec.base))

            @block.scalar
            def _(a):
                with a.Fori(0, SINK_ITERS) as i:
                    a.wait_ge(vec.s, i * 10 + (2 + vec.base))
                    a.activation(ex[:, :, :], la[:, :, :], ACT.Exp).then_inc(act.s, 1)
                    a.wait_ge(vec.s, i * 10 + (3 + vec.base))
                    a.activation(lg[:, :], sm[:, :], ACT.Ln).then_inc(act.s, 1)
                    a.wait_ge(vec.s, i * 10 + (8 + vec.base))
                    a.activation(ex[:, :, :], la[:, :, :], ACT.Exp).then_inc(act.s, 1)
                    a.wait_ge(vec.s, i * 10 + (9 + vec.base))
                    a.activation(lc[:, :], sc[:, :], ACT.Ln).then_inc(act.s, 1)
                a.wait_ge(vec.s, vec.at(10 * SINK_ITERS))
                a.activation(la[:, :, :], la[:, :, :], ACT.Exp).then_inc(act.s, 1)

            @block.tensor
            def _(pe):
                with pe.Fori(0, SINK_ITERS) as i:
                    pe.wait_ge(vec.s, i * 10 + (5 + vec.base))
                    pe.transpose(k.ps[0:E, 0, 0:P], mc[:, :], k.ident[:, :]).then_inc(mm.s, 1)
                    pe.wait_ge(vec.s, i * 10 + (7 + vec.base))
                    pe.matmul(k.ps[:, 1, 0:E], k.ones[0:E, :], dg[:, :], start=True, stop=True).then_inc(mm.s, 1)
                    pe.wait_ge(act.s, i * 4 + (3 + act.base))
                    pe.matmul(k.ps[:, 2, 0:NT * E], k.ones[:, :], ex[:, :, :].rearrange("p t e -> p (t e)"),
                              start=True, stop=True).then_inc(mm.s, 1)
    mm.passed(3 * SINK_ITERS)
    vec.passed(10 * SINK_ITERS)
    act.passed(4 * SINK_ITERS + 1)


def stage_top(nc, k, name, score, weight, top, gains=None):
    vec = k.sems["vec"]
    with ExitStack() as ctx:
        def sb(n, shape):
            return ctx.enter_context(nc.sbuf_tensor(name + "_" + n, shape, F32))

        best, first = sb("best", [P, NT]), sb("first", [P, NT])
        cand, hot = sb("cand", [P, NT, E]), sb("hot", [P, NT, E])
        iota = sub(k.row, ROW, "iota").unsqueeze(1).broadcast_to([P, NT, E])
        with nc.Block() as block:
            @block.vector
            def _(v):
                n = [0]

                def link(ins):
                    n[0] += 1
                    ins.then_inc(vec.s, 1)
                    v.wait_ge(vec.s, vec.at(n[0]))

                def over(a):
                    return a[:, :].unsqueeze(2).broadcast_to([P, NT, E])

                for r in range(top):
                    link(v.tensor_reduce(best[:, :], score[:, :, :], AX.X, ALU.max))
                    link(v.tensor_tensor(cand[:, :, :], score[:, :, :], over(best), ALU.is_ge))
                    link(v.scalar_tensor_tensor(out=cand[:, :, :], in0=cand[:, :, :], scalar=-float(E),
                                                in1=iota, op0=ALU.mult, op1=ALU.add))
                    link(v.tensor_reduce(first[:, :], cand[:, :, :], AX.X, ALU.min))
                    link(v.tensor_tensor(hot[:, :, :], cand[:, :, :], over(first), ALU.is_equal))
                    if gains is None:
                        link(v.tensor_copy(weight[:, :, :], hot[:, :, :]))
                    elif r == 0:
                        link(v.tensor_tensor(weight[:, :, :], hot[:, :, :], gains[r], ALU.mult))
                    else:
                        link(v.tensor_tensor(cand[:, :, :], hot[:, :, :], gains[r], ALU.mult))
                        link(v.tensor_tensor(weight[:, :, :], weight[:, :, :], cand[:, :, :], ALU.add))
                    if r < top - 1:
                        link(v.scalar_tensor_tensor(out=score[:, :, :], in0=hot[:, :, :], scalar=-4.0,
                                                    in1=score[:, :, :], op0=ALU.mult, op1=ALU.add))
        vec.passed(top * 6 + 2 * (top - 1))


def stage_experts(nc, k, name, srcT, w_in, w_down, weight, gated):
    mm, mm2, read, act, vec = (k.sems[n] for n in ("mm", "mm2", "read", "act", "vec"))
    weights = (k.sems["weights0"], k.sems["weights1"])
    nw = 2 if gated else 1
    U = 2 * FB
    with ExitStack() as ctx:
        def sb(n, shape, dtype=F32):
            return ctx.enter_context(nc.sbuf_tensor(name + "_" + n, shape, dtype))

        wi = sb("wi", [P, 2, nw * F])
        wd = sb("wd", [P, 2, FB * C])
        hid = sb("hid", [P, FB, NT * P])
        gate = sb("gate", [P, 2, 512]) if gated else None
        aff = None if gated else sb("aff", [P, 2, NT * P])
        b1 = None if gated else sb("b1", [P, 2, FB])
        with nc.Block() as block:
            @block.sync
            def _(sp):
                def load(e, par):
                    sp.wait_ge(mm2.s, e * 2 + (mm2.base - 2))
                    sp.dma_start(wi[:, par, :], w_in[bass.ds(e, 1), :, :].rearrange("e c f -> (e c) f")).then_inc(
                        weights[par].s, 16)
                    sp.dma_start(wd[:, par, :], w_down[bass.ds(e, 1), :, :].rearrange("e c f -> (e c) f")).then_inc(
                        weights[par].s, 16)

                rounds(sp, E, 2, load)

            @block.tensor
            def _(pe):
                def expert(e, par):
                    pe.wait_ge(weights[par].s, (e - par) * 16 + (32 + weights[par].base))
                    if not gated:
                        pe.wait_ge(vec.s, (e + 1) + vec.base)
                    for c in range(2):
                        for f in range(FB):
                            u = c * FB + f
                            done = act if not gated else vec
                            pe.wait_ge(done.s, e * U + (u - 1 + done.base))
                            rhs = (srcT if gated else aff[:, par, :])[:, c * 512:(c + 1) * 512]
                            for n in range(nw):
                                ins = pe.matmul(k.ps[:, 2 * n + u % 2, :],
                                                wi[:, par, n * F + f * P:n * F + (f + 1) * P], rhs,
                                                start=True, stop=True)
                            ins.then_inc(mm.s, 1)
                    for c in range(2):
                        done = act if not gated else vec
                        pe.wait_ge(done.s, e * U + (FB * (c + 1) + done.base))
                        pe.wait_ge(read.s, e * 2 + (c - 1 + read.base))
                        for t in range(4):
                            for f in range(FB):
                                ins = pe.matmul(k.ps[:, 4 + c, t * P:(t + 1) * P],
                                                hid[:, f, (c * 4 + t) * P:(c * 4 + t + 1) * P],
                                                wd[:, par, f * C:(f + 1) * C], start=(f == 0), stop=(f == FB - 1))
                        ins.then_inc(mm2.s, 1)

                rounds(pe, E, 2, expert)

            @block.scalar
            def _(a):
                def expert(e, par):
                    for c in range(2):
                        for f in range(FB):
                            u = c * FB + f
                            a.wait_ge(mm.s, e * U + (u + 1 + mm.base))
                            if gated:
                                a.wait_ge(vec.s, e * U + (u - 1 + vec.base))
                                a.activation(gate[:, u % 2, :], k.ps[:, u % 2, :], ACT.Silu).then_inc(act.s, 1)
                            else:
                                a.wait_ge(mm2.s, e * 2 + (c - 1 + mm2.base))
                                a.activation(hid[:, f, c * 512:(c + 1) * 512], k.ps[:, u % 2, :], ACT.Relu,
                                             bias=b1[:, par, f:f + 1]).then_inc(act.s, 1)

                rounds(a, E, 2, expert)

            @block.vector
            def _(v):
                def affine(e, par):
                    v.wait_ge(act.s, e * U + (act.base - U))
                    v.tensor_copy(b1[:, par, :], k.col[:, bass.ds(e * FB + COL["b1"][0], FB)])
                    v.tensor_scalar(aff[:, par, :], srcT[:, :], k.col[:, bass.ds(e + COL["ln_g"][0], 1)],
                                    k.col[:, bass.ds(e + COL["ln_b"][0], 1)], ALU.mult, ALU.add).then_inc(vec.s, 1)

                def expert(e, par):
                    if gated:
                        for c in range(2):
                            for f in range(FB):
                                u = c * FB + f
                                v.wait_ge(act.s, e * U + (u + 1 + act.base))
                                v.wait_ge(mm2.s, e * 2 + (c - 1 + mm2.base))
                                v.tensor_tensor(hid[:, f, c * 512:(c + 1) * 512], gate[:, u % 2, :],
                                                k.ps[:, 2 + u % 2, :], ALU.mult).then_inc(vec.s, 1)
                    else:
                        affine(e, par)
                    for c in range(2):
                        v.wait_ge(mm2.s, e * 2 + (c + 1 + mm2.base))
                        for t in range(4):
                            tile = c * 4 + t
                            ins = v.scalar_tensor_tensor(out=k.x[:, tile, :], in0=k.ps[:, 4 + c, t * P:(t + 1) * P],
                                                         scalar=weight[:, tile, bass.ds(e, 1)],
                                                         in1=k.x[:, tile, :], op0=ALU.mult, op1=ALU.add)
                        ins.then_inc(read.s, 1)
                        v.wait_ge(read.s, e * 2 + (c + 1 + read.base))

                rounds(v, E, 2, expert)

    mm.passed(E * U)
    mm2.passed(2 * E)
    read.passed(2 * E)
    act.passed(E * U)
    vec.passed(E * U if gated else E)
    for w in weights:
        w.passed(16 * E)


def stage_expert_bias(nc, k, weight, b2):
    mm, read = k.sems["mm"], k.sems["read"]
    with ExitStack() as ctx:
        wT = ctx.enter_context(nc.sbuf_tensor("bias_wT", [E, NT * P], F32))
        with nc.Block() as block:
            @block.tensor
            def _(pe):
                for t in range(NT):
                    ins = pe.transpose(k.ps[0:E, t // 4, (t % 4) * P:(t % 4 + 1) * P], weight[:, t, :], k.ident[:, :])
                ins.then_inc(mm.s, 1)
                pe.wait_ge(read.s, read.at(1))
                for t in range(NT):
                    ins = pe.matmul(k.ps[:, 2 + t // 4, (t % 4) * P:(t % 4 + 1) * P], wT[:, t * P:(t + 1) * P], b2,
                                    start=True, stop=True)
                ins.then_inc(mm.s, 1)

            @block.vector
            def _(v):
                v.wait_ge(mm.s, mm.at(1))
                v.tensor_copy(wT[:, :], k.ps[0:E, 0:2, :].rearrange("p a b -> p (a b)")).then_inc(read.s, 1)
                v.wait_ge(mm.s, mm.at(2))
                v.tensor_tensor(k.x[:, :, :].rearrange("p t c -> p (t c)"),
                                k.ps[:, 2:4, :].rearrange("p a b -> p (a b)"),
                                k.x[:, :, :].rearrange("p t c -> p (t c)"), ALU.add).then_inc(read.s, 1)
    mm.passed(2)
    read.passed(2)


def stage_mlp(nc, k, name, srcT, w2, b2, w3, bias):
    mm, mm2, act, vec = (k.sems[n] for n in ("mm", "mm2", "act", "vec"))
    with ExitStack() as ctx:
        hid = ctx.enter_context(nc.sbuf_tensor(name + "_hid", [P, FB, NT * P], F32))
        with nc.Block() as block:
            @block.gpsimd
            def _(g):
                g.tensor_tensor(k.x[:, :, :], k.x[:, :, :], bias.unsqueeze(1).broadcast_to([P, NT, C]), ALU.add)

            @block.tensor
            def _(pe):
                for u in range(2 * FB):
                    c, f = u // FB, u % FB
                    pe.wait_ge(act.s, act.at(u - 3))
                    pe.matmul(k.ps[:, u % 4, :], w2[:, f * P:(f + 1) * P], srcT[:, c * 512:(c + 1) * 512],
                              start=True, stop=True).then_inc(mm.s, 1)

            @block.scalar
            def _(a):
                for u in range(2 * FB):
                    c, f = u // FB, u % FB
                    a.wait_ge(mm.s, mm.at(u + 1))
                    a.activation(hid[:, f, c * 512:(c + 1) * 512], k.ps[:, u % 4, :], ACT.Gelu,
                                 bias=b2[:, f:f + 1]).then_inc(act.s, 1)
        mm.passed(2 * FB)
        act.passed(2 * FB)
        with nc.Block() as block:
            @block.tensor
            def _(pe):
                for t in range(NT):
                    for f in range(FB):
                        ins = pe.matmul(k.ps[:, t // 4, (t % 4) * P:(t % 4 + 1) * P], hid[:, f, t * P:(t + 1) * P],
                                        w3[:, f * C:(f + 1) * C], start=(f == 0), stop=(f == FB - 1))
                    if t % 4 == 3:
                        ins.then_inc(mm2.s, 1)

            @block.vector
            def _(v):
                for half in range(2):
                    v.wait_ge(mm2.s, mm2.at(half + 1))
                    xs = k.x[:, half * 4:half * 4 + 4, :].rearrange("p t c -> p (t c)")
                    v.tensor_tensor(xs, k.ps[:, half, :], xs, ALU.add).then_inc(vec.s, 1)
    mm2.passed(2)
    vec.passed(2)


def stage_add(nc, k, dst, a, b=None):
    with nc.Block() as block:
        @block.gpsimd
        def _(g):
            if b is None:
                g.tensor_copy(dst[:, :, :], a[:, :, :])
            else:
                g.tensor_tensor(dst[:, :, :], a[:, :, :], b[:, :, :], ALU.add)


def stage_sigmoid_of_best(nc, k, logits, best, weight):
    vec, act = k.sems["vec"], k.sems["act"]
    with nc.Block() as block:
        @block.vector
        def _(v):
            v.tensor_reduce(best[:, :], logits[:, :, :], AX.X, ALU.max).then_inc(vec.s, 1)
            v.wait_ge(act.s, act.at(1))
            v.tensor_scalar(best[:, :], best[:, :], 1.0, None, ALU.add).then_inc(vec.s, 1)
            v.wait_ge(vec.s, vec.at(2))
            v.reciprocal(best[:, :], best[:, :]).then_inc(vec.s, 1)
            v.wait_ge(vec.s, vec.at(3))
            v.tensor_tensor(weight[:, :, :], weight[:, :, :],
                            best[:, :].unsqueeze(2).broadcast_to([P, NT, E]), ALU.mult)

        @block.scalar
        def _(a):
            a.wait_ge(vec.s, vec.at(1))
            a.activation(best[:, :], best[:, :], ACT.Exp, scale=-1.0).then_inc(act.s, 1)
    vec.passed(3)
    act.passed(1)




def decoder(nc, d, out):
    k = K()
    with ExitStack() as whole:
        def sb_in(ctx, name, shape, dtype=F32):
            return ctx.enter_context(nc.sbuf_tensor(name, shape, dtype))

        stage_setup(nc, k, whole, d)

        def col(name, j=0, rows=P):
            a, w = COL[name]
            return k.col[0:rows, a + j:a + j + 1]

        def row(name):
            return sub(k.row, ROW, name)

        with ExitStack() as ctx:
            w0 = sb_in(ctx, "w0", [P, W0_N])
            wc0 = sb_in(ctx, "wc0", [CC, WC0_N])
            stage_load(nc, k, [(w0[:, :], d["w0"]), (wc0[:, :], d["wc0"])])
            stage_transpose(nc, k, k.x, [(k.xT, None, None)])
            with ExitStack() as c2:
                o0 = sb_in(c2, "o0", [P, BH // 4 * N])
                q0, k0 = Scratch(nc, "q0", 16, N, "q"), Scratch(nc, "k0", 16, N, "k")
                v0 = Values(nc, "v0", 16, N)
                heads = [(k.xT, w0[:, W0[n][0] + j * P:W0[n][0] + (j + 1) * P], None, scr, j * P)
                         for n, scr in (("wq", q0), ("wk", k0)) for j in range(2)]
                stage_project(nc, k, "p0", heads, (k.xT, sub(w0, W0, "wv"), None, v0))
                stage_attention(nc, k, "a0", N, 8 ** -0.5, "causal", q0, k0, v0, o0)
                stage_output(nc, k, [o0], sub(w0, W0, "wo"), None)
            stage_norm(nc, k, k.x, k.x)
            stage_transpose(nc, k, k.x, [(k.xT, None, None)])
            with ExitStack() as c2:
                o1 = sb_in(c2, "o1", [P, BH // 4 * N])
                oc = sb_in(c2, "oc", [P, BH // 4 * N])
                q1, k1 = Scratch(nc, "q1", 8, N, "q"), Scratch(nc, "k1", 8, N, "k")
                qc, kc = Scratch(nc, "qc", 8, N, "q"), Scratch(nc, "kc", 8, T_CTX, "k")
                v1, vc = Values(nc, "v1", 8, N), Values(nc, "vc", 8, T_CTX)
                heads = [(k.xT, sub(w0, W0, "xq"), col("xq"), q1, 0),
                         (k.xT, sub(w0, W0, "xk"), col("xk"), k1, 0),
                         (k.xT, sub(w0, W0, "xcq"), col("xcq"), qc, 0)]
                stage_project(nc, k, "p1", heads, (k.xT, sub(w0, W0, "xv"), row("xv"), v1))
                stage_context(nc, k, "c0", sub(wc0, WC0, "ck", CC), sub(wc0, WC0, "cv", CC), col("xck"),
                              row("xcv"), kc, vc, ctxT=d["ctxT"])
                stage_attention(nc, k, "a1", N, 8 ** -0.5, "causal", q1, k1, v1, o1)
                stage_attention(nc, k, "ac", T_CTX, 8 ** -0.5, None, qc, kc, vc, oc)
                stage_output(nc, k, [o1, oc], sub(w0, W0, "xp"), row("xp"))
            stage_norm(nc, k, k.x, k.x)
            stage_transpose(nc, k, k.x, [(k.xT, None, None)])
            with ExitStack() as c2:
                plan = sb_in(c2, "plan", [P, NT, E])
                kept = sb_in(c2, "kept", [P, NT, E])
                weight = sb_in(c2, "weight0", [P, NT, E])
                stage_logits(nc, k, sub(w0, W0, "gate"), plan, -1.0 / SINK_EPS)
                stage_sinkhorn(nc, k, plan)
                stage_add(nc, k, kept, plan)
                stage_top(nc, k, "top0", plan, weight, 2,
                          [kept[:, :, r:r + 1].broadcast_to([P, NT, E]) for r in range(2)])
                stage_experts(nc, k, "e0", k.xT, d["e0_in"], d["e0_down"], weight, True)
            stage_norm(nc, k, k.x, k.x)
        stage_transpose(nc, k, k.x, [(k.xT, None, None)])
        with ExitStack() as ctx:
            w1 = sb_in(ctx, "w1", [P, W1_N])
            wf = sb_in(ctx, "wf", [32, WF_N])
            o2 = sb_in(ctx, "o2", [P, BH // 2 * N])
            q2, k2 = Scratch(nc, "q2", 64, N, "q", True), Scratch(nc, "k2", 64, N, "k", True)
            v2 = Values(nc, "v2", 64, N)
            stage_load(nc, k, [(w1[:, :], d["w1"]), (wf[:, :], d["wf"])])
            stage_project_rotary(nc, k, w1, wf, q2, k2, v2)
            stage_attention(nc, k, "a2", N, 64 ** -0.5, None, q2, k2, v2, o2)
            stage_output(nc, k, [o2], sub(w1, W1, "o"), row("out"))
        stage_norm(nc, k, k.x, k.x)
        with ExitStack() as ctx:
            wx = sb_in(ctx, "wx", [P, WX_N])
            wc1 = sb_in(ctx, "wc1", [CC, WC1_N])
            xx = sb_in(ctx, "xx", [P, NT, C])
            keep = sb_in(ctx, "keep", [P, NT, C])
            z = sb_in(ctx, "z", [P, NT, C])
            yT = sb_in(ctx, "yT", [P, NT * P])
            cent = sb_in(ctx, "cent", [P, E])
            stage_load(nc, k, [(cent[:, :], d["cent"]), (wc1[:, :], d["wc1"])])
            stage_add(nc, k, xx, k.x)
            for unit in ("a1", "a2"):
                ln = "ln1" if unit == "a1" else "ln2"
                stage_load(nc, k, [(wx[:, :], d["w" + unit])])
                stage_norm(nc, k, k.x, k.x, row(ln + "_g"), row(ln + "_b"))
                stage_add(nc, k, keep, k.x)
                stage_norm(nc, k, k.x, z)
                with ExitStack() as c2:
                    T = N if unit == "a1" else T_CTX
                    qs, ks = Scratch(nc, unit + "q", 32, N, "q"), Scratch(nc, unit + "k", 32, T, "k")
                    vv = Values(nc, unit + "v", 32, T)
                    oo = sb_in(c2, unit + "o", [P, BH // 4 * N])
                    outs = [(k.xT, col(unit + "lnx_g"), col(unit + "lnx_b"))]
                    if unit == "a1":
                        outs.append((yT, col(unit + "lny_g"), col(unit + "lny_b")))
                    stage_transpose(nc, k, z, outs)
                    qa, ka = WX["q"][0], WX["k"][0]
                    heads = [(k.xT, wx[:, qa + j * P:qa + (j + 1) * P], None, qs, j * P) for j in range(4)]
                    if unit == "a1":
                        heads += [(yT, wx[:, ka + j * P:ka + (j + 1) * P], None, ks, j * P) for j in range(4)]
                    stage_project(nc, k, "p" + unit, heads,
                                  (yT, sub(wx, WX, "v"), None, vv) if unit == "a1" else None)
                    if unit == "a2":
                        stage_context(nc, k, "c1", sub(wc1, WC1, "k", CC), sub(wc1, WC1, "v", CC), None,
                                      None, ks, vv, ctx_rows=d["ctx"], gain=col("a2lny_g", rows=CC),
                                      shift=col("a2lny_b", rows=CC))
                    stage_attention(nc, k, "t" + unit, T, 32 ** -0.5, "after" if unit == "a1" else None,
                                    qs, ks, vv, oo)
                    stage_output(nc, k, [oo], sub(wx, WX, "li1"), row(unit + "li1"))
                stage_norm(nc, k, k.x, z)
                stage_transpose(nc, k, z, [(k.xT, col(unit + "ln3_g"), col(unit + "ln3_b"))])
                stage_mlp(nc, k, "m" + unit, k.xT, sub(wx, WX, "li2"),
                          k.col[:, COL[unit + "li2_b"][0]:COL[unit + "li2_b"][0] + FB],
                          sub(wx, WX, "li3"), row(unit + "li3"))
                stage_add(nc, k, k.x, k.x, keep)
            stage_add(nc, k, k.x, k.x, xx)
            stage_norm(nc, k, k.x, k.x)
            aff = sb_in(ctx, "affinity", [P, NT, E])
            best = sb_in(ctx, "affinity_best", [P, NT])
            weight = sb_in(ctx, "weight1", [P, NT, E])
            b2 = sb_in(ctx, "b2", [E, C])
            stage_load(nc, k, [(b2[:, :], d["b2"])])
            stage_transpose(nc, k, k.x, [(k.xT, None, None)])
            stage_logits(nc, k, cent[:, :], aff, 1.0)
            stage_top(nc, k, "top1", aff, weight, 1)
            stage_sigmoid_of_best(nc, k, aff, best, weight)
            stage_norm(nc, k, k.x, z)
            stage_transpose(nc, k, z, [(yT, None, None)])
            stage_add(nc, k, k.x, k.x, k.x)
            stage_expert_bias(nc, k, weight, b2[:, :])
            stage_experts(nc, k, "e1", yT, d["e1_in"], d["e1_down"], weight, False)
            stage_norm(nc, k, k.x, k.x)
        with nc.Block() as block:
            @block.sync
            def _(sp):
                o = k.sems["out"]
                sp.dma_start(out.rearrange("(t p) c -> p t c", p=P), k.x[:, :, :]).then_inc(o.s, 16)
                sp.wait_ge(o.s, o.at(16))


def layout(i):
    def pack(table, total, parts, rows=P):
        a = np.zeros((rows, total), np.float32)
        for name, v in parts.items():
            at, w = table[name]
            a[0:v.shape[0], at:at + w] = v
        return a

    def blocks(w):
        return w.reshape(-1, P, w.shape[1]).transpose(1, 0, 2).reshape(P, -1)

    def padded(w, D):
        a = np.zeros((H, 32, w.shape[1]), np.float32)
        a[:, 0:D] = w.reshape(H, D, -1)
        return blocks(a.reshape(H * 32, -1))

    d = {"x": i["x"].reshape(B * N, C), "ctx": i["ctx_512"].reshape(-1, CC)}
    d["ctxT"] = np.ascontiguousarray(d["ctx"].T)
    d["w0"] = pack(W0, W0_N, {
        "wq": i["L0_attn_Wq"], "wk": i["L0_attn_Wk"], "wv": i["L0_attn_Wv"], "wo": padded(i["L0_attn_Wo"], 16),
        "xk": i["L0_xattn_Wk"], "xq": i["L0_xattn_Wq"], "xv": i["L0_xattn_Wv"], "xcq": i["L0_xattn_Wcq"],
        "xp": padded(i["L0_xattn_Wp"], 8), "gate": i["L0_ffn_gate_W"].T})
    d["wc0"] = pack(WC0, WC0_N, {"ck": i["L0_xattn_Wck"], "cv": i["L0_xattn_Wcv"]}, CC)
    hd = 64
    freqs = np.float32(10000.0) ** (-np.arange(0, hd, 2, dtype=np.float32) / np.float32(hd))
    angles = np.arange(N, dtype=np.float32)[:, None] * freqs
    sin = np.repeat(np.sin(angles), 2, axis=1).T
    cos = np.repeat(np.cos(angles), 2, axis=1).T
    sign = np.where(np.arange(hd) < hd // 2, -1.0, 1.0).astype(np.float32)[:, None]
    turn = np.concatenate([np.arange(1, hd, 2), np.arange(0, hd, 2)])
    ff = np.arange(N, dtype=np.float32)[:, None] * np.arange(1, 17, dtype=np.float32)
    fourier = np.concatenate([np.sin(ff), np.cos(ff)], axis=-1).T
    wq, wk, wv = i["L1_attn_w_qkv"].reshape(3, H, hd, C)
    d["w1"] = pack(W1, W1_N, {
        "q": wq.reshape(-1, C).T, "qr": wq[:, turn].reshape(-1, C).T, "k": wk.reshape(-1, C).T,
        "kr": wk[:, turn].reshape(-1, C).T, "v": wv.reshape(-1, C).T, "o": blocks(i["L1_attn_w_out"].T),
        "cos": np.tile(cos, (2, 1)), "sin": np.tile(sin * sign, (2, 1))})
    d["wf"] = pack(WF, WF_N, {"fp": np.tile(i["L1_attn_w_fproj"].T, (1, 2)), "fourier": fourier}, 32)
    col = {}
    for a in ("a1", "a2"):
        g = {n: i["L1_xattn_" + a + "_" + n] for n in (
            "wq", "wk", "wv", "li1_w", "li2_w", "li3_w", "lnx_g", "lnx_b", "lny_g", "lny_b", "ln3_g", "ln3_b",
            "li2_b")}
        wx = {}
        for n in "qkv":
            w = g["w" + n].transpose(1, 0, 2).reshape(g["w" + n].shape[1], -1)
            if a == "a1" or n == "q":
                wx[n] = w
            else:
                g["ctx" + n] = w
        wx["li1"], wx["li2"], wx["li3"] = blocks(g["li1_w"]), g["li2_w"], blocks(g["li3_w"])
        d["w" + a] = pack(WX, WX_N, wx)
        for n in ("lnx_g", "lnx_b", "lny_g", "lny_b", "ln3_g", "ln3_b"):
            col[a + n] = g[n][:, None]
        col[a + "li2_b"] = g["li2_b"].reshape(FB, P).T
    d["cent"] = i["L1_ffn_centroids"].T
    d["wc1"] = pack(WC1, WC1_N, {"k": g["ctxk"], "v": g["ctxv"]}, CC)
    for n in ("xk", "xq", "xcq", "xck"):
        col[n] = i["L0_xattn_b" + n[1:]][:, None]
    col["fp"] = np.tile(i["L1_attn_b_fproj"], 2)[:, None]
    col["ln_g"], col["ln_b"] = i["L1_ffn_ln_g"].T, i["L1_ffn_ln_b"].T
    col["b1"] = i["L1_ffn_b1"].reshape(E * FB, P).T
    d["col"] = pack(COL, COL_N, col)
    row = {"xv": "L0_xattn_bv", "xcv": "L0_xattn_bcv", "xp": "L0_xattn_bp", "out": "L1_attn_b_out",
           "a1li1": "L1_xattn_a1_li1_b", "a1li3": "L1_xattn_a1_li3_b", "a2li1": "L1_xattn_a2_li1_b",
           "a2li3": "L1_xattn_a2_li3_b", "ln1_g": "L1_xattn_ln1_g", "ln1_b": "L1_xattn_ln1_b",
           "ln2_g": "L1_xattn_ln2_g", "ln2_b": "L1_xattn_ln2_b"}
    rows = {n: i[v][None, :] for n, v in row.items()}
    rows["iota"] = np.arange(E, dtype=np.float32)[None, :]
    d["row"] = pack(ROW, ROW_N, rows, 1)
    d["e0_in"] = np.concatenate([i["L0_ffn_W_gate"].transpose(0, 2, 1), i["L0_ffn_W_up"].transpose(0, 2, 1)], axis=2)

    def down(w):
        return w.transpose(0, 2, 1).reshape(E, FB, P, C).transpose(0, 2, 1, 3).reshape(E, P, FB * C)

    d["e0_down"] = down(i["L0_ffn_W_down"])
    d["e1_in"] = i["L1_ffn_w1"].transpose(0, 2, 1)
    d["e1_down"] = down(i["L1_ffn_w2"])
    d["b2"] = i["L1_ffn_b2"]
    return {n: np.ascontiguousarray(v) for n, v in d.items()}


def kernel(**inputs):
    import concourse.bacc as _bacc
    from concourse.bass_utils import run_bass_kernel_spmd as _run

    arrays = layout({n: np.asarray(v) for n, v in inputs.items()})
    nc = _bacc.Bacc("TRN2", target_bir_lowering=False, num_devices=1)
    d = {n: nc.dram_tensor("in_" + n, a.shape, F32, kind="ExternalInput").ap() for n, a in arrays.items()}
    out = nc.dram_tensor("out_0", (B * N, C), F32, kind="ExternalOutput").ap()
    decoder(nc, d, out)
    r = _run(nc, [{"in_" + n: a for n, a in arrays.items()}], core_ids=[0])
    return r.results[0]["out_0"].reshape(B, N, C)
```

```python
from contextlib import ExitStack

import numpy as np

import concourse.bass as bass
from concourse import mybir

F32 = mybir.dt.float32
BF16 = mybir.dt.bfloat16
ALU = mybir.AluOpType
ACT = mybir.ActivationFunctionType
AX = mybir.AxisListType

P = 128
B = 4
N = 256
C = 128
CC = 64
T_CTX = 1601
KT_CTX = -(-T_CTX // P)
TAIL = T_CTX - (KT_CTX - 1) * P
NT = B * N // P
H = 16
BH = B * H
E = 8
F = 512
FB = F // P
EPS = 1e-5
CREDIT = 16
NEG = -1e30
EXP_LN = "natural_log_exp_and_others"
SINK_ITERS = 20
SINK_EPS = 0.05

Q_PART = {1: (0, 0, 0, 1, 1, 2), 2: (0, 0, 1, 1, 0, 2)}
K_PART = {1: (0, 1, 2, 0, 1, 0), 2: (0, 1, 0, 1, 2, 0)}


class Sem:

    def __init__(self, ctx, nc, name):
        self.s = ctx.enter_context(nc.semaphore(name))
        self.base = CREDIT

    def at(self, n):
        return n + self.base

    def passed(self, n):
        self.base += n


class K:

    def __init__(self):
        self.sems = {}


def columns(widths):
    at, n = {}, 0
    for name, w in widths:
        at[name] = (n, w)
        n += w
    return at, n


W0, W0_N = columns([("wq", 256), ("wk", 256), ("wv", 256), ("wo", 4 * C), ("xk", 128), ("xq", 128),
                    ("xv", 128), ("xcq", 128), ("xp", 4 * C), ("gate", E)])
WC0, WC0_N = columns([("ck", 128), ("cv", 128)])
W1, W1_N = columns([("q", 1024), ("qr", 1024), ("k", 1024), ("kr", 1024), ("v", 1024), ("o", 1024),
                    ("cos", N), ("sin", N)])
WF, WF_N = columns([("fp", 128), ("fourier", N)])
WX, WX_N = columns([(n, 512) for n in ("q", "k", "v", "li1", "li2", "li3")])
WC1, WC1_N = columns([("k", 512), ("v", 512)])
COL, COL_N = columns([("xk", 1), ("xq", 1), ("xcq", 1), ("xck", 1), ("fp", 1)]
                     + [(a + n, w) for a in ("a1", "a2") for n, w in
                        (("lnx_g", 1), ("lnx_b", 1), ("lny_g", 1), ("lny_b", 1), ("ln3_g", 1), ("ln3_b", 1),
                         ("li2_b", FB))]
                     + [("ln_g", E), ("ln_b", E), ("b1", E * FB)])
ROW, ROW_N = columns([("xv", 128), ("xcv", 128), ("xp", 128), ("out", 128), ("a1li1", 128), ("a1li3", 128),
                      ("a2li1", 128), ("a2li3", 128), ("ln1_g", 128), ("ln1_b", 128), ("ln2_g", 128),
                      ("ln2_b", 128), ("iota", E)])


def sub(tensor, table, name, rows=P):
    a, w = table[name]
    return tensor[0:rows, a:a + w]


def rounds(eng, end, n, body):
    assert end % n == 0 and end > n
    with eng.Fori(0, end // n) as i:
        for r in range(n):
            body(i * n + r, r)


def stage_setup(nc, k, ctx, d):
    def sb(name, shape, dt=F32):
        return ctx.enter_context(nc.sbuf_tensor(name, shape, dt))

    k.ps = ctx.enter_context(nc.psum_tensor("ps", [P, 8, 512], F32))
    k.x = sb("x", [P, NT, C])
    k.xT = sb("xT", [P, NT * P])
    k.ident = sb("ident", [P, P])
    k.identb = sb("identb", [P, P], BF16)
    k.mask_qk = sb("mask_qk", [P, P], BF16)
    k.mask_kq = sb("mask_kq", [P, P], BF16)
    k.keep_kq = sb("keep_kq", [P, P])
    k.ones = sb("ones", [P, P])
    k.spread = sb("spread", [P, P])
    k.col = sb("col", [P, COL_N])
    k.row = sb("row", [P, ROW_N])
    k.eps = sb("eps", [P, 1])
    k.ln_st = sb("ln_st", [P, NT, 6])
    k.ln_mv = sb("ln_mv", [P, NT, 2])
    k.ln_lg = sb("ln_lg", [P, NT])
    k.ln_rs = sb("ln_rs", [P, NT])
    for name in ("loaded", "filled", "mm", "read", "mm2", "act", "pool", "vec",
                 "scores", "scores_read", "negmax", "shift_t", "shift_in", "st_ready", "exp_done",
                 "probs_used", "out_read", "masked", "ops0", "ops1", "ops2", "ops3", "weights0", "weights1",
                 "wrote0", "wrote1", "wrote2", "wrote3", "vwrote0", "vwrote1", "vwrote2", "vwrote3",
                 "values0", "values1", "divided", "inverted", "out"):
        k.sems[name] = Sem(ctx, nc, name)
    sems = k.sems
    with nc.Block() as block:
        @block.sync
        def _(sp):
            for s in sems.values():
                sp.sem_inc(s.s, CREDIT)
            sp.dma_start(k.col[:, :], d["col"]).then_inc(sems["loaded"].s, 16)
            sp.dma_start(k.row[:, :], d["row"].broadcast_to([P, ROW_N])).then_inc(sems["loaded"].s, 16)
            sp.dma_start(k.x[:, :, :], d["x"].rearrange("(t p) c -> p t c", p=P)).then_inc(sems["loaded"].s, 16)
    with nc.Block() as block:
        @block.sync
        def _(sp):
            sp.wait_ge(sems["loaded"].s, sems["loaded"].at(48))

        @block.gpsimd
        def _(g):
            f = sems["filled"]
            g.memset(k.ident[:, :], 0.0).then_inc(f.s, 1)
            g.memset(k.mask_qk[:, :], 0.0).then_inc(f.s, 1)
            g.memset(k.mask_kq[:, :], 0.0).then_inc(f.s, 1)
            g.memset(k.keep_kq[:, :], 0.0).then_inc(f.s, 1)
            g.memset(k.ones[:, :], 1.0).then_inc(f.s, 1)
            g.memset(k.eps[:, :], EPS).then_inc(f.s, 1)
            g.memset(k.spread[:, :], 0.0).then_inc(f.s, 1)
            g.wait_ge(f.s, f.at(7))
            g.affine_select(out=k.ident[:, :], in_=k.ident[:, :], compare_op=ALU.not_equal, fill=1.0,
                            base=0, pattern=[[-1, P]], channel_multiplier=1).then_inc(f.s, 1)
            g.affine_select(out=k.mask_qk[:, :], in_=k.mask_qk[:, :], compare_op=ALU.is_ge, fill=NEG,
                            base=0, pattern=[[-1, P]], channel_multiplier=1).then_inc(f.s, 1)
            g.affine_select(out=k.mask_kq[:, :], in_=k.mask_kq[:, :], compare_op=ALU.is_ge, fill=NEG,
                            base=0, pattern=[[1, P]], channel_multiplier=-1).then_inc(f.s, 1)
            g.affine_select(out=k.keep_kq[:, :], in_=k.keep_kq[:, :], compare_op=ALU.is_ge, fill=1.0,
                            base=0, pattern=[[1, P]], channel_multiplier=-1).then_inc(f.s, 1)
            for h in range(0, P, 32):
                g.affine_select(out=k.spread[:, h:h + 32], in_=k.spread[:, h:h + 32], compare_op=ALU.not_equal,
                                fill=1.0, base=-(h + 31), pattern=[[0, 32]], channel_multiplier=1).then_inc(f.s, 1)
            g.wait_ge(f.s, f.at(15))
            g.tensor_copy(k.identb[:, :], k.ident[:, :]).then_inc(f.s, 1)
            g.wait_ge(f.s, f.at(16))
    sems["loaded"].passed(48)
    sems["filled"].passed(16)


def stage_norm(nc, k, src, dst, gain=None, shift=None):
    vec, act = k.sems["vec"], k.sems["act"]
    nv = [0]
    with nc.Block() as block:
        @block.vector
        def _(v):
            for t in range(NT):
                ins = v.bn_stats(k.ln_st[:, t, :], src[:, t, :])
            ins.then_inc(vec.s, 1)
            v.wait_ge(vec.s, vec.at(1))
            for t in range(NT):
                ins = v.bn_aggr(k.ln_mv[:, t, :], k.ln_st[:, t, :])
            ins.then_inc(vec.s, 1)
            v.wait_ge(act.s, act.at(2))
            for t in range(NT):
                ins = v.tensor_scalar(dst[:, t, :], src[:, t, :], k.ln_mv[:, t, 0:1], k.ln_rs[:, t:t + 1],
                                      ALU.subtract, ALU.mult)
            ins.then_inc(vec.s, 1)
            nv[0] = 3
            if gain is not None:
                g3 = gain.unsqueeze(1).broadcast_to([P, NT, C])
                b3 = shift.unsqueeze(1).broadcast_to([P, NT, C])
                v.wait_ge(vec.s, vec.at(3))
                v.tensor_tensor(dst[:, :, :], dst[:, :, :], g3, ALU.mult).then_inc(vec.s, 1)
                v.wait_ge(vec.s, vec.at(4))
                v.tensor_tensor(dst[:, :, :], dst[:, :, :], b3, ALU.add).then_inc(vec.s, 1)
                nv[0] = 5

        @block.scalar
        def _(a):
            a.preload_act_table_set(EXP_LN)
            a.wait_ge(vec.s, vec.at(2))
            a.activation(k.ln_lg[:, :], k.ln_mv[:, :, 1], ACT.Ln, bias=k.eps[:, 0:1]).then_inc(act.s, 1)
            a.wait_ge(act.s, act.at(1))
            a.activation(k.ln_rs[:, :], k.ln_lg[:, :], ACT.Exp, scale=-0.5).then_inc(act.s, 1)
    vec.passed(nv[0])
    act.passed(2)


def stage_transpose(nc, k, src, outs):
    mm, read = k.sems["mm"], k.sems["read"]
    with nc.Block() as block:
        @block.tensor
        def _(pe):
            for t in range(NT):
                ins = pe.transpose(k.ps[:, t // 4, (t % 4) * P:(t % 4 + 1) * P], src[:, t, :], k.ident[:, :])
                if t % 4 == 3:
                    ins.then_inc(mm.s, 1)

        @block.vector
        def _(v):
            for half in range(2):
                v.wait_ge(mm.s, mm.at(half + 1))
                for dst, gain, shift in outs:
                    o = dst[:, half * 512:(half + 1) * 512]
                    if gain is None:
                        v.tensor_copy(o, k.ps[:, half, :]).then_inc(read.s, 1)
                    else:
                        v.tensor_scalar(o, k.ps[:, half, :], gain, shift, ALU.mult, ALU.add).then_inc(read.s, 1)
    mm.passed(2)
    read.passed(2 * len(outs))


def stage_load(nc, k, moves):
    loaded = k.sems["loaded"]
    with nc.Block() as block:
        @block.sync
        def _(sp):
            for dst, src in moves:
                sp.dma_start(dst, src).then_inc(loaded.s, 16)
            sp.wait_ge(loaded.s, loaded.at(16 * len(moves)))
    loaded.passed(16 * len(moves))


class Scratch:

    def __init__(self, nc, name, D, T, which, exact=False, thin=False):
        self.D, self.T = D, T
        self.exact = exact
        self.passes = 1 if exact or 6 * D <= P else 2
        self.spp = 1 if exact else 6 // self.passes
        self.R = D * self.spp
        self.thin = thin
        shape = (3, BH * D, T) if thin else (self.passes, BH * D, self.spp, T)
        self.ap = nc.dram_tensor(name, shape, F32 if exact else BF16, kind="Internal").ap()
        part = (Q_PART if which == "q" else K_PART)[self.passes]
        self.part = part
        self.moves = []
        for n, p in enumerate(part if not thin else ()):
            ps, sl = divmod(n, self.spp) if not exact else (0, 0)
            if self.moves and self.moves[-1][0] == ps:
                mp, ms, mn, m0, rep = self.moves[-1]
                if p == m0 and (mn == 1 or rep):
                    self.moves[-1] = (mp, ms, mn + 1, m0, True)
                    continue
                if p == m0 + mn and not rep:
                    self.moves[-1] = (mp, ms, mn + 1, m0, False)
                    continue
            self.moves.append((ps, sl, 1, p, False))
        self.stores = 1 if thin else len(self.moves)
        self.loads = 6 if thin else self.passes

    def store(self, sp, sem, row0, tile, col0, width):
        if self.thin:
            sp.dma_start(self.ap[:, bass.ds(row0, P), col0:col0 + width].rearrange("a r t -> r a t"),
                         tile[:, :, :]).then_inc(sem.s, 16)
            return
        for ps, slot, n, part, rep in self.moves:
            i = tile[:, part:part + 1, :].broadcast_to([P, n, width]) if rep else tile[:, part:part + n, :]
            sp.dma_start(self.ap[ps, bass.ds(row0, P), slot:slot + n, col0:col0 + width], i).then_inc(sem.s, 16)

    def load(self, sp, sem, dst, s, G):
        D, R = self.D, self.R
        if self.thin:
            for n, part in enumerate(self.part):
                ps, slot = divmod(n, self.spp)
                sp.dma_start(dst[slot * D:(slot + 1) * D, ps, :, :],
                             self.ap[part][bass.ds(s * (G * D), G * D), :].rearrange(
                                 "(g d) t -> d g t", g=G)).then_inc(sem.s, 16)
            return
        for ps in range(self.passes):
            v = self.ap[ps].rearrange("r s t -> (r s) t")[bass.ds(s * (G * R), G * R), :]
            sp.dma_start(dst[0:R, ps, :, :], v.rearrange("(g r) t -> r g t", g=G)).then_inc(sem.s, 16)


class Values:

    def __init__(self, nc, name, D, T):
        self.D, self.T = D, T
        self.DP = max(D, 32)
        self.G = P // self.DP
        self.NB = H // self.G
        self.ap = nc.dram_tensor(name, (B * self.NB, T, P), F32, kind="Internal").ap()

    def store(self, sp, sem, b, t0, n, tile):
        sp.dma_start(self.ap[bass.ds(b * self.NB, self.NB), t0:t0 + n, :].rearrange("k t c -> t k c"),
                     tile[0:n, :].rearrange("p (k c) -> p k c", c=P)).then_inc(sem.s, 16)


RING = 4
LAG = 2


def stage_project(nc, k, name, heads, values):
    mm, read, act, vec, pool = (k.sems[n] for n in ("mm", "read", "act", "vec", "pool"))
    wrote = [k.sems["wrote%d" % n] for n in range(RING)]
    vwrote = [k.sems["vwrote%d" % n] for n in range(RING)]
    units = [(item, c) for item in heads for c in range(2)]
    U = len(units)
    NV = NT if values else 0
    stored = [0] * RING
    before = []
    for u, (item, c) in enumerate(units):
        before.append(stored[u % RING])
        stored[u % RING] += 16 * 2 * item[3].stores
    if values:
        vsrc, vw, vbias, vals = values
        D, DP = vals.D, vals.DP
    with ExitStack() as ctx:
        full = ctx.enter_context(nc.sbuf_tensor(name + "_full", [P, RING, 512], F32))
        rest = ctx.enter_context(nc.sbuf_tensor(name + "_rest", [P, RING, 512], F32))
        part = ctx.enter_context(nc.sbuf_tensor(name + "_part", [P, RING, 3, 512], BF16))
        if values:
            vt = ctx.enter_context(nc.sbuf_tensor(name + "_vt", [P, RING, H * DP], F32))
            if DP > D:
                with nc.Block() as block:
                    @block.vector
                    def _(v):
                        v.memset(vt[:, :, :], 1.0)
        with nc.Block() as block:
            @block.tensor
            def _(pe):
                for u, ((srcT, w, bias, scr, row0), c) in enumerate(units):
                    pe.wait_ge(act.s, act.at(firsts(u - 4)))
                    pe.matmul(k.ps[:, u % 4, :], w, srcT[:, c * 512:(c + 1) * 512],
                              start=True, stop=True).then_inc(mm.s, 1)
                for t in range(NV):
                    pe.wait_ge(read.s, read.at(t - 3))
                    pe.matmul(k.ps[:, 4 + t % 4, 0:H * D], vsrc[:, t * P:(t + 1) * P], vw,
                              start=True, stop=True).then_inc(mm.s, 1)

            @block.scalar
            def _(a):
                for u in range(U + LAG):
                    if u < U:
                        bias = units[u][0][2]
                        a.wait_ge(mm.s, mm.at(u + 1))
                        if bias is None:
                            ins = a.activation(full[:, u % RING, :], k.ps[:, u % 4, :], ACT.Copy)
                        else:
                            ins = a.activation(full[:, u % RING, :], k.ps[:, u % 4, :], ACT.Identity, bias=bias)
                        ins.then_inc(act.s, 1)
                    if u >= LAG:
                        w_ = u - LAG
                        a.wait_ge(pool.s, pool.at(w_ + 1))
                        a.activation(part[:, w_ % RING, 1, :], rest[:, w_ % RING, :], ACT.Copy).then_inc(act.s, 1)

            @block.vector
            def _(v):
                for u in range(U + LAG):
                    if u < U:
                        v.wait_ge(act.s, act.at(firsts(u)))
                        v.wait_ge(wrote[u % RING].s, wrote[u % RING].at(before[u]))
                        v.tensor_copy(part[:, u % RING, 0, :], full[:, u % RING, :]).then_inc(vec.s, 1)
                    if u >= LAG:
                        w_ = u - LAG
                        v.wait_ge(act.s, act.at(seconds(w_, U)))
                        v.tensor_tensor(part[:, w_ % RING, 2, :], rest[:, w_ % RING, :], part[:, w_ % RING, 1, :],
                                        ALU.subtract).then_inc(vec.s, 1)
                for t in range(NV):
                    v.wait_ge(mm.s, mm.at(U + t + 1))
                    v.wait_ge(vwrote[t % RING].s, vwrote[t % RING].at(16 * (t // RING)))
                    o = vt[:, t % RING, :].rearrange("p (h d) -> p h d", d=DP)[:, :, 0:D]
                    i = k.ps[:, 4 + t % 4, 0:H * D].rearrange("p (h d) -> p h d", d=D)
                    if vbias is None:
                        v.tensor_copy(o, i).then_inc(read.s, 1)
                    else:
                        v.tensor_tensor(o, i, vbias.rearrange("p (h d) -> p h d", d=D), ALU.add).then_inc(read.s, 1)

            @block.gpsimd
            def _(g):
                for u in range(U):
                    g.wait_ge(vec.s, vec.at(firsts(u)))
                    g.tensor_tensor(rest[:, u % RING, :], full[:, u % RING, :], part[:, u % RING, 0, :],
                                    ALU.subtract).then_inc(pool.s, 1)

            @block.sync
            def _(sp):
                for u, ((srcT, w, bias, scr, row0), c) in enumerate(units):
                    sp.wait_ge(vec.s, vec.at(seconds(u, U)))
                    for bb in range(2):
                        scr.store(sp, wrote[u % RING], (2 * c + bb) * H * scr.D + row0,
                                  part[:, u % RING, :, bb * N:(bb + 1) * N], 0, N)
                for t in range(NV):
                    sp.wait_ge(read.s, read.at(t + 1))
                    vals.store(sp, vwrote[t % RING], t // 2, (t % 2) * P, P, vt[:, t % RING, :])
                for n in range(RING):
                    sp.wait_ge(wrote[n].s, wrote[n].at(stored[n]))
                    sp.wait_ge(vwrote[n].s, vwrote[n].at(16 * NV // RING))
    mm.passed(U + NV)
    act.passed(2 * U)
    vec.passed(2 * U)
    pool.passed(U)
    read.passed(NV)
    for n in range(RING):
        wrote[n].passed(stored[n])
        vwrote[n].passed(16 * NV // RING)


def firsts(u):
    return 0 if u < 0 else u + 1 + max(0, u - LAG)


def seconds(u, total):
    return min(u + LAG + 1, total) + u + 1


def stage_attention(nc, k, name, T, scale, mask, qs, ks, vals, out):
    cross = T == T_CTX
    fp32 = qs.exact
    dt = F32 if fp32 else BF16
    passes, R, G, DP = qs.passes, qs.R, vals.G, vals.DP
    SR = 64 if fp32 else 96
    NSH = 1 if fp32 else 2
    RS = R if fp32 else SR
    ident = k.ident if fp32 else k.identb
    NS = BH // G
    KT = KT_CTX if cross else 2
    NBUF = 4
    CW = 401
    if cross:
        slots = [(qt, g, 1, c) for g in range(G) for qt in range(2) for c in range(4)]
    elif mask == "causal":
        slots = [(0, 0, G, 0), (1, 0, 2, 0), (1, 2, 2, 0)]
    else:
        slots = [(qt, g, 2, 0) for qt in range(2) for g in range(0, G, 2)]
    groups = [[kt] for kt in range(KT)] if G == 4 else [[0, 1]]
    NG = len(groups)
    folded = DP > vals.D
    if folded:
        slots.insert((len(slots) + 1) // NG - 1, None)
    NSL = len(slots)
    PIECES = 2 if NSL == 2 else 4
    (scores, scores_read, negmax, shift_t, shift_in, st_ready, exp_done, probs_used, out_read,
     masked, vec, filled, divided, inverted) = (k.sems[n] for n in (
         "scores", "scores_read", "negmax", "shift_t", "shift_in", "st_ready", "exp_done", "probs_used",
         "out_read", "masked", "vec", "filled", "divided", "inverted"))
    ops = [k.sems["ops%d" % n] for n in range(NBUF)]
    arrived = [k.sems["values%d" % n] for n in range(2)]
    NDMA = qs.loads + ks.loads
    NVD = 2 if cross else 1
    VI = cross + (not fp32)
    NF = (5 if RS > R else 1) + folded

    with ExitStack() as ctx:
        def sb(n, shape, dtype=F32):
            return ctx.enter_context(nc.sbuf_tensor(name + "_" + n, shape, dtype))

        qb = sb("qb", [SR + NSH, NBUF, passes, G, N], dt)
        kb = sb("kb", [SR + NSH, NBUF, passes, G, T], dt)
        vs = sb("vs", [P, 2, KT, P])
        prob = sb("prob", [P, 2, 1024])
        pm = sb("pm", [P, 2, 2, G, P]) if mask == "after" else None
        mxp = sb("mxp", [P, 2 * G, 4]) if cross else None
        mx = sb("mx", [P, 2, 2 * G])
        negm = sb("negm", [P, 2, 2 * G, NSH], dt)
        sums = sb("sums", [P, 2, 2 * N])

        def rows_of(p, shifted):
            return SR + NSH if shifted and p == 0 else (RS if p == 0 else R)

        def st_columns(g, kt):
            if G < 4:
                return (kt * G + g) * N, 0
            if mask == "causal" and kt == 1:
                return g * P, P
            return g * N, 0

        def tile_rows(kt):
            return TAIL if cross and kt == KT - 1 else P

        with nc.Block() as block:
            @block.sync
            def _(sp):
                def load_qk(s, buf):
                    for dst, scr in ((qb, qs), (kb, ks)):
                        scr.load(sp, ops[buf], dst[:, buf, :, :, :], s, G)

                def load_values(s, vb):
                    v = vals.ap[bass.ds(s, 1), :, :].rearrange("s t c -> (s t) c")
                    n = (KT - 1) * P if cross else T
                    sp.dma_start(vs[:, vb, 0:n // P, :],
                                 v[0:n, :].rearrange("(k p) c -> p k c", p=P)).then_inc(arrived[vb].s, 16)
                    if cross:
                        sp.dma_start(vs[0:TAIL, vb, KT - 1, :], v[n:T, :]).then_inc(arrived[vb].s, 16)

                def load(s, buf, more=NBUF):
                    sp.wait_ge(probs_used.s, s * NG + probs_used.base)
                    if more > 2:
                        load_qk(s + 3, (buf + 3) % NBUF)
                    if more > 0:
                        load_values(s + 1, (buf + 1) % 2)

                sp.wait_ge(filled.s, filled.at(NF))
                for r in range(3):
                    load_qk(r, r)
                load_values(0, 0)
                rounds(sp, NS - NBUF, NBUF, load)
                for r in range(NBUF):
                    load(NS - NBUF + r, r, more=NBUF - 1 - r)

            @block.tensor
            def _(pe):
                def score_slot(s, buf, j):
                    if j == 0:
                        pe.wait_ge(ops[buf].s, (s - buf) * (16 * NDMA // NBUF) + (16 * NDMA + ops[buf].base))
                    pe.wait_ge(scores_read.s, (s * NSL + (j - 1)) + scores_read.base)
                    if slots[j] is None:
                        spread_denominators(s, (buf + 1) % 2, buf * NSL + j)
                        return
                    qt, g0, ng, c = slots[j]
                    bank = k.ps[:, (buf * NSL + j) % 2, :]
                    n = CW if cross else (P if mask == "causal" and qt == 0 else N)
                    k0 = c * (CW - 1)
                    for g in range(g0, g0 + ng):
                        o = bank[:, (g - g0) * n:(g - g0 + 1) * n]
                        r = rows_of(0, False)
                        ins = pe.matmul(o, qb[0:r, buf, 0, g, qt * P:(qt + 1) * P], kb[0:r, buf, 0, g, k0:k0 + n],
                                        start=True, stop=True)
                        if mask == "causal":
                            ins = pe.matmul(o[:, n - P:n], k.identb[:, :], k.mask_qk[:, :],
                                            start=False, stop=True, skip_group_check=True)
                    ins.then_inc(scores.s, 1)

                def shift_rows(s, buf):
                    pe.wait_ge(negmax.s, (s + 1) + negmax.base)
                    for g in range(G):
                        for qt in range(2):
                            r0 = 32 * (g // 2)
                            c0 = (g % 2) * N + qt * P
                            ins = pe.matmul(k.ps[r0:r0 + NSH, 7, c0:c0 + P], negm[:, buf % 2, qt * G + g, :],
                                            ident[:, :], start=True, stop=True)
                    ins.then_inc(shift_t.s, 1)

                def transposed_scores(s, buf, grp):
                    ring = (buf * NG + grp) % 2
                    if grp == 0:
                        pe.wait_ge(shift_in.s, (s + 1) + shift_in.base)
                    pe.wait_ge(exp_done.s, (s * NG + (grp - 1)) + exp_done.base)
                    banks = k.ps[:, 2 + 2 * ring:4 + 2 * ring, :].rearrange("p a b -> p (a b)")
                    for kt in groups[grp]:
                        rows = tile_rows(kt)
                        for g in range(G):
                            c, q0 = st_columns(g, kt)
                            o = banks[0:rows, c:c + N - q0]
                            for p in range(passes):
                                r = rows_of(p, True)
                                ins = pe.matmul(o, kb[0:r, buf, p, g, kt * P:kt * P + rows],
                                                qb[0:r, buf, p, g, q0:N], start=(p == 0), stop=(p == passes - 1))
                            if mask == "causal":
                                ins = pe.matmul(o[:, 0:P], k.identb[:, :], k.mask_kq[:, :],
                                                start=False, stop=True, skip_group_check=True)
                    ins.then_inc(st_ready.s, 1)

                def weigh(s, buf, grp, between=()):
                    ring = (buf * NG + grp) % 2
                    pe.wait_ge(exp_done.s, (s * NG + (grp + 1)) + exp_done.base)
                    if grp == 0:
                        pe.wait_ge(out_read.s, s + out_read.base)
                        pe.wait_ge(arrived[buf % 2].s,
                                   (s - buf % 2) * (8 * NVD) + (16 * NVD + arrived[buf % 2].base))
                    if mask == "after":
                        pe.wait_ge(masked.s, (s * NG + (grp + 1)) + masked.base)
                    for kt in groups[grp]:
                        rows = tile_rows(kt)
                        last = kt == KT - 1
                        for ones in (False,) if folded else (False, True):
                            for g in range(G):
                                c, q0 = st_columns(g, kt)
                                w = k.ones[0:rows, 0:DP] if ones else vs[0:rows, buf % 2, kt, g * DP:(g + 1) * DP]
                                o = k.ps[g * DP:(g + 1) * DP, 6, (N if ones else 0):(2 * N if ones else N)]
                                pr = prob[0:rows, ring, c:c + N - q0]
                                if ones or mask != "after":
                                    ins = pe.matmul(o[:, q0:N], w, pr, start=(kt == 0 and not ones), stop=last,
                                                    skip_group_check=True)
                                    continue
                                ins = pe.matmul(o[:, kt * P:(kt + 1) * P], w, pm[:, ring, kt, g, :], start=(kt == 0),
                                                stop=last, skip_group_check=True)
                                if kt == 1:
                                    ins = pe.matmul(o[:, 0:P], w, pr[:, 0:P], start=False, stop=last,
                                                    skip_group_check=True)
                            if kt == groups[grp][-1] and not ones:
                                for j in between:
                                    score_slot(s + 2, (buf + 2) % NBUF, j)
                    ins.then_inc(probs_used.s, 1)

                def spread_denominators(m, par, index):
                    pe.wait_ge(out_read.s, (m - 2) + out_read.base)
                    pe.matmul(k.ps[:, index % 2, 0:N], k.spread[:, :], sums[:, par, 0:N],
                              start=True, stop=True).then_inc(scores.s, 1)

                def last_denominators(s):
                    index = NS * NSL + (s - (NS - 2))
                    pe.wait_ge(scores_read.s, index - 1 + scores_read.base)
                    spread_denominators(s + 2, (s - 1) % 2, index)

                def step(s, buf, more=NBUF):
                    for grp in range(NG):
                        here = range(grp * NSL // NG, (grp + 1) * NSL // NG) if more > 1 else ()
                        n = len(here)
                        a_, b_ = (n, n) if NG == 1 else (max(0, n - 2), max(0, n - 1)) if cross else ((n + 1) // 2,) * 2
                        ahead, middle, beside = here[0:a_], here[a_:b_], here[b_:]
                        if NG == 1 and more > 0:
                            shift_rows(s + 1, buf + 1)
                        for j in ahead:
                            score_slot(s + 2, (buf + 2) % NBUF, j)
                        if grp < NG - 1:
                            transposed_scores(s, buf, grp + 1)
                        elif more > 0:
                            transposed_scores(s + 1, (buf + 1) % NBUF, 0)
                        for j in middle:
                            score_slot(s + 2, (buf + 2) % NBUF, j)
                        if NG > 1 and grp == 0 and more > 0:
                            shift_rows(s + 1, buf + 1)
                        weigh(s, buf, grp, beside)
                        if folded and grp == 0 and more <= 1:
                            last_denominators(NS - 1 - more)

                pe.wait_ge(filled.s, filled.at(NF))
                for r in range(2):
                    for j in range(NSL):
                        score_slot(r, r, j)
                shift_rows(0, 0)
                transposed_scores(0, 0, 0)
                rounds(pe, NS - NBUF, NBUF, step)
                for r in range(NBUF):
                    step(NS - NBUF + r, r, more=NBUF - 1 - r)
                if folded:
                    last_denominators(NS)

            @block.vector
            def _(v):
                def maxima(s, buf, between=None):
                    v.wait_ge(negmax.s, (s - 1) + negmax.base)
                    held = 0
                    for j, slot in enumerate(slots):
                        v.wait_ge(scores.s, (s * NSL + (j + 1)) + scores.base)
                        bank = k.ps[:, (buf * NSL + j) % 2, :]
                        if slot is None:
                            v.tensor_copy(sums[:, (buf + 1) % 2, N:2 * N], bank[:, 0:N]).then_inc(scores_read.s, 1)
                            held = j + 1
                            v.wait_ge(scores_read.s, (s * NSL + (j + 1)) + scores_read.base)
                            continue
                        qt, g0, ng, c = slot
                        if cross:
                            i, o = bank[:, 0:CW], mxp[:, qt * G + g0, c:c + 1]
                        else:
                            n = P if mask == "causal" and qt == 0 else N
                            i = bank[:, 0:ng * n].rearrange("p (g n) -> p g n", g=ng)
                            o = mx[:, buf % 2, qt * G + g0:qt * G + g0 + ng]
                        v.tensor_reduce(o, i, AX.X, ALU.max).then_inc(scores_read.s, 1)
                        if between and held <= j < PIECES + held and (held or not folded):
                            between(j - held)
                    v.wait_ge(scores_read.s, (s + 1) * NSL + scores_read.base)
                    high = negm[:, buf % 2, :, 0]
                    if cross:
                        v.tensor_reduce(mx[:, buf % 2, :], mxp[:, :, :], AX.X, ALU.max).then_inc(vec.s, 1)
                        v.wait_ge(vec.s, s * VI + (1 + vec.base))
                    if fp32:
                        v.tensor_scalar(high, mx[:, buf % 2, :], -1.0, None, ALU.mult).then_inc(negmax.s, 1)
                    else:
                        v.tensor_scalar(high, mx[:, buf % 2, :], -1.0, None, ALU.mult).then_inc(vec.s, 1)
                        v.wait_ge(vec.s, s * VI + (VI + vec.base))
                        v.scalar_tensor_tensor(out=negm[:, buf % 2, :, 1], in0=mx[:, buf % 2, :], scalar=-1.0, in1=high,
                                               op0=ALU.mult, op1=ALU.subtract).then_inc(negmax.s, 1)
                    for piece in range(NSL - held, PIECES):
                        if between:
                            between(piece)

                def invert(s, buf, piece):
                    if piece == 0 and not folded:
                        v.wait_ge(out_read.s, (s + 1) + out_read.base)
                    w_ = N // PIECES
                    d_ = sums[:, buf % 2, N + piece * w_:N + (piece + 1) * w_]
                    ins = v.reciprocal(d_, d_)
                    if piece == PIECES - 1:
                        ins.then_inc(inverted.s, 1)

                def both(s, buf, more=True):
                    if more:
                        maxima(s + 3, (buf + 3) % NBUF, lambda piece: invert(s, buf, piece))
                    else:
                        if folded:
                            index = NS * NSL + (buf - (NBUF - 3))
                            v.wait_ge(scores.s, index + 1 + scores.base)
                            v.tensor_copy(sums[:, buf % 2, N:2 * N],
                                          k.ps[:, index % 2, 0:N]).then_inc(scores_read.s, 1)
                            v.wait_ge(scores_read.s, index + 1 + scores_read.base)
                        for piece in range(PIECES):
                            invert(s, buf, piece)

                for r in range(3):
                    maxima(r, r)
                rounds(v, NS - NBUF, NBUF, both)
                for r in range(NBUF):
                    both(NS - NBUF + r, r, more=(r < NBUF - 3))

            @block.scalar
            def _(a):
                def shift(s, buf):
                    a.wait_ge(shift_t.s, (s + 1) + shift_t.base)
                    for g in range(0, G, 2):
                        ins = a.activation(qb[SR:SR + NSH, buf, 0, g:g + 2, :].rearrange("p g n -> p (g n)"),
                                           k.ps[16 * g:16 * g + NSH, 7, 0:2 * N], ACT.Copy)
                    ins.then_inc(shift_in.s, 1)

                def step(s, buf, more=True):
                    for grp in range(NG):
                        ring = (buf * NG + grp) % 2
                        rows = tile_rows(groups[grp][-1])
                        n = G * P if mask == "causal" and grp == 1 else len(groups[grp]) * G * N
                        a.wait_ge(st_ready.s, (s * NG + (grp + 1)) + st_ready.base)
                        a.wait_ge(probs_used.s, (s * NG + (grp - 1)) + probs_used.base)
                        banks = k.ps[:, 2 + 2 * ring:4 + 2 * ring, :].rearrange("p a b -> p (a b)")
                        a.activation(prob[0:rows, ring, 0:n], banks[0:rows, 0:n], ACT.Exp,
                                     scale=scale).then_inc(exp_done.s, 1)
                        if grp == min(1, NG - 1) and more:
                            shift(s + 1, (buf + 1) % NBUF)
                    a.wait_ge(divided.s, (s - 1) + divided.base)
                    a.wait_ge(probs_used.s, (s + 1) * NG + probs_used.base)
                    n = N if folded else 2 * N
                    a.activation(sums[:, buf % 2, 0:n], k.ps[:, 6, 0:n], ACT.Copy).then_inc(out_read.s, 1)

                shift(0, 0)
                rounds(a, NS - NBUF, NBUF, step)
                for r in range(NBUF):
                    step(NS - NBUF + r, r, more=(r < NBUF - 1))

            @block.gpsimd
            def _(g_):
                if folded:
                    g_.memset(sums[:, :, 0:N], 0.0).then_inc(filled.s, 1)
                    g_.wait_ge(filled.s, filled.at(1))
                if RS > R:
                    for buf in (kb, qb):
                        for r in (32, 64):
                            g_.memset(buf[r:r + 32, :, :, :, :], 0.0).then_inc(filled.s, 1)
                g_.memset(kb[SR:SR + NSH, :, 0, :, :], 1.0).then_inc(filled.s, 1)
                g_.wait_ge(filled.s, filled.at(NF))

                def masks(s, buf):
                    keep = k.keep_kq[:, :].unsqueeze(1).broadcast_to([P, G, P])
                    for kt in range(2):
                        ring = (buf * NG + kt) % 2
                        g_.wait_ge(exp_done.s, (s * NG + (kt + 1)) + exp_done.base)
                        g_.wait_ge(probs_used.s, (s * NG + (kt - 1)) + probs_used.base)
                        i = prob[:, ring, :].rearrange("p (g n) -> p g n", g=G)
                        g_.tensor_tensor(pm[:, ring, kt, :, :], i[:, :, kt * P:(kt + 1) * P], keep,
                                         ALU.mult).then_inc(masked.s, 1)

                def divide(s, buf):
                    g_.wait_ge(inverted.s, (s + 1) + inverted.base)
                    g_.tensor_tensor(out[:, bass.ds(s * N, N)], sums[:, buf % 2, 0:N], sums[:, buf % 2, N:2 * N],
                                     ALU.mult).then_inc(divided.s, 1)

                def both(s, buf, more=True):
                    if mask == "after" and more:
                        masks(s + 1, (buf + 1) % NBUF)
                    divide(s, buf)

                if mask == "after":
                    masks(0, 0)
                rounds(g_, NS - NBUF, NBUF, both)
                for r in range(NBUF):
                    both(NS - NBUF + r, r, more=(r < NBUF - 1))

    for s_, n_ in [(scores, NS * NSL + 3 * folded), (scores_read, NS * NSL + 3 * folded), (negmax, NS),
                   (shift_t, NS), (shift_in, NS), (st_ready, NS * NG), (exp_done, NS * NG),
                   (probs_used, NS * NG), (out_read, NS), (divided, NS), (inverted, NS),
                   (masked, NS * NG if mask == "after" else 0), (vec, VI * NS), (filled, NF)] \
            + [(o, NS // NBUF * 16 * NDMA) for o in ops] + [(o, NS // 2 * 16 * NVD) for o in arrived]:
        s_.passed(n_)


def stage_output(nc, k, terms, w, bias):
    mm2, vec = k.sems["mm2"], k.sems["vec"]
    nb = w.shape[1] // C
    with nc.Block() as block:
        @block.gpsimd
        def _(g):
            if bias is not None:
                g.tensor_tensor(k.x[:, :, :], k.x[:, :, :], bias.unsqueeze(1).broadcast_to([P, NT, C]),
                                ALU.add).then_inc(k.sems["pool"].s, 1)

        @block.tensor
        def _(pe):
            for t in range(NT):
                todo = [(o, j) for o in terms for j in range(nb)]
                for n, (o, j) in enumerate(todo):
                    c0 = ((t // 2) * nb + j) * N + (t % 2) * P
                    ins = pe.matmul(k.ps[:, t // 4, (t % 4) * P:(t % 4 + 1) * P], o[:, c0:c0 + P],
                                    w[:, j * C:(j + 1) * C], start=(n == 0), stop=(n == len(todo) - 1))
                if t % 4 == 3:
                    ins.then_inc(mm2.s, 1)

        @block.vector
        def _(v):
            if bias is not None:
                v.wait_ge(k.sems["pool"].s, k.sems["pool"].at(1))
            for half in range(2):
                v.wait_ge(mm2.s, mm2.at(half + 1))
                xs = k.x[:, half * 4:half * 4 + 4, :].rearrange("p t c -> p (t c)")
                v.tensor_tensor(xs, k.ps[:, half, :], xs, ALU.add).then_inc(vec.s, 1)
    mm2.passed(2)
    vec.passed(2)
    if bias is not None:
        k.sems["pool"].passed(1)


def stage_project_rotary(nc, k, w1, wf, qs, ks, values):
    mm, read, vec, pool, act = (k.sems[n] for n in ("mm", "read", "vec", "pool", "act"))
    wrote = (k.sems["wrote0"], k.sems["wrote1"])
    D = 64
    units = [(which, j, c) for which in "qk" for j in range(8) for c in range(2)]
    vunits = [(t, half) for t in range(NT) for half in range(2)]
    vwrote = [k.sems["vwrote%d" % n] for n in range(RING)]
    with ExitStack() as ctx:
        vt = ctx.enter_context(nc.sbuf_tensor("rot_vt", [P, RING, H * D], F32))
        fenc = ctx.enter_context(nc.sbuf_tensor("fenc", [P, N], F32))
        turned = ctx.enter_context(nc.sbuf_tensor("turned", [P, 2, 2, 512], F32))
        full = ctx.enter_context(nc.sbuf_tensor("rot_full", [P, 2, 512], F32))
        with nc.Block() as block:
            @block.tensor
            def _(pe):
                pe.matmul(k.ps[:, 7, 0:N], sub(wf, WF, "fp", 32), sub(wf, WF, "fourier", 32),
                          start=True, stop=True).then_inc(mm.s, 1)

            @block.scalar
            def _(a):
                a.wait_ge(mm.s, mm.at(1))
                a.activation(fenc[:, :], k.ps[:, 7, 0:N], ACT.Identity,
                             bias=sub(k.col, COL, "fp")).then_inc(act.s, 1)
        mm.passed(1)
        act.passed(1)
        with nc.Block() as block:
            @block.tensor
            def _(pe):
                for u, (which, j, c) in enumerate(units):
                    pe.wait_ge(vec.s, vec.at(2 * (u - 1)))
                    for r, suffix in enumerate(("", "r")):
                        a0 = W1[which + suffix][0] + j * P
                        ins = pe.matmul(k.ps[:, (u % 2) * 2 + r, :], w1[:, a0:a0 + P],
                                        k.xT[:, c * 512:(c + 1) * 512], start=True, stop=True)
                    ins.then_inc(mm.s, 1)
                for u, (t, half) in enumerate(vunits):
                    pe.wait_ge(act.s, act.at(u - 3))
                    a0 = W1["v"][0] + half * 512
                    pe.matmul(k.ps[:, 4 + u % 4, :], k.xT[:, t * P:(t + 1) * P], w1[:, a0:a0 + 512],
                              start=True, stop=True).then_inc(mm.s, 1)

            @block.vector
            def _(v):
                for u, (which, j, c) in enumerate(units):
                    v.wait_ge(mm.s, mm.at(u + 1))
                    v.wait_ge(pool.s, pool.at(2 * (u - 1)))
                    for r, table in enumerate(("cos", "sin")):
                        v.tensor_tensor(turned[:, u % 2, r, :].rearrange("p (b n) -> p b n", b=2),
                                        k.ps[:, (u % 2) * 2 + r, :].rearrange("p (b n) -> p b n", b=2),
                                        sub(w1, W1, table).unsqueeze(1).broadcast_to([P, 2, N]),
                                        ALU.mult).then_inc(vec.s, 1)

            @block.gpsimd
            def _(g):
                for u, (which, j, c) in enumerate(units):
                    g.wait_ge(vec.s, vec.at(2 * u + 2))
                    g.wait_ge(wrote[u % 2].s, wrote[u % 2].at(16 * (u // 2)))
                    g.tensor_tensor(full[:, u % 2, :], turned[:, u % 2, 0, :], turned[:, u % 2, 1, :],
                                    ALU.add).then_inc(pool.s, 1)
                    g.wait_ge(pool.s, pool.at(2 * u + 1))
                    f3 = full[:, u % 2, :].rearrange("p (b n) -> p b n", b=2)
                    g.tensor_tensor(f3, f3, fenc[:, :].unsqueeze(1).broadcast_to([P, 2, N]),
                                    ALU.add).then_inc(pool.s, 1)

            @block.scalar
            def _(a):
                for u, (t, half) in enumerate(vunits):
                    a.wait_ge(mm.s, mm.at(len(units) + u + 1))
                    a.wait_ge(vwrote[t % RING].s, vwrote[t % RING].at(16 * (t // RING)))
                    a.activation(vt[:, t % RING, half * 512:(half + 1) * 512], k.ps[:, 4 + u % 4, :],
                                 ACT.Copy).then_inc(act.s, 1)

            @block.sync
            def _(sp):
                for u, (which, j, c) in enumerate(units):
                    sp.wait_ge(pool.s, pool.at(2 * u + 2))
                    dst = (qs if which == "q" else ks).ap[0].rearrange("(b r) s t -> r b (s t)", b=B)
                    sp.dma_start(dst[j * P:(j + 1) * P, 2 * c:2 * c + 2, :],
                                 full[:, u % 2, :].rearrange("p (b n) -> p b n", b=2)).then_inc(wrote[u % 2].s, 16)
                for t in range(NT):
                    sp.wait_ge(act.s, act.at(2 * t + 2))
                    values.store(sp, vwrote[t % RING], t // 2, (t % 2) * P, P, vt[:, t % RING, :])
                for n in range(2):
                    sp.wait_ge(wrote[n].s, wrote[n].at(16 * len(units) // 2))
                for n in range(RING):
                    sp.wait_ge(vwrote[n].s, vwrote[n].at(16 * NT // RING))
    mm.passed(len(units) + len(vunits))
    vec.passed(2 * len(units))
    pool.passed(2 * len(units))
    act.passed(len(vunits))
    for w_ in vwrote:
        w_.passed(16 * NT // RING)
    for n in range(2):
        wrote[n].passed(16 * len(units) // 2)


def stage_context(nc, k, name, wk, wv, kbias, vbias, scratch, vals, ctxT=None, ctx_rows=None,
                  gain=None, shift=None):
    norm = ctx_rows is not None
    D, DP = vals.D, vals.DP
    HD = H * D
    widths = [401, 400, 400, 400]
    starts = [0, 401, 801, 1201]
    units = [(j, c) for j in range(HD // P) for c in range(4)]
    U = len(units)
    NTR = 4 if norm else 0
    RD = NTR + KT_CTX
    MM = NTR + U + KT_CTX
    ND = 16 * scratch.stores
    NV = 2 * U + (3 if norm else 0)
    NA = 2 * U + (2 if norm else 0)
    NLOAD = 32 if norm else 16
    VN = [len(range(r, KT_CTX, RING)) * 16 for r in range(RING)]
    mm, read, act, vec, pool, loaded = (k.sems[n] for n in ("mm", "read", "act", "vec", "pool", "loaded"))
    wrote = [k.sems["wrote%d" % n] for n in range(RING)]
    vwrote = [k.sems["vwrote%d" % n] for n in range(RING)]
    va, vv = act.base + NA - 2 * U, vec.base + NV - 2 * U
    with ExitStack() as ctx:
        def sb(n, shape, dtype=F32):
            return ctx.enter_context(nc.sbuf_tensor(name + "_" + n, shape, dtype))

        cT = sb("cT", [CC, KT_CTX * P if norm else T_CTX])
        full = sb("full", [P, RING, 401])
        rest = sb("rest", [P, RING, 401])
        part = sb("part", [P, RING, 3, 401], BF16)
        vt = sb("vt", [P, RING, H * DP])
        if norm:
            rows = sb("rows", [P, KT_CTX, CC])
            st = sb("st", [P, KT_CTX, 6])
            mv = sb("mv", [P, KT_CTX, 2])
            lg = sb("lg", [P, KT_CTX])
            rs = sb("rs", [P, KT_CTX])
        with nc.Block() as block:
            @block.gpsimd
            def _(g):
                if norm:
                    g.memset(rows[:, KT_CTX - 1, :], 0.0)

            @block.vector
            def _(v):
                if DP > D:
                    v.memset(vt[:, :, :], 1.0)
        with nc.Block() as block:
            @block.sync
            def _(sp):
                with sp.Fori(0, B) as b:
                    sp.wait_ge(mm.s, b * MM + mm.base)
                    if norm:
                        src = ctx_rows[bass.ds(b * T_CTX, T_CTX), :]
                        sp.dma_start(rows[:, 0:KT_CTX - 1, :], src[0:T_CTX - TAIL, :].rearrange(
                            "(t p) c -> p t c", p=P)).then_inc(loaded.s, 16)
                        sp.dma_start(rows[0:TAIL, KT_CTX - 1, :], src[T_CTX - TAIL:T_CTX, :]).then_inc(loaded.s, 16)
                    else:
                        sp.dma_start(cT[:, :], ctxT[:, bass.ds(b * T_CTX, T_CTX)]).then_inc(loaded.s, 16)
                    for u, (j, c) in enumerate(units):
                        sp.wait_ge(vec.s, b * NV + (seconds(u, U) + vv))
                        scratch.store(sp, wrote[u % RING], b * HD + j * P, part[:, u % RING, :, 0:widths[c]],
                                      starts[c], widths[c])
                    for t in range(KT_CTX):
                        sp.wait_ge(read.s, b * RD + (NTR + t + 1 + read.base))
                        vals.store(sp, vwrote[t % RING], b, t * P, P if t < KT_CTX - 1 else TAIL,
                                   vt[:, t % RING, :])
                for n in range(RING):
                    sp.wait_ge(wrote[n].s, wrote[n].at(B * U // RING * ND))
                    sp.wait_ge(vwrote[n].s, vwrote[n].at(B * VN[n]))

            @block.tensor
            def _(pe):
                with pe.Fori(0, B) as b:
                    if norm:
                        pe.wait_ge(vec.s, b * NV + (3 + vec.base))
                        pe.wait_ge(read.s, b * RD + read.base)
                        pe.transpose(k.ps[:, 4, 0:P], k.x[:, 0, :], k.ident[:, :])
                        for t in range(KT_CTX):
                            ins = pe.transpose(k.ps[0:CC, 4 + t // 4, (t % 4) * P:(t % 4 + 1) * P],
                                               rows[:, t, :], k.ident[:, :])
                            if t % 4 == 3 or t == KT_CTX - 1:
                                ins.then_inc(mm.s, 1)
                        pe.wait_ge(read.s, b * RD + (NTR + read.base))
                    else:
                        pe.wait_ge(loaded.s, b * NLOAD + (NLOAD + loaded.base))
                    for u, (j, c) in enumerate(units):
                        pe.wait_ge(act.s, b * NA + (firsts(u - 4) + va))
                        pe.matmul(k.ps[:, u % 4, 0:widths[c]], wk[:, j * P:(j + 1) * P],
                                  cT[:, starts[c]:starts[c] + widths[c]], start=True, stop=True).then_inc(mm.s, 1)
                    for t in range(KT_CTX):
                        n = P if t < KT_CTX - 1 else TAIL
                        pe.wait_ge(read.s, b * RD + ((NTR + t - 3 if t > 3 else NTR) + read.base))
                        pe.matmul(k.ps[0:n, 4 + t % 4, 0:HD], cT[:, t * P:t * P + n], wv,
                                  start=True, stop=True).then_inc(mm.s, 1)

            @block.scalar
            def _(a):
                if norm:
                    a.preload_act_table_set(EXP_LN)
                with a.Fori(0, B) as b:
                    if norm:
                        a.wait_ge(vec.s, b * NV + (2 + vec.base))
                        a.activation(lg[:, :], mv[:, :, 1], ACT.Ln, bias=k.eps[:, 0:1]).then_inc(act.s, 1)
                        a.wait_ge(act.s, b * NA + (1 + act.base))
                        a.activation(rs[:, :], lg[:, :], ACT.Exp, scale=-0.5).then_inc(act.s, 1)
                    for u in range(U + LAG):
                        if u < U:
                            W = widths[units[u][1]]
                            i, o = k.ps[:, u % 4, 0:W], full[:, u % RING, 0:W]
                            a.wait_ge(mm.s, b * MM + (NTR + u + 1 + mm.base))
                            if kbias is None:
                                a.activation(o, i, ACT.Copy).then_inc(act.s, 1)
                            else:
                                a.activation(o, i, ACT.Identity, bias=kbias).then_inc(act.s, 1)
                        if u >= LAG:
                            w_, W = u - LAG, widths[units[u - LAG][1]]
                            a.wait_ge(pool.s, b * U + (w_ + 1 + pool.base))
                            a.activation(part[:, w_ % RING, 1, 0:W], rest[:, w_ % RING, 0:W],
                                         ACT.Copy).then_inc(act.s, 1)

            @block.vector
            def _(v):
                def value_tile(b, t):
                    n = P if t < KT_CTX - 1 else TAIL
                    v.wait_ge(mm.s, b * MM + (NTR + U + t + 1 + mm.base))
                    r = t % RING
                    v.wait_ge(vwrote[r].s, b * VN[r] + (16 * (t // RING) + vwrote[r].base))
                    o = vt[0:n, r, :].rearrange("p (h d) -> p h d", d=DP)[:, :, 0:D]
                    i = k.ps[0:n, 4 + t % 4, 0:HD].rearrange("p (h d) -> p h d", d=D)
                    if vbias is None:
                        v.tensor_copy(o, i).then_inc(read.s, 1)
                    else:
                        v.tensor_tensor(o, i, vbias[0:n, :].rearrange("p (h d) -> p h d", d=D),
                                        ALU.add).then_inc(read.s, 1)

                with v.Fori(0, B) as b:
                    if norm:
                        v.wait_ge(loaded.s, b * NLOAD + (NLOAD + loaded.base))
                        for t in range(KT_CTX):
                            ins = v.bn_stats(st[:, t, :], rows[:, t, :])
                        ins.then_inc(vec.s, 1)
                        v.wait_ge(vec.s, b * NV + (1 + vec.base))
                        v.memset(lg[:, :], 0.0)
                        for t in range(KT_CTX):
                            ins = v.bn_aggr(mv[:, t, :], st[:, t, :])
                        ins.then_inc(vec.s, 1)
                        v.wait_ge(act.s, b * NA + (2 + act.base))
                        for t in range(KT_CTX):
                            ins = v.tensor_scalar(rows[:, t, :], rows[:, t, :], mv[:, t, 0:1], rs[:, t:t + 1],
                                                  ALU.subtract, ALU.mult)
                        ins.then_inc(vec.s, 1)
                        for q in range(NTR):
                            n = 512 if q < 3 else P
                            v.wait_ge(mm.s, b * MM + (q + 1 + mm.base))
                            v.tensor_scalar(cT[:, q * 512:q * 512 + n], k.ps[0:CC, 4 + q, 0:n], gain, shift,
                                            ALU.mult, ALU.add).then_inc(read.s, 1)
                    for u in range(U + LAG):
                        if u < U:
                            W = widths[units[u][1]]
                            v.wait_ge(act.s, b * NA + (firsts(u) + va))
                            s_ = wrote[u % RING]
                            v.wait_ge(s_.s, b * (U // RING * ND) + (u // RING * ND + s_.base))
                            v.tensor_copy(part[:, u % RING, 0, 0:W], full[:, u % RING, 0:W]).then_inc(vec.s, 1)
                        if u >= LAG:
                            w_, W = u - LAG, widths[units[u - LAG][1]]
                            v.wait_ge(act.s, b * NA + (seconds(w_, U) + va))
                            v.tensor_tensor(part[:, w_ % RING, 2, 0:W], rest[:, w_ % RING, 0:W],
                                            part[:, w_ % RING, 1, 0:W], ALU.subtract).then_inc(vec.s, 1)
                    for t in range(KT_CTX):
                        value_tile(b, t)

            @block.gpsimd
            def _(g):
                with g.Fori(0, B) as b:
                    for u, (j, c) in enumerate(units):
                        W = widths[c]
                        g.wait_ge(vec.s, b * NV + (firsts(u) + vv))
                        g.tensor_tensor(rest[:, u % RING, 0:W], full[:, u % RING, 0:W], part[:, u % RING, 0, 0:W],
                                        ALU.subtract).then_inc(pool.s, 1)
    mm.passed(B * MM)
    read.passed(B * RD)
    act.passed(B * NA)
    vec.passed(B * NV)
    pool.passed(B * U)
    loaded.passed(B * NLOAD)
    for n in range(RING):
        wrote[n].passed(B * U // RING * ND)
        vwrote[n].passed(B * VN[n])


def stage_logits(nc, k, w, dst, scale):
    mm, vec = k.sems["mm"], k.sems["vec"]
    with nc.Block() as block:
        @block.tensor
        def _(pe):
            for t in range(NT):
                ins = pe.matmul(k.ps[:, 0, t * E:(t + 1) * E], k.xT[:, t * P:(t + 1) * P], w, start=True, stop=True)
            ins.then_inc(mm.s, 1)

        @block.vector
        def _(v):
            v.wait_ge(mm.s, mm.at(1))
            v.tensor_scalar(dst[:, :, :].rearrange("p t e -> p (t e)"), k.ps[:, 0, 0:NT * E], scale, None,
                            ALU.mult).then_inc(vec.s, 1)
    mm.passed(1)
    vec.passed(1)


def stage_sinkhorn(nc, k, la):
    mm, vec, act = k.sems["mm"], k.sems["vec"], k.sems["act"]
    with ExitStack() as ctx:
        def sb(n, shape):
            return ctx.enter_context(nc.sbuf_tensor("sink_" + n, shape, F32))

        mr, sm, lg = sb("mr", [P, NT]), sb("sm", [P, NT]), sb("lg", [P, NT])
        ex = sb("ex", [P, NT, E])
        mc, sc, lc = sb("mc", [P, E]), sb("sc", [P, E]), sb("lc", [P, E])
        m8, dg = sb("m8", [E, 1]), sb("dg", [E, E])
        la_et = la[:, :, :].rearrange("p t e -> p e t")

        def over_experts(a):
            return a.unsqueeze(2).broadcast_to([P, NT, E])

        def over_tiles(a):
            return a.unsqueeze(1).broadcast_to([P, NT, E])

        with nc.Block() as block:
            @block.vector
            def _(v):
                with v.Fori(0, SINK_ITERS) as i:
                    v.tensor_reduce(mr[:, :], la[:, :, :], AX.X, ALU.max).then_inc(vec.s, 1)
                    v.wait_ge(vec.s, i * 10 + (1 + vec.base))
                    v.tensor_tensor(la[:, :, :], la[:, :, :], over_experts(mr[:, :]), ALU.subtract).then_inc(vec.s, 1)
                    v.wait_ge(act.s, i * 4 + (1 + act.base))
                    v.tensor_reduce(sm[:, :], ex[:, :, :], AX.X, ALU.add).then_inc(vec.s, 1)
                    v.wait_ge(act.s, i * 4 + (2 + act.base))
                    v.tensor_tensor(la[:, :, :], la[:, :, :], over_experts(lg[:, :]), ALU.subtract).then_inc(vec.s, 1)
                    v.wait_ge(vec.s, i * 10 + (4 + vec.base))
                    v.tensor_reduce(mc[:, :], la_et, AX.X, ALU.max).then_inc(vec.s, 1)
                    v.wait_ge(mm.s, i * 3 + (1 + mm.base))
                    v.tensor_reduce(m8[:, :], k.ps[0:E, 0, 0:P], AX.X, ALU.max).then_inc(vec.s, 1)
                    v.wait_ge(vec.s, i * 10 + (6 + vec.base))
                    v.tensor_scalar(dg[:, :], k.ident[0:E, 0:E], m8[:, 0:1], None, ALU.mult).then_inc(vec.s, 1)
                    v.wait_ge(mm.s, i * 3 + (2 + mm.base))
                    v.tensor_tensor(la[:, :, :], la[:, :, :], over_tiles(k.ps[:, 1, 0:E]),
                                    ALU.subtract).then_inc(vec.s, 1)
                    v.wait_ge(mm.s, i * 3 + (3 + mm.base))
                    v.tensor_reduce(sc[:, :], k.ps[:, 2, 0:NT * E].rearrange("p (t e) -> p e t", e=E),
                                    AX.X, ALU.add).then_inc(vec.s, 1)
                    v.wait_ge(act.s, i * 4 + (4 + act.base))
                    v.tensor_tensor(la[:, :, :], la[:, :, :], over_tiles(lc[:, :]), ALU.subtract).then_inc(vec.s, 1)
                    v.wait_ge(vec.s, i * 10 + (10 + vec.base))

            @block.scalar
            def _(a):
                a.preload_act_table_set(EXP_LN)
                with a.Fori(0, SINK_ITERS) as i:
                    a.wait_ge(vec.s, i * 10 + (2 + vec.base))
                    a.activation(ex[:, :, :], la[:, :, :], ACT.Exp).then_inc(act.s, 1)
                    a.wait_ge(vec.s, i * 10 + (3 + vec.base))
                    a.activation(lg[:, :], sm[:, :], ACT.Ln).then_inc(act.s, 1)
                    a.wait_ge(vec.s, i * 10 + (8 + vec.base))
                    a.activation(ex[:, :, :], la[:, :, :], ACT.Exp).then_inc(act.s, 1)
                    a.wait_ge(vec.s, i * 10 + (9 + vec.base))
                    a.activation(lc[:, :], sc[:, :], ACT.Ln).then_inc(act.s, 1)
                a.wait_ge(vec.s, vec.at(10 * SINK_ITERS))
                a.activation(la[:, :, :], la[:, :, :], ACT.Exp).then_inc(act.s, 1)

            @block.tensor
            def _(pe):
                with pe.Fori(0, SINK_ITERS) as i:
                    pe.wait_ge(vec.s, i * 10 + (5 + vec.base))
                    pe.transpose(k.ps[0:E, 0, 0:P], mc[:, :], k.ident[:, :]).then_inc(mm.s, 1)
                    pe.wait_ge(vec.s, i * 10 + (7 + vec.base))
                    pe.matmul(k.ps[:, 1, 0:E], k.ones[0:E, :], dg[:, :], start=True, stop=True).then_inc(mm.s, 1)
                    pe.wait_ge(act.s, i * 4 + (3 + act.base))
                    pe.matmul(k.ps[:, 2, 0:NT * E], k.ones[:, :], ex[:, :, :].rearrange("p t e -> p (t e)"),
                              start=True, stop=True).then_inc(mm.s, 1)
    mm.passed(3 * SINK_ITERS)
    vec.passed(10 * SINK_ITERS)
    act.passed(4 * SINK_ITERS + 1)


def stage_top(nc, k, name, score, weight, top, gains=None):
    vec = k.sems["vec"]
    with ExitStack() as ctx:
        def sb(n, shape):
            return ctx.enter_context(nc.sbuf_tensor(name + "_" + n, shape, F32))

        best, first = sb("best", [P, NT]), sb("first", [P, NT])
        cand, hot = sb("cand", [P, NT, E]), sb("hot", [P, NT, E])
        iota = sub(k.row, ROW, "iota").unsqueeze(1).broadcast_to([P, NT, E])
        with nc.Block() as block:
            @block.vector
            def _(v):
                n = [0]

                def link(ins):
                    n[0] += 1
                    ins.then_inc(vec.s, 1)
                    v.wait_ge(vec.s, vec.at(n[0]))

                def over(a):
                    return a[:, :].unsqueeze(2).broadcast_to([P, NT, E])

                for r in range(top):
                    link(v.tensor_reduce(best[:, :], score[:, :, :], AX.X, ALU.max))
                    link(v.tensor_tensor(cand[:, :, :], score[:, :, :], over(best), ALU.is_ge))
                    link(v.scalar_tensor_tensor(out=cand[:, :, :], in0=cand[:, :, :], scalar=-float(E),
                                                in1=iota, op0=ALU.mult, op1=ALU.add))
                    link(v.tensor_reduce(first[:, :], cand[:, :, :], AX.X, ALU.min))
                    link(v.tensor_tensor(hot[:, :, :], cand[:, :, :], over(first), ALU.is_equal))
                    if gains is None:
                        link(v.tensor_copy(weight[:, :, :], hot[:, :, :]))
                    elif r == 0:
                        link(v.tensor_tensor(weight[:, :, :], hot[:, :, :], gains[r], ALU.mult))
                    else:
                        link(v.tensor_tensor(cand[:, :, :], hot[:, :, :], gains[r], ALU.mult))
                        link(v.tensor_tensor(weight[:, :, :], weight[:, :, :], cand[:, :, :], ALU.add))
                    if r < top - 1:
                        link(v.scalar_tensor_tensor(out=score[:, :, :], in0=hot[:, :, :], scalar=-4.0,
                                                    in1=score[:, :, :], op0=ALU.mult, op1=ALU.add))
        vec.passed(top * 6 + 2 * (top - 1))


def stage_experts(nc, k, name, srcT, w_in, w_down, weight, gated):
    mm, mm2, read, act, vec = (k.sems[n] for n in ("mm", "mm2", "read", "act", "vec"))
    weights = (k.sems["weights0"], k.sems["weights1"])
    nw = 2 if gated else 1
    U = 2 * FB
    with ExitStack() as ctx:
        def sb(n, shape, dtype=F32):
            return ctx.enter_context(nc.sbuf_tensor(name + "_" + n, shape, dtype))

        wi = sb("wi", [P, 2, nw * F])
        wd = sb("wd", [P, 2, FB * C])
        hid = sb("hid", [P, FB, NT * P])
        gate = sb("gate", [P, 2, 512]) if gated else None
        aff = None if gated else sb("aff", [P, 2, NT * P])
        b1 = None if gated else sb("b1", [P, 2, FB])
        with nc.Block() as block:
            @block.sync
            def _(sp):
                def load(e, par):
                    sp.wait_ge(mm2.s, e * 2 + (mm2.base - 2))
                    sp.dma_start(wi[:, par, :], w_in[bass.ds(e, 1), :, :].rearrange("e c f -> (e c) f")).then_inc(
                        weights[par].s, 16)
                    sp.dma_start(wd[:, par, :], w_down[bass.ds(e, 1), :, :].rearrange("e c f -> (e c) f")).then_inc(
                        weights[par].s, 16)

                rounds(sp, E, 2, load)

            @block.tensor
            def _(pe):
                def expert(e, par):
                    pe.wait_ge(weights[par].s, (e - par) * 16 + (32 + weights[par].base))
                    if not gated:
                        pe.wait_ge(vec.s, (e + 1) + vec.base)
                    for c in range(2):
                        for f in range(FB):
                            u = c * FB + f
                            done = act if not gated else vec
                            pe.wait_ge(done.s, e * U + (u - 1 + done.base))
                            rhs = (srcT if gated else aff[:, par, :])[:, c * 512:(c + 1) * 512]
                            for n in range(nw):
                                ins = pe.matmul(k.ps[:, 2 * n + u % 2, :],
                                                wi[:, par, n * F + f * P:n * F + (f + 1) * P], rhs,
                                                start=True, stop=True)
                            ins.then_inc(mm.s, 1)
                    for c in range(2):
                        done = act if not gated else vec
                        pe.wait_ge(done.s, e * U + (FB * (c + 1) + done.base))
                        pe.wait_ge(read.s, e * 2 + (c - 1 + read.base))
                        for t in range(4):
                            for f in range(FB):
                                ins = pe.matmul(k.ps[:, 4 + c, t * P:(t + 1) * P],
                                                hid[:, f, (c * 4 + t) * P:(c * 4 + t + 1) * P],
                                                wd[:, par, f * C:(f + 1) * C], start=(f == 0), stop=(f == FB - 1))
                        ins.then_inc(mm2.s, 1)

                rounds(pe, E, 2, expert)

            @block.scalar
            def _(a):
                def expert(e, par):
                    for c in range(2):
                        for f in range(FB):
                            u = c * FB + f
                            a.wait_ge(mm.s, e * U + (u + 1 + mm.base))
                            if gated:
                                a.wait_ge(vec.s, e * U + (u - 1 + vec.base))
                                a.activation(gate[:, u % 2, :], k.ps[:, u % 2, :], ACT.Silu).then_inc(act.s, 1)
                            else:
                                a.wait_ge(mm2.s, e * 2 + (c - 1 + mm2.base))
                                a.activation(hid[:, f, c * 512:(c + 1) * 512], k.ps[:, u % 2, :], ACT.Relu,
                                             bias=b1[:, par, f:f + 1]).then_inc(act.s, 1)

                rounds(a, E, 2, expert)

            @block.vector
            def _(v):
                def affine(e, par):
                    v.wait_ge(act.s, e * U + (act.base - U))
                    v.tensor_copy(b1[:, par, :], k.col[:, bass.ds(e * FB + COL["b1"][0], FB)])
                    v.tensor_scalar(aff[:, par, :], srcT[:, :], k.col[:, bass.ds(e + COL["ln_g"][0], 1)],
                                    k.col[:, bass.ds(e + COL["ln_b"][0], 1)], ALU.mult, ALU.add).then_inc(vec.s, 1)

                def expert(e, par, more=True):
                    if gated:
                        for c in range(2):
                            for f in range(FB):
                                u = c * FB + f
                                v.wait_ge(act.s, e * U + (u + 1 + act.base))
                                v.wait_ge(mm2.s, e * 2 + (c - 1 + mm2.base))
                                v.tensor_tensor(hid[:, f, c * 512:(c + 1) * 512], gate[:, u % 2, :],
                                                k.ps[:, 2 + u % 2, :], ALU.mult).then_inc(vec.s, 1)
                    elif more:
                        affine(e + 1, 1 - par)
                    for c in range(2):
                        v.wait_ge(mm2.s, e * 2 + (c + 1 + mm2.base))
                        for t in range(4):
                            tile = c * 4 + t
                            ins = v.scalar_tensor_tensor(out=k.x[:, tile, :], in0=k.ps[:, 4 + c, t * P:(t + 1) * P],
                                                         scalar=weight[:, tile, bass.ds(e, 1)],
                                                         in1=k.x[:, tile, :], op0=ALU.mult, op1=ALU.add)
                        ins.then_inc(read.s, 1)
                        v.wait_ge(read.s, e * 2 + (c + 1 + read.base))

                if gated:
                    rounds(v, E, 2, expert)
                else:
                    affine(0, 0)
                    rounds(v, E - 2, 2, expert)
                    for par in range(2):
                        expert(E - 2 + par, par, more=(par == 0))

    mm.passed(E * U)
    mm2.passed(2 * E)
    read.passed(2 * E)
    act.passed(E * U)
    vec.passed(E * U if gated else E)
    for w in weights:
        w.passed(16 * E)


def stage_expert_bias(nc, k, weight, b2):
    mm, read = k.sems["mm"], k.sems["read"]
    with ExitStack() as ctx:
        wT = ctx.enter_context(nc.sbuf_tensor("bias_wT", [E, NT * P], F32))
        with nc.Block() as block:
            @block.tensor
            def _(pe):
                for t in range(NT):
                    ins = pe.transpose(k.ps[0:E, t // 4, (t % 4) * P:(t % 4 + 1) * P], weight[:, t, :], k.ident[:, :])
                ins.then_inc(mm.s, 1)
                pe.wait_ge(read.s, read.at(1))
                for t in range(NT):
                    ins = pe.matmul(k.ps[:, 2 + t // 4, (t % 4) * P:(t % 4 + 1) * P], wT[:, t * P:(t + 1) * P], b2,
                                    start=True, stop=True)
                ins.then_inc(mm.s, 1)

            @block.vector
            def _(v):
                v.wait_ge(mm.s, mm.at(1))
                v.tensor_copy(wT[:, :], k.ps[0:E, 0:2, :].rearrange("p a b -> p (a b)")).then_inc(read.s, 1)
                v.wait_ge(mm.s, mm.at(2))
                v.tensor_tensor(k.x[:, :, :].rearrange("p t c -> p (t c)"),
                                k.ps[:, 2:4, :].rearrange("p a b -> p (a b)"),
                                k.x[:, :, :].rearrange("p t c -> p (t c)"), ALU.add).then_inc(read.s, 1)
    mm.passed(2)
    read.passed(2)


def stage_mlp(nc, k, name, srcT, w2, b2, w3, bias):
    mm, mm2, act, vec = (k.sems[n] for n in ("mm", "mm2", "act", "vec"))
    with ExitStack() as ctx:
        hid = ctx.enter_context(nc.sbuf_tensor(name + "_hid", [P, FB, NT * P], F32))
        with nc.Block() as block:
            @block.gpsimd
            def _(g):
                g.tensor_tensor(k.x[:, :, :], k.x[:, :, :], bias.unsqueeze(1).broadcast_to([P, NT, C]), ALU.add)

            @block.tensor
            def _(pe):
                for u in range(2 * FB):
                    c, f = u // FB, u % FB
                    pe.wait_ge(act.s, act.at(u - 3))
                    pe.matmul(k.ps[:, u % 4, :], w2[:, f * P:(f + 1) * P], srcT[:, c * 512:(c + 1) * 512],
                              start=True, stop=True).then_inc(mm.s, 1)

            @block.scalar
            def _(a):
                for u in range(2 * FB):
                    c, f = u // FB, u % FB
                    a.wait_ge(mm.s, mm.at(u + 1))
                    a.activation(hid[:, f, c * 512:(c + 1) * 512], k.ps[:, u % 4, :], ACT.Gelu,
                                 bias=b2[:, f:f + 1]).then_inc(act.s, 1)
        mm.passed(2 * FB)
        act.passed(2 * FB)
        with nc.Block() as block:
            @block.tensor
            def _(pe):
                for t in range(NT):
                    for f in range(FB):
                        ins = pe.matmul(k.ps[:, t // 4, (t % 4) * P:(t % 4 + 1) * P], hid[:, f, t * P:(t + 1) * P],
                                        w3[:, f * C:(f + 1) * C], start=(f == 0), stop=(f == FB - 1))
                    if t % 4 == 3:
                        ins.then_inc(mm2.s, 1)

            @block.vector
            def _(v):
                for half in range(2):
                    v.wait_ge(mm2.s, mm2.at(half + 1))
                    xs = k.x[:, half * 4:half * 4 + 4, :].rearrange("p t c -> p (t c)")
                    v.tensor_tensor(xs, k.ps[:, half, :], xs, ALU.add).then_inc(vec.s, 1)
    mm2.passed(2)
    vec.passed(2)


def stage_add(nc, k, dst, a, b=None):
    with nc.Block() as block:
        @block.gpsimd
        def _(g):
            if b is None:
                g.tensor_copy(dst[:, :, :], a[:, :, :])
            else:
                g.tensor_tensor(dst[:, :, :], a[:, :, :], b[:, :, :], ALU.add)


def stage_sigmoid_of_best(nc, k, logits, best, weight):
    vec, act = k.sems["vec"], k.sems["act"]
    with nc.Block() as block:
        @block.vector
        def _(v):
            v.tensor_reduce(best[:, :], logits[:, :, :], AX.X, ALU.max).then_inc(vec.s, 1)
            v.wait_ge(act.s, act.at(1))
            v.tensor_scalar(best[:, :], best[:, :], 1.0, None, ALU.add).then_inc(vec.s, 1)
            v.wait_ge(vec.s, vec.at(2))
            v.reciprocal(best[:, :], best[:, :]).then_inc(vec.s, 1)
            v.wait_ge(vec.s, vec.at(3))
            v.tensor_tensor(weight[:, :, :], weight[:, :, :],
                            best[:, :].unsqueeze(2).broadcast_to([P, NT, E]), ALU.mult)

        @block.scalar
        def _(a):
            a.wait_ge(vec.s, vec.at(1))
            a.activation(best[:, :], best[:, :], ACT.Exp, scale=-1.0).then_inc(act.s, 1)
    vec.passed(3)
    act.passed(1)




def decoder(nc, d, out):
    k = K()
    with ExitStack() as whole:
        def sb_in(ctx, name, shape, dtype=F32):
            return ctx.enter_context(nc.sbuf_tensor(name, shape, dtype))

        stage_setup(nc, k, whole, d)

        def col(name, j=0, rows=P):
            a, w = COL[name]
            return k.col[0:rows, a + j:a + j + 1]

        def row(name):
            return sub(k.row, ROW, name)

        with ExitStack() as ctx:
            w0 = sb_in(ctx, "w0", [P, W0_N])
            wc0 = sb_in(ctx, "wc0", [CC, WC0_N])
            stage_load(nc, k, [(w0[:, :], d["w0"]), (wc0[:, :], d["wc0"])])
            stage_transpose(nc, k, k.x, [(k.xT, None, None)])
            with ExitStack() as c2:
                o0 = sb_in(c2, "o0", [P, BH // 4 * N])
                q0, k0 = Scratch(nc, "q0", 16, N, "q"), Scratch(nc, "k0", 16, N, "k")
                v0 = Values(nc, "v0", 16, N)
                heads = [(k.xT, w0[:, W0[n][0] + j * P:W0[n][0] + (j + 1) * P], None, scr, j * P)
                         for n, scr in (("wq", q0), ("wk", k0)) for j in range(2)]
                stage_project(nc, k, "p0", heads, (k.xT, sub(w0, W0, "wv"), None, v0))
                stage_attention(nc, k, "a0", N, 8 ** -0.5, "causal", q0, k0, v0, o0)
                stage_output(nc, k, [o0], sub(w0, W0, "wo"), None)
            stage_norm(nc, k, k.x, k.x)
            stage_transpose(nc, k, k.x, [(k.xT, None, None)])
            with ExitStack() as c2:
                o1 = sb_in(c2, "o1", [P, BH // 4 * N])
                oc = sb_in(c2, "oc", [P, BH // 4 * N])
                q1, k1 = Scratch(nc, "q1", 8, N, "q"), Scratch(nc, "k1", 8, N, "k")
                qc, kc = Scratch(nc, "qc", 8, N, "q", thin=True), Scratch(nc, "kc", 8, T_CTX, "k", thin=True)
                v1, vc = Values(nc, "v1", 8, N), Values(nc, "vc", 8, T_CTX)
                heads = [(k.xT, sub(w0, W0, "xq"), col("xq"), q1, 0),
                         (k.xT, sub(w0, W0, "xk"), col("xk"), k1, 0),
                         (k.xT, sub(w0, W0, "xcq"), col("xcq"), qc, 0)]
                stage_project(nc, k, "p1", heads, (k.xT, sub(w0, W0, "xv"), row("xv"), v1))
                stage_context(nc, k, "c0", sub(wc0, WC0, "ck", CC), sub(wc0, WC0, "cv", CC), col("xck"),
                              row("xcv"), kc, vc, ctxT=d["ctxT"])
                stage_attention(nc, k, "a1", N, 8 ** -0.5, "causal", q1, k1, v1, o1)
                stage_attention(nc, k, "ac", T_CTX, 8 ** -0.5, None, qc, kc, vc, oc)
                stage_output(nc, k, [o1, oc], sub(w0, W0, "xp"), row("xp"))
            stage_norm(nc, k, k.x, k.x)
            stage_transpose(nc, k, k.x, [(k.xT, None, None)])
            with ExitStack() as c2:
                plan = sb_in(c2, "plan", [P, NT, E])
                kept = sb_in(c2, "kept", [P, NT, E])
                weight = sb_in(c2, "weight0", [P, NT, E])
                stage_logits(nc, k, sub(w0, W0, "gate"), plan, -1.0 / SINK_EPS)
                stage_sinkhorn(nc, k, plan)
                stage_add(nc, k, kept, plan)
                stage_top(nc, k, "top0", plan, weight, 2,
                          [kept[:, :, r:r + 1].broadcast_to([P, NT, E]) for r in range(2)])
                stage_experts(nc, k, "e0", k.xT, d["e0_in"], d["e0_down"], weight, True)
            stage_norm(nc, k, k.x, k.x)
        stage_transpose(nc, k, k.x, [(k.xT, None, None)])
        with ExitStack() as ctx:
            w1 = sb_in(ctx, "w1", [P, W1_N])
            wf = sb_in(ctx, "wf", [32, WF_N])
            o2 = sb_in(ctx, "o2", [P, BH // 2 * N])
            q2, k2 = Scratch(nc, "q2", 64, N, "q", True), Scratch(nc, "k2", 64, N, "k", True)
            v2 = Values(nc, "v2", 64, N)
            stage_load(nc, k, [(w1[:, :], d["w1"]), (wf[:, :], d["wf"])])
            stage_project_rotary(nc, k, w1, wf, q2, k2, v2)
            stage_attention(nc, k, "a2", N, 64 ** -0.5, None, q2, k2, v2, o2)
            stage_output(nc, k, [o2], sub(w1, W1, "o"), row("out"))
        stage_norm(nc, k, k.x, k.x)
        with ExitStack() as ctx:
            wx = sb_in(ctx, "wx", [P, WX_N])
            wc1 = sb_in(ctx, "wc1", [CC, WC1_N])
            xx = sb_in(ctx, "xx", [P, NT, C])
            keep = sb_in(ctx, "keep", [P, NT, C])
            z = sb_in(ctx, "z", [P, NT, C])
            yT = sb_in(ctx, "yT", [P, NT * P])
            cent = sb_in(ctx, "cent", [P, E])
            stage_load(nc, k, [(cent[:, :], d["cent"]), (wc1[:, :], d["wc1"])])
            stage_add(nc, k, xx, k.x)
            for unit in ("a1", "a2"):
                ln = "ln1" if unit == "a1" else "ln2"
                stage_load(nc, k, [(wx[:, :], d["w" + unit])])
                stage_norm(nc, k, k.x, k.x, row(ln + "_g"), row(ln + "_b"))
                stage_add(nc, k, keep, k.x)
                stage_norm(nc, k, k.x, z)
                with ExitStack() as c2:
                    T = N if unit == "a1" else T_CTX
                    qs, ks = (Scratch(nc, unit + which, 32, n, which, thin=(unit == "a2"))
                              for which, n in (("q", N), ("k", T)))
                    vv = Values(nc, unit + "v", 32, T)
                    oo = sb_in(c2, unit + "o", [P, BH // 4 * N])
                    outs = [(k.xT, col(unit + "lnx_g"), col(unit + "lnx_b"))]
                    if unit == "a1":
                        outs.append((yT, col(unit + "lny_g"), col(unit + "lny_b")))
                    stage_transpose(nc, k, z, outs)
                    qa, ka = WX["q"][0], WX["k"][0]
                    heads = [(k.xT, wx[:, qa + j * P:qa + (j + 1) * P], None, qs, j * P) for j in range(4)]
                    if unit == "a1":
                        heads += [(yT, wx[:, ka + j * P:ka + (j + 1) * P], None, ks, j * P) for j in range(4)]
                    stage_project(nc, k, "p" + unit, heads,
                                  (yT, sub(wx, WX, "v"), None, vv) if unit == "a1" else None)
                    if unit == "a2":
                        stage_context(nc, k, "c1", sub(wc1, WC1, "k", CC), sub(wc1, WC1, "v", CC), None,
                                      None, ks, vv, ctx_rows=d["ctx"], gain=col("a2lny_g", rows=CC),
                                      shift=col("a2lny_b", rows=CC))
                    stage_attention(nc, k, "t" + unit, T, 32 ** -0.5, "after" if unit == "a1" else None,
                                    qs, ks, vv, oo)
                    stage_output(nc, k, [oo], sub(wx, WX, "li1"), row(unit + "li1"))
                stage_norm(nc, k, k.x, z)
                stage_transpose(nc, k, z, [(k.xT, col(unit + "ln3_g"), col(unit + "ln3_b"))])
                stage_mlp(nc, k, "m" + unit, k.xT, sub(wx, WX, "li2"),
                          k.col[:, COL[unit + "li2_b"][0]:COL[unit + "li2_b"][0] + FB],
                          sub(wx, WX, "li3"), row(unit + "li3"))
                stage_add(nc, k, k.x, k.x, keep)
            stage_add(nc, k, k.x, k.x, xx)
            stage_norm(nc, k, k.x, k.x)
            aff = sb_in(ctx, "affinity", [P, NT, E])
            best = sb_in(ctx, "affinity_best", [P, NT])
            weight = sb_in(ctx, "weight1", [P, NT, E])
            b2 = sb_in(ctx, "b2", [E, C])
            stage_load(nc, k, [(b2[:, :], d["b2"])])
            stage_transpose(nc, k, k.x, [(k.xT, None, None)])
            stage_logits(nc, k, cent[:, :], aff, 1.0)
            stage_top(nc, k, "top1", aff, weight, 1)
            stage_sigmoid_of_best(nc, k, aff, best, weight)
            stage_norm(nc, k, k.x, z)
            stage_transpose(nc, k, z, [(yT, None, None)])
            stage_add(nc, k, k.x, k.x, k.x)
            stage_expert_bias(nc, k, weight, b2[:, :])
            stage_experts(nc, k, "e1", yT, d["e1_in"], d["e1_down"], weight, False)
            stage_norm(nc, k, k.x, k.x)
        with nc.Block() as block:
            @block.sync
            def _(sp):
                o = k.sems["out"]
                sp.dma_start(out.rearrange("(t p) c -> p t c", p=P), k.x[:, :, :]).then_inc(o.s, 16)
                sp.wait_ge(o.s, o.at(16))


def layout(i):
    def pack(table, total, parts, rows=P):
        a = np.zeros((rows, total), np.float32)
        for name, v in parts.items():
            at, w = table[name]
            a[0:v.shape[0], at:at + w] = v
        return a

    def blocks(w):
        return w.reshape(-1, P, w.shape[1]).transpose(1, 0, 2).reshape(P, -1)

    def padded(w, D):
        a = np.zeros((H, 32, w.shape[1]), np.float32)
        a[:, 0:D] = w.reshape(H, D, -1)
        return blocks(a.reshape(H * 32, -1))

    d = {"x": i["x"].reshape(B * N, C), "ctx": i["ctx_512"].reshape(-1, CC)}
    d["ctxT"] = np.ascontiguousarray(d["ctx"].T)
    d["w0"] = pack(W0, W0_N, {
        "wq": i["L0_attn_Wq"], "wk": i["L0_attn_Wk"], "wv": i["L0_attn_Wv"], "wo": padded(i["L0_attn_Wo"], 16),
        "xk": i["L0_xattn_Wk"], "xq": i["L0_xattn_Wq"], "xv": i["L0_xattn_Wv"], "xcq": i["L0_xattn_Wcq"],
        "xp": padded(i["L0_xattn_Wp"], 8), "gate": i["L0_ffn_gate_W"].T})
    d["wc0"] = pack(WC0, WC0_N, {"ck": i["L0_xattn_Wck"], "cv": i["L0_xattn_Wcv"]}, CC)
    hd = 64
    freqs = np.float32(10000.0) ** (-np.arange(0, hd, 2, dtype=np.float32) / np.float32(hd))
    angles = np.arange(N, dtype=np.float32)[:, None] * freqs
    sin = np.repeat(np.sin(angles), 2, axis=1).T
    cos = np.repeat(np.cos(angles), 2, axis=1).T
    sign = np.where(np.arange(hd) < hd // 2, -1.0, 1.0).astype(np.float32)[:, None]
    turn = np.concatenate([np.arange(1, hd, 2), np.arange(0, hd, 2)])
    ff = np.arange(N, dtype=np.float32)[:, None] * np.arange(1, 17, dtype=np.float32)
    fourier = np.concatenate([np.sin(ff), np.cos(ff)], axis=-1).T
    wq, wk, wv = i["L1_attn_w_qkv"].reshape(3, H, hd, C)
    d["w1"] = pack(W1, W1_N, {
        "q": wq.reshape(-1, C).T, "qr": wq[:, turn].reshape(-1, C).T, "k": wk.reshape(-1, C).T,
        "kr": wk[:, turn].reshape(-1, C).T, "v": wv.reshape(-1, C).T, "o": blocks(i["L1_attn_w_out"].T),
        "cos": np.tile(cos, (2, 1)), "sin": np.tile(sin * sign, (2, 1))})
    d["wf"] = pack(WF, WF_N, {"fp": np.tile(i["L1_attn_w_fproj"].T, (1, 2)), "fourier": fourier}, 32)
    col = {}
    for a in ("a1", "a2"):
        g = {n: i["L1_xattn_" + a + "_" + n] for n in (
            "wq", "wk", "wv", "li1_w", "li2_w", "li3_w", "lnx_g", "lnx_b", "lny_g", "lny_b", "ln3_g", "ln3_b",
            "li2_b")}
        wx = {}
        for n in "qkv":
            w = g["w" + n].transpose(1, 0, 2).reshape(g["w" + n].shape[1], -1)
            if a == "a1" or n == "q":
                wx[n] = w
            else:
                g["ctx" + n] = w
        wx["li1"], wx["li2"], wx["li3"] = blocks(g["li1_w"]), g["li2_w"], blocks(g["li3_w"])
        d["w" + a] = pack(WX, WX_N, wx)
        for n in ("lnx_g", "lnx_b", "lny_g", "lny_b", "ln3_g", "ln3_b"):
            col[a + n] = g[n][:, None]
        col[a + "li2_b"] = g["li2_b"].reshape(FB, P).T
    d["cent"] = i["L1_ffn_centroids"].T
    d["wc1"] = pack(WC1, WC1_N, {"k": g["ctxk"], "v": g["ctxv"]}, CC)
    for n in ("xk", "xq", "xcq", "xck"):
        col[n] = i["L0_xattn_b" + n[1:]][:, None]
    col["fp"] = np.tile(i["L1_attn_b_fproj"], 2)[:, None]
    col["ln_g"], col["ln_b"] = i["L1_ffn_ln_g"].T, i["L1_ffn_ln_b"].T
    col["b1"] = i["L1_ffn_b1"].reshape(E * FB, P).T
    d["col"] = pack(COL, COL_N, col)
    row = {"xv": "L0_xattn_bv", "xcv": "L0_xattn_bcv", "xp": "L0_xattn_bp", "out": "L1_attn_b_out",
           "a1li1": "L1_xattn_a1_li1_b", "a1li3": "L1_xattn_a1_li3_b", "a2li1": "L1_xattn_a2_li1_b",
           "a2li3": "L1_xattn_a2_li3_b", "ln1_g": "L1_xattn_ln1_g", "ln1_b": "L1_xattn_ln1_b",
           "ln2_g": "L1_xattn_ln2_g", "ln2_b": "L1_xattn_ln2_b"}
    rows = {n: i[v][None, :] for n, v in row.items()}
    rows["iota"] = np.arange(E, dtype=np.float32)[None, :]
    d["row"] = pack(ROW, ROW_N, rows, 1)
    d["e0_in"] = np.concatenate([i["L0_ffn_W_gate"].transpose(0, 2, 1), i["L0_ffn_W_up"].transpose(0, 2, 1)], axis=2)

    def down(w):
        return w.transpose(0, 2, 1).reshape(E, FB, P, C).transpose(0, 2, 1, 3).reshape(E, P, FB * C)

    d["e0_down"] = down(i["L0_ffn_W_down"])
    d["e1_in"] = i["L1_ffn_w1"].transpose(0, 2, 1)
    d["e1_down"] = down(i["L1_ffn_w2"])
    d["b2"] = i["L1_ffn_b2"]
    return {n: np.ascontiguousarray(v) for n, v in d.items()}


def kernel(**inputs):
    import concourse.bacc as _bacc
    from concourse.bass_utils import run_bass_kernel_spmd as _run

    arrays = layout({n: np.asarray(v) for n, v in inputs.items()})
    nc = _bacc.Bacc("TRN2", target_bir_lowering=False, num_devices=1)
    d = {n: nc.dram_tensor("in_" + n, a.shape, F32, kind="ExternalInput").ap() for n, a in arrays.items()}
    out = nc.dram_tensor("out_0", (B * N, C), F32, kind="ExternalOutput").ap()
    decoder(nc, d, out)
    r = _run(nc, [{"in_" + n: a for n, a in arrays.items()}], core_ids=[0])
    return r.results[0]["out_0"].reshape(B, N, C)
```
